# Optimizing a Trainium2 kernel written in Bass

```python
import numpy as np
import jax
import jax.numpy as jnp

def _softmax(x, axis=-1):
    return jax.nn.softmax(x, axis=axis)

def _gelu(x):
    return jax.nn.gelu(x, approximate=True)

def _silu(x):
    return jax.nn.silu(x)

def _sigmoid(x):
    return jax.nn.sigmoid(x)

def _layernorm(x, axis=-1, eps=1e-05):
    m = jnp.mean(x, axis=axis, keepdims=True)
    v = jnp.var(x, axis=axis, keepdims=True)
    return (x - m) / jnp.sqrt(v + eps)

def _scatter_add(tgt, idx, src, axis=0):
    return tgt.at[idx].add(src)

def _segment_sum(src, seg, n):
    return jax.ops.segment_sum(src, seg, n)
kernel_name = 'mk_gnn_preln_d4_gnn_r32_d15c81'

def setup_inputs(seed: int=0):
    np.random.seed(seed)
    _w = jnp.asarray

    def _rec_inputs():
        import jax
        import jax.numpy as jnp
        _gk = jax.random.key(seed)
        x = -0.0005121 + 1.001 * jax.random.normal(jax.random.fold_in(_gk, 1), (3125, 160), jnp.float32)
        src = jax.random.randint(jax.random.fold_in(_gk, 2), (50000,), 0, 3125, jnp.int32)
        dst = jnp.minimum((3125 * jax.random.uniform(jax.random.fold_in(_gk, 3), (50000,)) ** 2.0).astype(jnp.int32), 99999)
        _o = jnp.argsort(dst, stable=True)
        src = src[_o]
        dst = dst[_o]
        edge_attr_16 = jax.random.uniform(jax.random.fold_in(_gk, 12), (50000, 16), jnp.float32, 0.0, 1)
        edge_attr_3 = 0.00047201 + 1.00023 * jax.random.normal(jax.random.fold_in(_gk, 13), (50000, 3), jnp.float32)
        edge_attr_4 = 0.000898722 + 1.00012 * jax.random.normal(jax.random.fold_in(_gk, 14), (50000, 4), jnp.float32)
        edge_attr_64 = 0.000279952 + 1.00013 * jax.random.normal(jax.random.fold_in(_gk, 15), (50000, 64), jnp.float32)
        node_vec1 = jax.random.uniform(jax.random.fold_in(_gk, 17), (3125, 1), jnp.float32, 0.0, 1)
        return (x, src, dst, edge_attr_16, edge_attr_3, edge_attr_4, edge_attr_64, node_vec1)
    x, src, dst, edge_attr_16, edge_attr_3, edge_attr_4, edge_attr_64, node_vec1 = _rec_inputs()

    def _L0_gnn_setup():
        import jax, jax.numpy as jnp
        import numpy as np
        N, E = (625, 10000)
        CS, CV = (64, 32)
        AS_, AV, H = (16, 8, 4)
        NB = 16
        SQRT3 = 1.7320508075688772
        SQRT2 = 1.4142135623730951
        EPS = 1e-05

        def _cg_tp(s, v, y0, y1, w_ss, w_sv, w_vs, w_vv0, w_vv1):
            out_s = jnp.concatenate([w_ss * s * y0[:, None], w_vv0 * (jnp.einsum('eci,ei->ec', v, y1) / SQRT3)], axis=-1)
            out_v = jnp.concatenate([(w_sv * s)[:, :, None] * y1[:, None, :], (w_vs * jnp.ones_like(v[..., 0]))[..., None] * v * y0[:, None, None], (w_vv1 * jnp.ones_like(v[..., 0]))[..., None] * (jnp.cross(v, y1[:, None, :]) / SQRT2)], axis=1)
            return (out_s, out_v)

        def _equiv_layernorm(s, v, gamma_s, beta_s, gamma_v):
            mu = jnp.mean(s, axis=-1, keepdims=True)
            var = jnp.var(s, axis=-1, keepdims=True)
            s_n = (s - mu) * jax.lax.rsqrt(var + EPS) * gamma_s + beta_s
            rms = jnp.sqrt(jnp.mean(jnp.sum(v * v, axis=-1), axis=-1, keepdims=True) + EPS)
            v_n = v / rms[..., None] * gamma_v[None, :, None]
            return (s_n, v_n)
        key = jax.random.key(seed)
        ks = jax.random.split(key, 26)

        def rn(k, shape, fan):
            return jax.random.normal(k, shape, jnp.float32) / np.sqrt(fan)
        D1S, D1V = (CS + CV, CS + 2 * CV)
        WN = 2 * CS + 3 * CV
        inp = {'node': jax.random.normal(ks[0], (N, CS + 3 * CV), jnp.float32), 'edge_index': jax.random.randint(ks[1], (2, E), 0, N, jnp.int64 if jax.config.jax_enable_x64 else jnp.int32), 'rbf': jax.random.uniform(ks[2], (E, NB), jnp.float32), 'rsh': jax.random.normal(ks[3], (E, 4), jnp.float32), 'gamma_s': jnp.ones((CS,), jnp.float32), 'beta_s': jnp.zeros((CS,), jnp.float32), 'gamma_v': jnp.ones((CV,), jnp.float32), 'Ws_src': rn(ks[4], (CS, CS), CS), 'Wv_src': rn(ks[5], (CV, CV), CV), 'Ws_dst': rn(ks[6], (CS, CS), CS), 'Wv_dst': rn(ks[7], (CV, CV), CV), 'W_rbf': rn(ks[8], (NB, WN), NB), 'W_alpha': rn(ks[9], (D1S, H * AS_), D1S), 'alpha_dot': rn(ks[10], (1, H, AS_), AS_), 'Ws_val': rn(ks[11], (D1S, CS), D1S), 'Wv_val': rn(ks[12], (D1V, CV), D1V), 'Wg': rn(ks[13], (CS, CV), CS), 'w2_ss': rn(ks[14], (CS,), 1), 'w2_sv': rn(ks[15], (CS,), 1), 'w2_vs': rn(ks[16], (CV,), 1), 'w2_vv0': rn(ks[17], (CV,), 1), 'w2_vv1': rn(ks[18], (CV,), 1), 'Ws_vlin': rn(ks[19], (D1S, H * AS_), D1S), 'Wv_vlin': rn(ks[20], (D1V, H * AV), D1V), 'Wps': rn(ks[21], (H * AS_, CS), H * AS_), 'Wpv': rn(ks[22], (H * AV, CV), H * AV)}
        return inp
    _L0_gnn_all = _L0_gnn_setup()
    _L0_gnn_in = {k: v for k, v in _L0_gnn_all.items() if k in ('gamma_s', 'beta_s', 'gamma_v', 'Ws_src', 'Wv_src', 'Ws_dst', 'Wv_dst', 'W_rbf', 'W_alpha', 'alpha_dot', 'Ws_val', 'Wv_val', 'Wg', 'w2_ss', 'w2_sv', 'w2_vs', 'w2_vv0', 'w2_vv1', 'Ws_vlin', 'Wv_vlin', 'Wps', 'Wpv')}
    del _L0_gnn_all

    def _L1_gnn_setup():
        import jax, jax.numpy as jnp
        import numpy as np
        N_NODES = 10000
        N_EDGES = 10000
        MUL0, MUL1 = (64, 32)
        EDGE_DIM = 64
        W_NUMEL = 224
        DENOM = 32.0
        SQRT3 = 3.0 ** 0.5
        INV_SQRT3 = 1.0 / SQRT3
        INV_SQRT2 = 2.0 ** (-0.5)

        def _forward(node_feature, edge_attr, edge_feature, W_skip0, W_skip1, W_nl0, W_nl1, W_fc1, W_fc2, W_out_s, W_out_v, edge_index):
            N = node_feature.shape[0]
            E = edge_attr.shape[0]
            s = node_feature[:, :MUL0]
            v = node_feature[:, MUL0:].reshape(N, MUL1, 3)
            skip_s = s @ W_skip0
            skip_v = jnp.einsum('nmi,mk->nki', v, W_skip1)
            s = s @ W_nl0
            v = jnp.einsum('nmi,mk->nki', v, W_nl1)
            rhat = edge_attr / jnp.linalg.norm(edge_attr, axis=-1, keepdims=True)
            sh1 = SQRT3 * rhat
            w = jax.nn.relu(edge_feature @ W_fc1) @ W_fc2
            w0, w1, w2, w3, w4 = jnp.split(w, [64, 128, 160, 192], axis=-1)
            src, dst = (edge_index[0], edge_index[1])
            xs = s[dst]
            xv = v[dst]
            out0a = w0 * xs
            out0b = w3 * (jnp.einsum('emi,ei->em', xv, sh1) * INV_SQRT3)
            out1a = (w1 * xs)[:, :, None] * sh1[:, None, :]
            out1b = w2[:, :, None] * xv
            out1c = w4[:, :, None] * (jnp.cross(xv, sh1[:, None, :]) * INV_SQRT2)
            tp = jnp.concatenate([out0a, out0b, out1a.reshape(E, -1), out1b.reshape(E, -1), out1c.reshape(E, -1)], axis=-1)
            agg = jax.ops.segment_sum(tp, src, num_segments=N) / DENOM
            agg_s = agg[:, :96]
            agg_v = agg[:, 96:].reshape(N, 128, 3)
            out_s = agg_s @ W_out_s + skip_s
            out_v = jnp.einsum('nmi,mk->nki', agg_v, W_out_v) + skip_v
            fs = jax.nn.silu(out_s[:, :MUL0])
            gate = jax.nn.sigmoid(out_s[:, MUL0:MUL0 + 32])
            gv = gate[:, :, None] * out_v
            return jnp.concatenate([fs, gv.reshape(N, -1)], axis=-1)
        key = jax.random.key(seed)
        ks = jax.random.split(key, 12)

        def lin(k, fi, fo):
            return jax.random.normal(k, (fi, fo), jnp.float32) / np.float32(np.sqrt(fi))
        return {'node_feature': jax.random.normal(ks[0], (N_NODES, MUL0 + 3 * MUL1), jnp.float32), 'edge_attr': jax.random.normal(ks[1], (N_EDGES, 3), jnp.float32), 'edge_feature': jax.random.normal(ks[2], (N_EDGES, EDGE_DIM), jnp.float32), 'W_skip0': lin(ks[3], MUL0, 96), 'W_skip1': lin(ks[4], MUL1, 32), 'W_nl0': lin(ks[5], MUL0, MUL0), 'W_nl1': lin(ks[6], MUL1, MUL1), 'W_fc1': lin(ks[7], EDGE_DIM, 64), 'W_fc2': lin(ks[8], 64, W_NUMEL), 'W_out_s': lin(ks[9], 96, 96), 'W_out_v': lin(ks[10], 128, 32), 'edge_index': jax.random.randint(ks[11], (2, N_EDGES), 0, N_NODES)}
    _L1_gnn_all = _L1_gnn_setup()
    _L1_gnn_in = {k: v for k, v in _L1_gnn_all.items() if k in ('W_skip0', 'W_skip1', 'W_nl0', 'W_nl1', 'W_fc1', 'W_fc2', 'W_out_s', 'W_out_v')}
    del _L1_gnn_all

    def _L2_gnn_setup():
        import jax, jax.numpy as jnp
        import numpy as np
        N, E = (1250, 20000)
        S_IN, V_IN = (64, 32)
        S_MID, V_MID = (96, 128)
        S_OUT, V_OUT = (96, 32)
        R = 64
        FC_HID = 64
        W_NUMEL = 64 + 64 + 32 + 32 + 32
        NUM_NEIGHBORS = 16.0

        def _inv(d):
            return 1.0 / jnp.sqrt(jnp.float32(d))

        def _forward(node_features, node_attr, edge_attr, edge_scalars, lin1_ws, lin1_wv, fc_w1, fc_w2, sc_ws, sc_wv, lin2_ws, lin2_wv, edge_src, edge_dst):
            n = node_features.shape[0]
            s = node_features[:, :S_IN]
            v = node_features[:, S_IN:].reshape(n, V_IN, 3)
            a = node_attr
            sc_s = s @ sc_ws * a * _inv(S_IN)
            sc_v = jnp.einsum('nci,cd->ndi', v, sc_wv) * a[:, :, None] * _inv(V_IN)
            h_s = s @ lin1_ws * a * _inv(S_IN)
            h_v = jnp.einsum('nci,cd->ndi', v, lin1_wv) * a[:, :, None] * _inv(V_IN)
            hid = jax.nn.silu(edge_scalars @ fc_w1 * _inv(R))
            w = hid @ fc_w2 * _inv(FC_HID)
            w1, w2, w3, w4, w5 = jnp.split(w, [64, 128, 160, 192], axis=-1)
            es = h_s[edge_src]
            ev = h_v[edge_src]
            e0 = edge_attr[:, :1]
            e1 = edge_attr[:, 1:4]
            m_s1 = w1 * es * e0
            m_s2 = w4 * jnp.einsum('eci,ei->ec', ev, e1) * _inv(3)
            m_v1 = (w2 * es)[:, :, None] * e1[:, None, :]
            m_v2 = w3[:, :, None] * ev * e0[:, :, None]
            m_v3 = w5[:, :, None] * jnp.cross(ev, e1[:, None, :]) * _inv(2)
            mid_s = jnp.concatenate([m_s1, m_s2], axis=-1)
            mid_v = jnp.concatenate([m_v1, m_v2, m_v3], axis=1)
            inv_nn = 1.0 / jnp.sqrt(jnp.float32(NUM_NEIGHBORS))
            agg_s = jax.ops.segment_sum(mid_s, edge_dst, num_segments=n) * inv_nn
            agg_v = jax.ops.segment_sum(mid_v, edge_dst, num_segments=n) * inv_nn
            o_s = agg_s @ lin2_ws * a * _inv(S_MID)
            o_v = jnp.einsum('nci,cd->ndi', agg_v, lin2_wv) * a[:, :, None] * _inv(V_MID)
            pre_s = sc_s + o_s
            pre_v = sc_v + o_v
            scalars = jax.nn.silu(pre_s[:, :64])
            gates = jax.nn.sigmoid(pre_s[:, 64:96])
            gated = gates[:, :, None] * pre_v
            return jnp.concatenate([scalars, gated.reshape(n, 3 * V_OUT)], axis=-1)
        key = jax.random.key(seed)
        ks = jax.random.split(key, 13)
        return {'node_features': jax.random.normal(ks[0], (N, S_IN + 3 * V_IN), jnp.float32), 'node_attr': jnp.ones((N, 1), jnp.float32), 'edge_src': jax.random.randint(ks[1], (E,), 0, N), 'edge_dst': jax.random.randint(ks[2], (E,), 0, N), 'edge_attr': jax.random.normal(ks[3], (E, 4), jnp.float32), 'edge_scalars': jax.random.normal(ks[4], (E, R), jnp.float32), 'lin1_ws': jax.random.normal(ks[5], (S_IN, S_IN), jnp.float32), 'lin1_wv': jax.random.normal(ks[6], (V_IN, V_IN), jnp.float32), 'fc_w1': jax.random.normal(ks[7], (R, FC_HID), jnp.float32), 'fc_w2': jax.random.normal(ks[8], (FC_HID, W_NUMEL), jnp.float32), 'sc_ws': jax.random.normal(ks[9], (S_IN, S_OUT), jnp.float32), 'sc_wv': jax.random.normal(ks[10], (V_IN, V_OUT), jnp.float32), 'lin2_ws': jax.random.normal(ks[11], (S_MID, S_OUT), jnp.float32), 'lin2_wv': jax.random.normal(ks[12], (V_MID, V_OUT), jnp.float32)}
    _L2_gnn_all = _L2_gnn_setup()
    _L2_gnn_in = {k: v for k, v in _L2_gnn_all.items() if k in ('lin1_ws', 'lin1_wv', 'fc_w1', 'fc_w2', 'sc_ws', 'sc_wv', 'lin2_ws', 'lin2_wv')}
    del _L2_gnn_all

    def _L3_gnn_setup():
        import jax, jax.numpy as jnp
        import numpy as np
        N, E = (10000, 5000)
        C0, C1 = (64, 32)
        H, A = (8, 8)
        H0, H1 = (8, 4)
        M0, M1 = (128, 64)
        NG, RH = (64, 64)
        WN = C0 + C0 + C1 + C1 + C1
        DS, DV = (C0 + C1, C0 + 2 * C1)
        EPS = 1e-05
        SQ3 = np.float32(np.sqrt(3.0))
        SQ2 = np.float32(np.sqrt(2.0))

        def _split(x):
            return (x[:, :C0], x[:, C0:].reshape(x.shape[0], C1, 3))

        def _merge(s, v):
            return jnp.concatenate([s, v.reshape(v.shape[0], -1)], axis=1)

        def _eq_ln(x, w0, b0, w1):
            s, v = _split(x)
            s = s - s.mean(axis=1, keepdims=True)
            s = s * jax.lax.rsqrt(jnp.square(s).mean(axis=1, keepdims=True) + EPS) * w0 + b0
            v = v * jax.lax.rsqrt(jnp.square(v).mean(axis=(1, 2), keepdims=True) + EPS) * w1[None, :, None]
            return (s, v)

        def _eq_lin(s, v, ws, bs, wv):
            return (s @ ws + bs, jnp.einsum('nud,uk->nkd', v, wv))

        def _ln(x, g, b):
            xc = x - x.mean(-1, keepdims=True)
            return xc * jax.lax.rsqrt(jnp.square(xc).mean(-1, keepdims=True) + EPS) * g + b

        def _smooth_leaky(x, alpha=0.2):
            return 0.5 * (1 + alpha) * x + 0.5 * (1 - alpha) * x * (2.0 * jax.nn.sigmoid(x) - 1.0)

        def _forward(node_input, node_attr, edge_vec, edge_scalars, edge_src, edge_dst, ln1_w0, ln1_b0, ln1_w1, ln2_w0, ln2_b0, ln2_w1, msrc_ws, msrc_wv, mdst_ws, mdst_bs, mdst_wv, rw1, rb1, rg1, rbe1, rw2, rb2, rg2, rbe2, rw3, roff, lin_ws, lin_bs, lin_wv, alpha_dot, proj_ws, proj_bs, proj_wv, f1_ws, f1_bs, f1_wv, f2_ws, f2_bs, f2_wv):
            n = node_input.shape[0]
            s, v = _eq_ln(node_input, ln1_w0, ln1_b0, ln1_w1)
            src_s = s @ msrc_ws
            src_v = jnp.einsum('nud,uk->nkd', v, msrc_wv)
            dst_s = s @ mdst_ws + mdst_bs
            dst_v = jnp.einsum('nud,uk->nkd', v, mdst_wv)
            ms = src_s[edge_src] + dst_s[edge_dst]
            mv = src_v[edge_src] + dst_v[edge_dst]
            h = jax.nn.silu(_ln(edge_scalars @ rw1 + rb1, rg1, rbe1))
            h = jax.nn.silu(_ln(h @ rw2 + rb2, rg2, rbe2))
            w = h @ rw3 + roff
            rhat = edge_vec * jax.lax.rsqrt(jnp.sum(jnp.square(edge_vec), -1, keepdims=True) + 1e-12)
            Y1 = SQ3 * rhat
            w1, w2, w3, w4, w5 = jnp.split(w, [C0, 2 * C0, 2 * C0 + C1, 2 * C0 + 2 * C1], axis=1)
            o0a = w1 * ms
            o0b = w4 * (jnp.einsum('eud,ed->eu', mv, Y1) / SQ3)
            o1a = (w2 * ms)[:, :, None] * Y1[:, None, :]
            o1b = w3[:, :, None] * mv
            o1c = w5[:, :, None] * (jnp.cross(mv, Y1[:, None, :]) / SQ2)
            ds = jnp.concatenate([o0a, o0b], axis=1)
            dv = jnp.concatenate([o1a, o1b, o1c], axis=1)
            ls, lv = _eq_lin(ds, dv, lin_ws, lin_bs, lin_wv)
            e = ls.shape[0]
            alpha = ls[:, :H * A].reshape(e, H, A)
            vs = ls[:, H * A:].reshape(e, H, H0)
            vv = lv.reshape(e, H, H1, 3)
            a = jnp.einsum('ehk,hk->eh', _smooth_leaky(alpha), alpha_dot)
            amax = jax.lax.stop_gradient(jax.ops.segment_max(a, edge_dst, num_segments=n))
            a = jnp.exp(a - amax[edge_dst])
            a = a / (jax.ops.segment_sum(a, edge_dst, num_segments=n)[edge_dst] + 1e-12)
            ns = jax.ops.segment_sum(vs * a[..., None], edge_dst, num_segments=n).reshape(n, H * H0)
            nv = jax.ops.segment_sum(vv * a[..., None, None], edge_dst, num_segments=n).reshape(n, H * H1, 3)
            ps, pv = _eq_lin(ns, nv, proj_ws, proj_bs, proj_wv)
            x = node_input + _merge(ps, pv)
            s2, v2 = _eq_ln(x, ln2_w0, ln2_b0, ln2_w1)
            a0 = node_attr[:, :1]
            fs, fv = _eq_lin(s2, v2, f1_ws, f1_bs, f1_wv)
            fs = fs * a0
            fv = fv * a0[:, :, None]
            sc = jax.nn.silu(fs[:, :M0])
            fv = fv * jax.nn.sigmoid(fs[:, M0:])[:, :, None]
            os_, ov = _eq_lin(sc, fv, f2_ws, f2_bs, f2_wv)
            os_ = os_ * a0
            ov = ov * a0[:, :, None]
            return x + _merge(os_, ov)
        key = jax.random.key(seed)
        ks = iter(jax.random.split(key, 24))

        def nrm(shape, fan):
            return jax.random.normal(next(ks), shape, jnp.float32) / np.float32(np.sqrt(fan))
        inp = {}
        inp['node_input'] = jax.random.normal(next(ks), (N, C0 + 3 * C1), jnp.float32)
        inp['node_attr'] = jnp.ones((N, 1), jnp.float32)
        inp['edge_vec'] = jax.random.normal(next(ks), (E, 3), jnp.float32)
        inp['edge_scalars'] = jax.random.uniform(next(ks), (E, NG), dtype=jnp.float32)
        inp['edge_src'] = jax.random.randint(next(ks), (E,), 0, N)
        inp['edge_dst'] = jax.random.randint(next(ks), (E,), 0, N)
        inp['ln1_w0'] = jnp.ones((C0,), jnp.float32)
        inp['ln1_b0'] = jnp.zeros((C0,), jnp.float32)
        inp['ln1_w1'] = jnp.ones((C1,), jnp.float32)
        inp['ln2_w0'] = jnp.ones((C0,), jnp.float32)
        inp['ln2_b0'] = jnp.zeros((C0,), jnp.float32)
        inp['ln2_w1'] = jnp.ones((C1,), jnp.float32)
        inp['msrc_ws'] = nrm((C0, C0), C0)
        inp['msrc_wv'] = nrm((C1, C1), C1)
        inp['mdst_ws'] = nrm((C0, C0), C0)
        inp['mdst_bs'] = jnp.zeros((C0,), jnp.float32)
        inp['mdst_wv'] = nrm((C1, C1), C1)
        inp['rw1'] = nrm((NG, RH), NG)
        inp['rb1'] = jnp.zeros((RH,), jnp.float32)
        inp['rg1'] = jnp.ones((RH,), jnp.float32)
        inp['rbe1'] = jnp.zeros((RH,), jnp.float32)
        inp['rw2'] = nrm((RH, RH), RH)
        inp['rb2'] = jnp.zeros((RH,), jnp.float32)
        inp['rg2'] = jnp.ones((RH,), jnp.float32)
        inp['rbe2'] = jnp.zeros((RH,), jnp.float32)
        inp['rw3'] = nrm((RH, WN), RH)
        inp['roff'] = 0.1 * jax.random.normal(next(ks), (WN,), jnp.float32)
        inp['lin_ws'] = nrm((DS, H * A + H * H0), DS)
        inp['lin_bs'] = jnp.zeros((H * A + H * H0,), jnp.float32)
        inp['lin_wv'] = nrm((DV, H * H1), DV)
        inp['alpha_dot'] = nrm((H, A), A)
        inp['proj_ws'] = nrm((H * H0, C0), H * H0)
        inp['proj_bs'] = jnp.zeros((C0,), jnp.float32)
        inp['proj_wv'] = nrm((H * H1, C1), H * H1)
        inp['f1_ws'] = nrm((C0, M0 + M1), C0)
        inp['f1_bs'] = jnp.zeros((M0 + M1,), jnp.float32)
        inp['f1_wv'] = nrm((C1, M1), C1)
        inp['f2_ws'] = nrm((M0, C0), M0)
        inp['f2_bs'] = jnp.zeros((C0,), jnp.float32)
        inp['f2_wv'] = nrm((M1, C1), M1)
        return inp
    _L3_gnn_all = _L3_gnn_setup()
    _L3_gnn_in = {k: v for k, v in _L3_gnn_all.items() if k in ('ln1_w0', 'ln1_b0', 'ln1_w1', 'ln2_w0', 'ln2_b0', 'ln2_w1', 'msrc_ws', 'msrc_wv', 'mdst_ws', 'mdst_bs', 'mdst_wv', 'rw1', 'rb1', 'rg1', 'rbe1', 'rw2', 'rb2', 'rg2', 'rbe2', 'rw3', 'roff', 'lin_ws', 'lin_bs', 'lin_wv', 'alpha_dot', 'proj_ws', 'proj_bs', 'proj_wv', 'f1_ws', 'f1_bs', 'f1_wv', 'f2_ws', 'f2_bs', 'f2_wv')}
    del _L3_gnn_all
    return {'x': x, 'src': src, 'dst': dst, 'edge_attr_16': edge_attr_16, 'edge_attr_3': edge_attr_3, 'edge_attr_4': edge_attr_4, 'edge_attr_64': edge_attr_64, 'node_vec1': node_vec1, 'L0_gnn_gamma_s': _L0_gnn_in['gamma_s'], 'L0_gnn_beta_s': _L0_gnn_in['beta_s'], 'L0_gnn_gamma_v': _L0_gnn_in['gamma_v'], 'L0_gnn_Ws_src': _L0_gnn_in['Ws_src'], 'L0_gnn_Wv_src': _L0_gnn_in['Wv_src'], 'L0_gnn_Ws_dst': _L0_gnn_in['Ws_dst'], 'L0_gnn_Wv_dst': _L0_gnn_in['Wv_dst'], 'L0_gnn_W_rbf': _L0_gnn_in['W_rbf'], 'L0_gnn_W_alpha': _L0_gnn_in['W_alpha'], 'L0_gnn_alpha_dot': _L0_gnn_in['alpha_dot'], 'L0_gnn_Ws_val': _L0_gnn_in['Ws_val'], 'L0_gnn_Wv_val': _L0_gnn_in['Wv_val'], 'L0_gnn_Wg': _L0_gnn_in['Wg'], 'L0_gnn_w2_ss': _L0_gnn_in['w2_ss'], 'L0_gnn_w2_sv': _L0_gnn_in['w2_sv'], 'L0_gnn_w2_vs': _L0_gnn_in['w2_vs'], 'L0_gnn_w2_vv0': _L0_gnn_in['w2_vv0'], 'L0_gnn_w2_vv1': _L0_gnn_in['w2_vv1'], 'L0_gnn_Ws_vlin': _L0_gnn_in['Ws_vlin'], 'L0_gnn_Wv_vlin': _L0_gnn_in['Wv_vlin'], 'L0_gnn_Wps': _L0_gnn_in['Wps'], 'L0_gnn_Wpv': _L0_gnn_in['Wpv'], 'L1_gnn_W_skip0': _L1_gnn_in['W_skip0'], 'L1_gnn_W_skip1': _L1_gnn_in['W_skip1'], 'L1_gnn_W_nl0': _L1_gnn_in['W_nl0'], 'L1_gnn_W_nl1': _L1_gnn_in['W_nl1'], 'L1_gnn_W_fc1': _L1_gnn_in['W_fc1'], 'L1_gnn_W_fc2': _L1_gnn_in['W_fc2'], 'L1_gnn_W_out_s': _L1_gnn_in['W_out_s'], 'L1_gnn_W_out_v': _L1_gnn_in['W_out_v'], 'L2_gnn_lin1_ws': _L2_gnn_in['lin1_ws'], 'L2_gnn_lin1_wv': _L2_gnn_in['lin1_wv'], 'L2_gnn_fc_w1': _L2_gnn_in['fc_w1'], 'L2_gnn_fc_w2': _L2_gnn_in['fc_w2'], 'L2_gnn_sc_ws': _L2_gnn_in['sc_ws'], 'L2_gnn_sc_wv': _L2_gnn_in['sc_wv'], 'L2_gnn_lin2_ws': _L2_gnn_in['lin2_ws'], 'L2_gnn_lin2_wv': _L2_gnn_in['lin2_wv'], 'L3_gnn_ln1_w0': _L3_gnn_in['ln1_w0'], 'L3_gnn_ln1_b0': _L3_gnn_in['ln1_b0'], 'L3_gnn_ln1_w1': _L3_gnn_in['ln1_w1'], 'L3_gnn_ln2_w0': _L3_gnn_in['ln2_w0'], 'L3_gnn_ln2_b0': _L3_gnn_in['ln2_b0'], 'L3_gnn_ln2_w1': _L3_gnn_in['ln2_w1'], 'L3_gnn_msrc_ws': _L3_gnn_in['msrc_ws'], 'L3_gnn_msrc_wv': _L3_gnn_in['msrc_wv'], 'L3_gnn_mdst_ws': _L3_gnn_in['mdst_ws'], 'L3_gnn_mdst_bs': _L3_gnn_in['mdst_bs'], 'L3_gnn_mdst_wv': _L3_gnn_in['mdst_wv'], 'L3_gnn_rw1': _L3_gnn_in['rw1'], 'L3_gnn_rb1': _L3_gnn_in['rb1'], 'L3_gnn_rg1': _L3_gnn_in['rg1'], 'L3_gnn_rbe1': _L3_gnn_in['rbe1'], 'L3_gnn_rw2': _L3_gnn_in['rw2'], 'L3_gnn_rb2': _L3_gnn_in['rb2'], 'L3_gnn_rg2': _L3_gnn_in['rg2'], 'L3_gnn_rbe2': _L3_gnn_in['rbe2'], 'L3_gnn_rw3': _L3_gnn_in['rw3'], 'L3_gnn_roff': _L3_gnn_in['roff'], 'L3_gnn_lin_ws': _L3_gnn_in['lin_ws'], 'L3_gnn_lin_bs': _L3_gnn_in['lin_bs'], 'L3_gnn_lin_wv': _L3_gnn_in['lin_wv'], 'L3_gnn_alpha_dot': _L3_gnn_in['alpha_dot'], 'L3_gnn_proj_ws': _L3_gnn_in['proj_ws'], 'L3_gnn_proj_bs': _L3_gnn_in['proj_bs'], 'L3_gnn_proj_wv': _L3_gnn_in['proj_wv'], 'L3_gnn_f1_ws': _L3_gnn_in['f1_ws'], 'L3_gnn_f1_bs': _L3_gnn_in['f1_bs'], 'L3_gnn_f1_wv': _L3_gnn_in['f1_wv'], 'L3_gnn_f2_ws': _L3_gnn_in['f2_ws'], 'L3_gnn_f2_bs': _L3_gnn_in['f2_bs'], 'L3_gnn_f2_wv': _L3_gnn_in['f2_wv']}

def reference(x, src, dst, edge_attr_16, edge_attr_3, edge_attr_4, edge_attr_64, node_vec1, L0_gnn_gamma_s, L0_gnn_beta_s, L0_gnn_gamma_v, L0_gnn_Ws_src, L0_gnn_Wv_src, L0_gnn_Ws_dst, L0_gnn_Wv_dst, L0_gnn_W_rbf, L0_gnn_W_alpha, L0_gnn_alpha_dot, L0_gnn_Ws_val, L0_gnn_Wv_val, L0_gnn_Wg, L0_gnn_w2_ss, L0_gnn_w2_sv, L0_gnn_w2_vs, L0_gnn_w2_vv0, L0_gnn_w2_vv1, L0_gnn_Ws_vlin, L0_gnn_Wv_vlin, L0_gnn_Wps, L0_gnn_Wpv, L1_gnn_W_skip0, L1_gnn_W_skip1, L1_gnn_W_nl0, L1_gnn_W_nl1, L1_gnn_W_fc1, L1_gnn_W_fc2, L1_gnn_W_out_s, L1_gnn_W_out_v, L2_gnn_lin1_ws, L2_gnn_lin1_wv, L2_gnn_fc_w1, L2_gnn_fc_w2, L2_gnn_sc_ws, L2_gnn_sc_wv, L2_gnn_lin2_ws, L2_gnn_lin2_wv, L3_gnn_ln1_w0, L3_gnn_ln1_b0, L3_gnn_ln1_w1, L3_gnn_ln2_w0, L3_gnn_ln2_b0, L3_gnn_ln2_w1, L3_gnn_msrc_ws, L3_gnn_msrc_wv, L3_gnn_mdst_ws, L3_gnn_mdst_bs, L3_gnn_mdst_wv, L3_gnn_rw1, L3_gnn_rb1, L3_gnn_rg1, L3_gnn_rbe1, L3_gnn_rw2, L3_gnn_rb2, L3_gnn_rg2, L3_gnn_rbe2, L3_gnn_rw3, L3_gnn_roff, L3_gnn_lin_ws, L3_gnn_lin_bs, L3_gnn_lin_wv, L3_gnn_alpha_dot, L3_gnn_proj_ws, L3_gnn_proj_bs, L3_gnn_proj_wv, L3_gnn_f1_ws, L3_gnn_f1_bs, L3_gnn_f1_wv, L3_gnn_f2_ws, L3_gnn_f2_bs, L3_gnn_f2_wv):
    import jax
    import jax.numpy as jnp

    def _L0_gnn_ref(node, rbf, rsh, gamma_s, beta_s, gamma_v, Ws_src, Wv_src, Ws_dst, Wv_dst, W_rbf, W_alpha, alpha_dot, Ws_val, Wv_val, Wg, w2_ss, w2_sv, w2_vs, w2_vv0, w2_vv1, Ws_vlin, Wv_vlin, Wps, Wpv, edge_index):
        import jax, jax.numpy as jnp
        import numpy as np
        N, E = (625, 10000)
        CS, CV = (64, 32)
        AS_, AV, H = (16, 8, 4)
        NB = 16
        SQRT3 = 1.7320508075688772
        SQRT2 = 1.4142135623730951
        EPS = 1e-05

        def _cg_tp(s, v, y0, y1, w_ss, w_sv, w_vs, w_vv0, w_vv1):
            out_s = jnp.concatenate([w_ss * s * y0[:, None], w_vv0 * (jnp.einsum('eci,ei->ec', v, y1) / SQRT3)], axis=-1)
            out_v = jnp.concatenate([(w_sv * s)[:, :, None] * y1[:, None, :], (w_vs * jnp.ones_like(v[..., 0]))[..., None] * v * y0[:, None, None], (w_vv1 * jnp.ones_like(v[..., 0]))[..., None] * (jnp.cross(v, y1[:, None, :]) / SQRT2)], axis=1)
            return (out_s, out_v)

        def _equiv_layernorm(s, v, gamma_s, beta_s, gamma_v):
            mu = jnp.mean(s, axis=-1, keepdims=True)
            var = jnp.var(s, axis=-1, keepdims=True)
            s_n = (s - mu) * jax.lax.rsqrt(var + EPS) * gamma_s + beta_s
            rms = jnp.sqrt(jnp.mean(jnp.sum(v * v, axis=-1), axis=-1, keepdims=True) + EPS)
            v_n = v / rms[..., None] * gamma_v[None, :, None]
            return (s_n, v_n)
        n = node.shape[0]
        e = rsh.shape[0]
        s = node[:, :CS]
        v = node[:, CS:].reshape(n, CV, 3)
        s_n, v_n = _equiv_layernorm(s, v, gamma_s, beta_s, gamma_v)
        src, dst = (edge_index[0], edge_index[1])
        msg_s = (s_n @ Ws_src)[src] + (s_n @ Ws_dst)[dst]
        msg_v = jnp.einsum('ncx,cd->ndx', v_n, Wv_src)[src] + jnp.einsum('ncx,cd->ndx', v_n, Wv_dst)[dst]
        y0, y1 = (rsh[:, 0], rsh[:, 1:4])
        w1 = rbf @ W_rbf
        m1_s, m1_v = _cg_tp(msg_s, msg_v, y0, y1, w1[:, :CS], w1[:, CS:2 * CS], w1[:, 2 * CS:2 * CS + CV], w1[:, 2 * CS + CV:2 * CS + 2 * CV], w1[:, 2 * CS + 2 * CV:])
        a = (m1_s @ W_alpha).reshape(e, H, AS_)
        a = jnp.where(a > 0, a, 0.2 * a)
        a = jnp.sum(a * alpha_dot, axis=-1, keepdims=True)
        amax = jax.ops.segment_max(a, dst, num_segments=n)
        amax = jnp.where(jnp.isfinite(amax), amax, 0.0)
        ex = jnp.exp(a - amax[dst])
        den = jax.ops.segment_sum(ex, dst, num_segments=n)
        alpha = ex / (den[dst] + 1e-16)
        val_s = m1_s @ Ws_val
        val_v = jnp.einsum('ecx,cd->edx', m1_v, Wv_val)
        val_v = val_v * jax.nn.sigmoid(val_s @ Wg)[..., None]
        val_s = jax.nn.sigmoid(val_s)
        m2_s, m2_v = _cg_tp(val_s, val_v, y0, y1, w2_ss, w2_sv, w2_vs, w2_vv0, w2_vv1)
        hs = (m2_s @ Ws_vlin).reshape(e, H, AS_)
        hv = jnp.einsum('ecx,cd->edx', m2_v, Wv_vlin).reshape(e, H, AV, 3)
        h = jnp.concatenate([hs, hv.reshape(e, H, AV * 3)], axis=-1)
        agg = jax.ops.segment_sum(alpha * h, dst, num_segments=n)
        agg_s = agg[:, :, :AS_].reshape(n, H * AS_)
        agg_v = agg[:, :, AS_:].reshape(n, H * AV, 3)
        out = node + jnp.concatenate([agg_s @ Wps, jnp.einsum('ncx,cd->ndx', agg_v, Wpv).reshape(n, CV * 3)], axis=-1)
        return out

    def _L1_gnn_ref(node_feature, edge_attr, edge_feature, W_skip0, W_skip1, W_nl0, W_nl1, W_fc1, W_fc2, W_out_s, W_out_v, edge_index):
        import jax, jax.numpy as jnp
        import numpy as np
        N_NODES = 10000
        N_EDGES = 10000
        MUL0, MUL1 = (64, 32)
        EDGE_DIM = 64
        W_NUMEL = 224
        DENOM = 32.0
        SQRT3 = 3.0 ** 0.5
        INV_SQRT3 = 1.0 / SQRT3
        INV_SQRT2 = 2.0 ** (-0.5)

        def _forward(node_feature, edge_attr, edge_feature, W_skip0, W_skip1, W_nl0, W_nl1, W_fc1, W_fc2, W_out_s, W_out_v, edge_index):
            N = node_feature.shape[0]
            E = edge_attr.shape[0]
            s = node_feature[:, :MUL0]
            v = node_feature[:, MUL0:].reshape(N, MUL1, 3)
            skip_s = s @ W_skip0
            skip_v = jnp.einsum('nmi,mk->nki', v, W_skip1)
            s = s @ W_nl0
            v = jnp.einsum('nmi,mk->nki', v, W_nl1)
            rhat = edge_attr / jnp.linalg.norm(edge_attr, axis=-1, keepdims=True)
            sh1 = SQRT3 * rhat
            w = jax.nn.relu(edge_feature @ W_fc1) @ W_fc2
            w0, w1, w2, w3, w4 = jnp.split(w, [64, 128, 160, 192], axis=-1)
            src, dst = (edge_index[0], edge_index[1])
            xs = s[dst]
            xv = v[dst]
            out0a = w0 * xs
            out0b = w3 * (jnp.einsum('emi,ei->em', xv, sh1) * INV_SQRT3)
            out1a = (w1 * xs)[:, :, None] * sh1[:, None, :]
            out1b = w2[:, :, None] * xv
            out1c = w4[:, :, None] * (jnp.cross(xv, sh1[:, None, :]) * INV_SQRT2)
            tp = jnp.concatenate([out0a, out0b, out1a.reshape(E, -1), out1b.reshape(E, -1), out1c.reshape(E, -1)], axis=-1)
            agg = jax.ops.segment_sum(tp, src, num_segments=N) / DENOM
            agg_s = agg[:, :96]
            agg_v = agg[:, 96:].reshape(N, 128, 3)
            out_s = agg_s @ W_out_s + skip_s
            out_v = jnp.einsum('nmi,mk->nki', agg_v, W_out_v) + skip_v
            fs = jax.nn.silu(out_s[:, :MUL0])
            gate = jax.nn.sigmoid(out_s[:, MUL0:MUL0 + 32])
            gv = gate[:, :, None] * out_v
            return jnp.concatenate([fs, gv.reshape(N, -1)], axis=-1)
        return _forward(node_feature, edge_attr, edge_feature, W_skip0, W_skip1, W_nl0, W_nl1, W_fc1, W_fc2, W_out_s, W_out_v, edge_index)

    def _L2_gnn_ref(node_features, node_attr, edge_src, edge_dst, edge_attr, edge_scalars, lin1_ws, lin1_wv, fc_w1, fc_w2, sc_ws, sc_wv, lin2_ws, lin2_wv):
        import jax, jax.numpy as jnp
        import numpy as np
        N, E = (1250, 20000)
        S_IN, V_IN = (64, 32)
        S_MID, V_MID = (96, 128)
        S_OUT, V_OUT = (96, 32)
        R = 64
        FC_HID = 64
        W_NUMEL = 64 + 64 + 32 + 32 + 32
        NUM_NEIGHBORS = 16.0

        def _inv(d):
            return 1.0 / jnp.sqrt(jnp.float32(d))

        def _forward(node_features, node_attr, edge_attr, edge_scalars, lin1_ws, lin1_wv, fc_w1, fc_w2, sc_ws, sc_wv, lin2_ws, lin2_wv, edge_src, edge_dst):
            n = node_features.shape[0]
            s = node_features[:, :S_IN]
            v = node_features[:, S_IN:].reshape(n, V_IN, 3)
            a = node_attr
            sc_s = s @ sc_ws * a * _inv(S_IN)
            sc_v = jnp.einsum('nci,cd->ndi', v, sc_wv) * a[:, :, None] * _inv(V_IN)
            h_s = s @ lin1_ws * a * _inv(S_IN)
            h_v = jnp.einsum('nci,cd->ndi', v, lin1_wv) * a[:, :, None] * _inv(V_IN)
            hid = jax.nn.silu(edge_scalars @ fc_w1 * _inv(R))
            w = hid @ fc_w2 * _inv(FC_HID)
            w1, w2, w3, w4, w5 = jnp.split(w, [64, 128, 160, 192], axis=-1)
            es = h_s[edge_src]
            ev = h_v[edge_src]
            e0 = edge_attr[:, :1]
            e1 = edge_attr[:, 1:4]
            m_s1 = w1 * es * e0
            m_s2 = w4 * jnp.einsum('eci,ei->ec', ev, e1) * _inv(3)
            m_v1 = (w2 * es)[:, :, None] * e1[:, None, :]
            m_v2 = w3[:, :, None] * ev * e0[:, :, None]
            m_v3 = w5[:, :, None] * jnp.cross(ev, e1[:, None, :]) * _inv(2)
            mid_s = jnp.concatenate([m_s1, m_s2], axis=-1)
            mid_v = jnp.concatenate([m_v1, m_v2, m_v3], axis=1)
            inv_nn = 1.0 / jnp.sqrt(jnp.float32(NUM_NEIGHBORS))
            agg_s = jax.ops.segment_sum(mid_s, edge_dst, num_segments=n) * inv_nn
            agg_v = jax.ops.segment_sum(mid_v, edge_dst, num_segments=n) * inv_nn
            o_s = agg_s @ lin2_ws * a * _inv(S_MID)
            o_v = jnp.einsum('nci,cd->ndi', agg_v, lin2_wv) * a[:, :, None] * _inv(V_MID)
            pre_s = sc_s + o_s
            pre_v = sc_v + o_v
            scalars = jax.nn.silu(pre_s[:, :64])
            gates = jax.nn.sigmoid(pre_s[:, 64:96])
            gated = gates[:, :, None] * pre_v
            return jnp.concatenate([scalars, gated.reshape(n, 3 * V_OUT)], axis=-1)
        return _forward(node_features, node_attr, edge_attr, edge_scalars, lin1_ws, lin1_wv, fc_w1, fc_w2, sc_ws, sc_wv, lin2_ws, lin2_wv, edge_src, edge_dst)

    def _L3_gnn_ref(node_input, node_attr, edge_vec, edge_scalars, edge_src, edge_dst, ln1_w0, ln1_b0, ln1_w1, ln2_w0, ln2_b0, ln2_w1, msrc_ws, msrc_wv, mdst_ws, mdst_bs, mdst_wv, rw1, rb1, rg1, rbe1, rw2, rb2, rg2, rbe2, rw3, roff, lin_ws, lin_bs, lin_wv, alpha_dot, proj_ws, proj_bs, proj_wv, f1_ws, f1_bs, f1_wv, f2_ws, f2_bs, f2_wv):
        import jax, jax.numpy as jnp
        import numpy as np
        N, E = (10000, 5000)
        C0, C1 = (64, 32)
        H, A = (8, 8)
        H0, H1 = (8, 4)
        M0, M1 = (128, 64)
        NG, RH = (64, 64)
        WN = C0 + C0 + C1 + C1 + C1
        DS, DV = (C0 + C1, C0 + 2 * C1)
        EPS = 1e-05
        SQ3 = np.float32(np.sqrt(3.0))
        SQ2 = np.float32(np.sqrt(2.0))

        def _split(x):
            return (x[:, :C0], x[:, C0:].reshape(x.shape[0], C1, 3))

        def _merge(s, v):
            return jnp.concatenate([s, v.reshape(v.shape[0], -1)], axis=1)

        def _eq_ln(x, w0, b0, w1):
            s, v = _split(x)
            s = s - s.mean(axis=1, keepdims=True)
            s = s * jax.lax.rsqrt(jnp.square(s).mean(axis=1, keepdims=True) + EPS) * w0 + b0
            v = v * jax.lax.rsqrt(jnp.square(v).mean(axis=(1, 2), keepdims=True) + EPS) * w1[None, :, None]
            return (s, v)

        def _eq_lin(s, v, ws, bs, wv):
            return (s @ ws + bs, jnp.einsum('nud,uk->nkd', v, wv))

        def _ln(x, g, b):
            xc = x - x.mean(-1, keepdims=True)
            return xc * jax.lax.rsqrt(jnp.square(xc).mean(-1, keepdims=True) + EPS) * g + b

        def _smooth_leaky(x, alpha=0.2):
            return 0.5 * (1 + alpha) * x + 0.5 * (1 - alpha) * x * (2.0 * jax.nn.sigmoid(x) - 1.0)

        def _forward(node_input, node_attr, edge_vec, edge_scalars, edge_src, edge_dst, ln1_w0, ln1_b0, ln1_w1, ln2_w0, ln2_b0, ln2_w1, msrc_ws, msrc_wv, mdst_ws, mdst_bs, mdst_wv, rw1, rb1, rg1, rbe1, rw2, rb2, rg2, rbe2, rw3, roff, lin_ws, lin_bs, lin_wv, alpha_dot, proj_ws, proj_bs, proj_wv, f1_ws, f1_bs, f1_wv, f2_ws, f2_bs, f2_wv):
            n = node_input.shape[0]
            s, v = _eq_ln(node_input, ln1_w0, ln1_b0, ln1_w1)
            src_s = s @ msrc_ws
            src_v = jnp.einsum('nud,uk->nkd', v, msrc_wv)
            dst_s = s @ mdst_ws + mdst_bs
            dst_v = jnp.einsum('nud,uk->nkd', v, mdst_wv)
            ms = src_s[edge_src] + dst_s[edge_dst]
            mv = src_v[edge_src] + dst_v[edge_dst]
            h = jax.nn.silu(_ln(edge_scalars @ rw1 + rb1, rg1, rbe1))
            h = jax.nn.silu(_ln(h @ rw2 + rb2, rg2, rbe2))
            w = h @ rw3 + roff
            rhat = edge_vec * jax.lax.rsqrt(jnp.sum(jnp.square(edge_vec), -1, keepdims=True) + 1e-12)
            Y1 = SQ3 * rhat
            w1, w2, w3, w4, w5 = jnp.split(w, [C0, 2 * C0, 2 * C0 + C1, 2 * C0 + 2 * C1], axis=1)
            o0a = w1 * ms
            o0b = w4 * (jnp.einsum('eud,ed->eu', mv, Y1) / SQ3)
            o1a = (w2 * ms)[:, :, None] * Y1[:, None, :]
            o1b = w3[:, :, None] * mv
            o1c = w5[:, :, None] * (jnp.cross(mv, Y1[:, None, :]) / SQ2)
            ds = jnp.concatenate([o0a, o0b], axis=1)
            dv = jnp.concatenate([o1a, o1b, o1c], axis=1)
            ls, lv = _eq_lin(ds, dv, lin_ws, lin_bs, lin_wv)
            e = ls.shape[0]
            alpha = ls[:, :H * A].reshape(e, H, A)
            vs = ls[:, H * A:].reshape(e, H, H0)
            vv = lv.reshape(e, H, H1, 3)
            a = jnp.einsum('ehk,hk->eh', _smooth_leaky(alpha), alpha_dot)
            amax = jax.lax.stop_gradient(jax.ops.segment_max(a, edge_dst, num_segments=n))
            a = jnp.exp(a - amax[edge_dst])
            a = a / (jax.ops.segment_sum(a, edge_dst, num_segments=n)[edge_dst] + 1e-12)
            ns = jax.ops.segment_sum(vs * a[..., None], edge_dst, num_segments=n).reshape(n, H * H0)
            nv = jax.ops.segment_sum(vv * a[..., None, None], edge_dst, num_segments=n).reshape(n, H * H1, 3)
            ps, pv = _eq_lin(ns, nv, proj_ws, proj_bs, proj_wv)
            x = node_input + _merge(ps, pv)
            s2, v2 = _eq_ln(x, ln2_w0, ln2_b0, ln2_w1)
            a0 = node_attr[:, :1]
            fs, fv = _eq_lin(s2, v2, f1_ws, f1_bs, f1_wv)
            fs = fs * a0
            fv = fv * a0[:, :, None]
            sc = jax.nn.silu(fs[:, :M0])
            fv = fv * jax.nn.sigmoid(fs[:, M0:])[:, :, None]
            os_, ov = _eq_lin(sc, fv, f2_ws, f2_bs, f2_wv)
            os_ = os_ * a0
            ov = ov * a0[:, :, None]
            return x + _merge(os_, ov)
        return _forward(node_input, node_attr, edge_vec, edge_scalars, edge_src, edge_dst, ln1_w0, ln1_b0, ln1_w1, ln2_w0, ln2_b0, ln2_w1, msrc_ws, msrc_wv, mdst_ws, mdst_bs, mdst_wv, rw1, rb1, rg1, rbe1, rw2, rb2, rg2, rbe2, rw3, roff, lin_ws, lin_bs, lin_wv, alpha_dot, proj_ws, proj_bs, proj_wv, f1_ws, f1_bs, f1_wv, f2_ws, f2_bs, f2_wv)
    edge_index = jnp.stack([src, dst])
    h = jnp.maximum(_layernorm(x, axis=-1), 0.0)
    x = x + _L0_gnn_ref(h, edge_attr_16, edge_attr_4, L0_gnn_gamma_s, L0_gnn_beta_s, L0_gnn_gamma_v, L0_gnn_Ws_src, L0_gnn_Wv_src, L0_gnn_Ws_dst, L0_gnn_Wv_dst, L0_gnn_W_rbf, L0_gnn_W_alpha, L0_gnn_alpha_dot, L0_gnn_Ws_val, L0_gnn_Wv_val, L0_gnn_Wg, L0_gnn_w2_ss, L0_gnn_w2_sv, L0_gnn_w2_vs, L0_gnn_w2_vv0, L0_gnn_w2_vv1, L0_gnn_Ws_vlin, L0_gnn_Wv_vlin, L0_gnn_Wps, L0_gnn_Wpv, edge_index)
    h = jnp.maximum(_layernorm(x, axis=-1), 0.0)
    x = x + _L1_gnn_ref(h, edge_attr_3, edge_attr_64, L1_gnn_W_skip0, L1_gnn_W_skip1, L1_gnn_W_nl0, L1_gnn_W_nl1, L1_gnn_W_fc1, L1_gnn_W_fc2, L1_gnn_W_out_s, L1_gnn_W_out_v, edge_index)
    h = jnp.maximum(_layernorm(x, axis=-1), 0.0)
    x = x + _L2_gnn_ref(h, node_vec1, src, dst, edge_attr_4, edge_attr_64, L2_gnn_lin1_ws, L2_gnn_lin1_wv, L2_gnn_fc_w1, L2_gnn_fc_w2, L2_gnn_sc_ws, L2_gnn_sc_wv, L2_gnn_lin2_ws, L2_gnn_lin2_wv)
    h = jnp.maximum(_layernorm(x, axis=-1), 0.0)
    x = x + _L3_gnn_ref(h, node_vec1, edge_attr_3, edge_attr_64, src, dst, L3_gnn_ln1_w0, L3_gnn_ln1_b0, L3_gnn_ln1_w1, L3_gnn_ln2_w0, L3_gnn_ln2_b0, L3_gnn_ln2_w1, L3_gnn_msrc_ws, L3_gnn_msrc_wv, L3_gnn_mdst_ws, L3_gnn_mdst_bs, L3_gnn_mdst_wv, L3_gnn_rw1, L3_gnn_rb1, L3_gnn_rg1, L3_gnn_rbe1, L3_gnn_rw2, L3_gnn_rb2, L3_gnn_rg2, L3_gnn_rbe2, L3_gnn_rw3, L3_gnn_roff, L3_gnn_lin_ws, L3_gnn_lin_bs, L3_gnn_lin_wv, L3_gnn_alpha_dot, L3_gnn_proj_ws, L3_gnn_proj_bs, L3_gnn_proj_wv, L3_gnn_f1_ws, L3_gnn_f1_bs, L3_gnn_f1_wv, L3_gnn_f2_ws, L3_gnn_f2_bs, L3_gnn_f2_wv)
    return x

_drawn_inputs = setup_inputs


def setup_inputs(seed=0):
    import zlib

    import numpy as np

    out = dict(_drawn_inputs(seed))
    spreads = {'L0_gnn_gamma_s': (1.0, 0.6),
     'L0_gnn_beta_s': (0.0, 0.8),
     'L0_gnn_gamma_v': (1.0, 0.6),
     'L3_gnn_ln1_w0': (1.0, 0.6),
     'L3_gnn_ln1_b0': (0.0, 0.432),
     'L3_gnn_ln1_w1': (1.0, 0.6),
     'L3_gnn_ln2_w0': (1.0, 0.6),
     'L3_gnn_ln2_b0': (0.0, 0.8),
     'L3_gnn_ln2_w1': (1.0, 0.6),
     'L3_gnn_mdst_bs': (0.0, 0.8),
     'L3_gnn_rb1': (0.0, 0.303),
     'L3_gnn_rg1': (1.0, 0.2),
     'L3_gnn_rbe1': (0.0, 0.374),
     'L3_gnn_rb2': (0.0, 0.1),
     'L3_gnn_rg2': (1.0, 0.2),
     'L3_gnn_rbe2': (0.0, 0.404),
     'L3_gnn_lin_bs': (0.0, 0.313),
     'L3_gnn_proj_bs': (0.0, 0.283),
     'L3_gnn_f1_bs': (0.0, 0.8),
     'L3_gnn_f2_bs': (0.0, 0.523)}
    factors = {'L0_gnn_w2_vv1': 2.681,
     'L1_gnn_W_nl1': 3.436,
     'L1_gnn_W_fc1': 3.119,
     'L1_gnn_W_out_v': 3.321}
    for name, (base, spread) in spreads.items():
        noise = np.random.default_rng([zlib.crc32(name.encode()), seed]).standard_normal(out[name].shape)
        drawn = base * np.exp(spread * noise) if base else spread * noise
        out[name] = jnp.asarray(drawn.astype(out[name].dtype))
    for name, factor in factors.items():
        out[name] = (out[name] * factor).astype(out[name].dtype)
    return out
```

```python
from contextlib import ExitStack

import concourse.bass as bass
from concourse import mybir

F32 = mybir.dt.float32
I32 = mybir.dt.int32
ALU = mybir.AluOpType
ACT = mybir.ActivationFunctionType
AX_X = mybir.AxisListType.X
ds = bass.ds

N, E = 3125, 50000
CS, CV = 64, 32
FV = 3 * CV
FN = CS + FV
WN = 2 * CS + 3 * CV
PB, NB = 125, 25
EP, EC = 125, 400
GE = 256
NG = E // GE + NB
SLOTS = NG * GE
RING = 4
DEEP = 5
BIG = 1.0e30
EPS = 1e-5
SQ2, SQ3 = 2.0 ** 0.5, 3.0 ** 0.5
assert PB * NB == N and EP * EC == E and (E + NB * (GE - 1)) // GE <= NG and NG % RING == 0

R_A64, R_A16, R_Y, R_U1, R_U3, R_SRC, R_DST, R_LSRC, R_LDST = 0, 64, 80, 84, 87, 90, 91, 92, 93
RH, RW = 84, 94

P_A, P_C, P_D, P_B, P_X, PW = 0, 64, 224, 320, 384, 640
MW = 512

CONST_COLS = dict(ident=128, before=PB, nodes=PB, blocks=NB, groups=NG)
WEIGHTS = dict(
    l0_src_s=(CS, CS), l0_src_v=(FV, FV), l0_dst_s=(CS, CS), l0_dst_v=(FV, FV), l0_rbf=(16, WN),
    l0_as=(96, 160), l0_val_t=(CS, 96), l0_gate=(CS, CV), l0_val_v=(128, CV), l0_vlin_s=(96, CS),
    l0_vlin_v=(128, CV), l0_ps=(CS, CS), l0_pv=(FV, FV), l0_w2s=(96, 1), l0_w2v=(128, 1),
    l1_skip_s=(CS, 96), l1_skip_v=(FV, FV), l1_in_s=(CS, CS), l1_in_v=(FV, FV), l1_fc1=(64, 64),
    l1_fc2=(64, WN), l1_out_s=(96, 96), l1_out_v=(128, CV),
    l2_skip_s=(CS, 96), l2_skip_v=(FV, FV), l2_in_s=(CS, CS), l2_in_v=(FV, FV), l2_fc1=(64, 64),
    l2_fc2=(64, WN), l2_out_s=(96, 96), l2_out_v=(128, CV),
    l3_src_s=(CS, CS), l3_src_v=(FV, FV), l3_dst_s=(CS, CS), l3_dst_v=(FV, FV),
    l3_rw1=(65, 64), l3_rw2=(65, 64), l3_rw3=(65, WN), l3_rg1=(64, 1), l3_rb1=(64, 1),
    l3_rg2=(64, 1), l3_rb2=(64, 1), l3_lin_s=(97, 128), l3_lin_v=(128, CV),
    l3_proj_s=(CS, CS), l3_proj_v=(FV, FV), l3_f1_s=(CS, 192), l3_f1_v=(FV, 192),
    l3_f2_s=(128, CS), l3_f2_v=(64, CV),
)
ROWS = dict(
    l0_gs=CS, l0_bs=CS, l0_gv=FV, l0_adot=64, l3_gs1=CS, l3_bs1=CS, l3_gv1=FV, l3_gs2=CS,
    l3_bs2=CS, l3_gv2=FV, l3_adot=64, l3_dst_b=CS, l3_proj_b=CS, l3_f1_b=192, l3_f2_b=CS,
)


def offsets(columns):
    at, out = 0, {}
    for name, n in columns.items():
        out[name] = (at, n)
        at += n
    return out, at


CONST_AT, CONST_W = offsets(CONST_COLS)
WEIGHT_AT, WEIGHT_W = offsets({k: c for k, (_, c) in WEIGHTS.items()})
ROW_AT, ROW_W = offsets(ROWS)


class Chain:

    def __init__(self, eng, sem):
        self.eng, self.sem, self.n = eng, sem, 0

    def add(self, ins):
        ins.then_inc(self.sem, 1)
        self.n += 1

    def then(self, ins):
        self.add(ins)
        self.eng.wait_ge(self.sem, self.n)


def group(j, c, lag, ring=RING, count=NG):
    g = ring * j + (c - lag)
    if isinstance(g, int) and not 0 <= g < count:
        return None
    return g, (c - lag) % ring, j + (c - lag) // ring


def past(g, n):
    return g >= n if isinstance(g, int) else True


def steps(eng, body, lag, ring=RING, count=NG):
    first = -(-(lag + ring) // ring)
    for j in range(first):
        for c in range(ring):
            body(j, c)
    with eng.Fori(first, count // ring) as j:
        for c in range(ring):
            body(j, c)
    for i in range(count - count % ring, count + lag):
        body(i // ring, i % ring)


class Kernel:
    def __init__(self, nc, stack, args):
        self.nc = nc
        self.args = args
        self.stack = stack
        self.scope = stack
        self.sems = []
        self.tag = "k"
        d = nc.dram_tensor
        self.by_dst = d("rows_by_dst", (SLOTS, RW), F32, kind="Internal").ap()
        self.by_src = d("rows_by_src", (SLOTS, RW), F32, kind="Internal").ap()
        self.table = d("message_table", (N, FN), F32, kind="Internal").ap()
        self.hidden = d("radial_hidden", (NG * 64, GE), F32, kind="Internal").ap()
        self.x = self.sb("x", [PB, NB, FN])
        self.h = self.sb("h", [PB, NB, FN])
        self.c = self.sb("consts", [128, CONST_W])
        self.w = self.sb("weights", [128, WEIGHT_W])
        self.r = self.sb("rows", [128, ROW_W])
        self.block_of_dst = self.sb("block_of_dst", [1, NG], I32)
        self.block_of_src = self.sb("block_of_src", [1, NG], I32)
        self.a0 = self.sb("node_attr", [PB, NB])
        self.half = self.sb("minus_half", [128, 512])

    def sb(self, name, shape, dt=F32):
        return self.scope.enter_context(self.nc.sbuf_tensor(f"{self.tag}_{name}", shape, dt))

    def ps(self, name, shape):
        return self.scope.enter_context(self.nc.psum_tensor(f"{self.tag}_{name}", shape, F32))

    def sem(self, name):
        s = self.nc.alloc_semaphore(name=f"{self.tag}_{name}")
        self.sems.append(s)
        return s

    def const(self, name, rows=128):
        at, n = CONST_AT[name]
        return self.c[0:rows, at:at + n]

    def wt(self, name, lo=0, hi=None):
        at, n = WEIGHT_AT[name]
        return self.w[lo:WEIGHTS[name][0] if hi is None else hi, at:at + n]

    def wt_pair(self, a, b):
        at = WEIGHT_AT[a][0]
        assert WEIGHT_AT[b][0] == at + 1
        return self.w[0:WEIGHTS[a][0], at:at + 2]

    def row(self, name, rows=128):
        at, n = ROW_AT[name]
        return self.r[0:rows, at:at + n]

    def blockrow(self, name):
        return self.row(name, PB).unsqueeze(1).to_broadcast([PB, NB, ROWS[name]])

    def phase(self, tag):
        return Phase(self, tag)


class Phase:

    def __init__(self, k, tag):
        self.k, self.tag = k, tag

    def __enter__(self):
        self.old = (self.k.scope, self.k.tag, self.k.sems)
        self.k.sems = []
        self.stack = ExitStack()
        self.stack.__enter__()
        self.k.scope, self.k.tag = self.stack, self.tag
        return self.k

    def __exit__(self, *e):
        done = self.k.sems
        self.k.scope, self.k.tag, self.k.sems = self.old
        self.stack.__exit__(*e)
        if done and e[0] is None:
            self.k.nc.clear_and_free_semaphores(done)
            self.k.nc.all_engine_barrier()


def prepare(k):
    nc = k.nc
    with k.phase("prep"), nc.Block() as block:
        loaded, scaled, gated, zeroed = (k.sem(n) for n in ("loaded", "scaled", "gated", "zeroed"))
        pg = k.ps("gate_product", [128, 512])
        mean = k.sb("row_mean", [128, 2])

        @block.sync
        def _(sp):
            for dst, src in ((k.x[:], k.args["x_rows"]), (k.c[:], k.args["consts"]),
                             (k.w[:], k.args["weights"]), (k.r[:], k.args["row_vectors"]),
                             (k.a0[:], k.args["node_attr"])):
                sp.dma_start(dst, src).then_inc(loaded, 16)
            sp.wait_ge(loaded, 80)

        @block.gpsimd
        def _(pool):
            pool.memset(k.half[:], -0.5).then_inc(zeroed, 1)

        @block.tensor
        def _(pe):
            pe.wait_ge(loaded, 80)
            pe.matmul(pg[0:96, 0:CV], k.wt("l0_val_t"), k.wt("l0_gate"), start=True, stop=True)\
                .then_inc(gated, 1)

        @block.vector
        def _(dve):
            ch = Chain(dve, scaled)
            dve.wait_ge(loaded, 80)
            dve.wait_ge(gated, 1)
            ch.then(dve.tensor_copy(k.wt("l0_as")[:, 128:160], pg[0:96, 0:CV]))

            def scale(name, lo, hi, by):
                ap = k.wt(name, lo, hi)
                ch.then(dve.tensor_scalar(ap, ap, by, None, ALU.mult))

            scale("l0_as", 64, 96, 1 / SQ3)
            scale("l0_val_v", 96, 128, 1 / SQ2)
            scale("l0_vlin_s", 0, 96, k.wt("l0_w2s"))
            scale("l0_vlin_s", 64, 96, 1 / SQ3)
            scale("l0_vlin_v", 0, 128, k.wt("l0_w2v"))
            scale("l0_vlin_v", 96, 128, 1 / SQ2)
            scale("l1_out_s", 0, 96, 1 / 32)
            scale("l1_out_v", 0, 64, SQ3 / 32)
            scale("l1_out_v", 64, 96, 1 / 32)
            scale("l1_out_v", 96, 128, SQ3 / SQ2 / 32)
            for n in ("l2_skip_s", "l2_in_s"):
                scale(n, 0, CS, 1 / 8)
            for n in ("l2_skip_v", "l2_in_v"):
                scale(n, 0, FV, 32 ** -0.5)
            scale("l2_out_s", 0, 64, 96 ** -0.5 / 512)
            scale("l2_out_s", 64, 96, 96 ** -0.5 / SQ3 / 512)
            scale("l2_out_v", 0, 96, 128 ** -0.5 / 512)
            scale("l2_out_v", 96, 128, 128 ** -0.5 / SQ2 / 512)
            scale("l3_lin_v", 0, 64, SQ3)
            scale("l3_lin_v", 96, 128, SQ3 / SQ2)
            scale("l3_rw2", 0, 64, 0.5)
            scale("l3_rw3", 0, 64, 0.5)
            for n, name in enumerate(("l3_rw1", "l3_rw2")):
                m = mean[0:65, n:n + 1]
                ch.then(dve.tensor_reduce(m, k.wt(name), AX_X, ALU.add))
                ch.then(dve.tensor_scalar(m, m, 1 / 64, None, ALU.mult))
                ch.then(dve.tensor_scalar(k.wt(name), k.wt(name), m, None, ALU.subtract))


def sort_edges(k):
    nc = k.nc
    CH = 8
    with k.phase("sort"):
        loaded, padded, counted, totalled, unit, fills = (
            k.sem(n) for n in ("loaded", "padded", "counted", "totalled", "unit", "fills"))
        pos = [k.sb(f"position{i}", [EP, EC], I32) for i in range(2)]
        tail = k.sb("tail", [EP, EC, RW - RH])
        with k.phase("count"):
            key_i = [k.sb(f"key_i{i}", [EP, EC], I32) for i in range(2)]
            vec = k.sb("vec", [EP, EC, 3])
            sq = k.sb("sq", [EP, EC, 3])
            n2 = k.sb("n2", [EP, 2, EC])
            zeros = k.sb("zeros", [EP, EC])
            bf = k.sb("block", [EP, EC])
            hot = k.sb("hot", [EP, NB, EC])
            rank = k.sb("rank", [EP, NB, EC])
            tot = k.sb("tot", [EP, NB])
            ones = k.sb("ones", [EP, EP])
            cnt_i = k.sb("cnt_i", [EP, NB], I32)
            ngr = k.sb("ngr", [EP, NB])
            inc = k.sb("inc", [EP, NB])
            base = k.sb("base", [EP, NB])
            gm = k.sb("gm", [1, NG, NB])
            gmf = k.sb("gmf", [1, NG])
            pad = k.sb("pad", [128, 22, RW])
            pc = k.ps("counts", [EP, 512])
            with nc.Block() as block:

                @block.sync
                def _(sp):
                    sp.dma_start(key_i[0][:], k.args["dst"]).then_inc(loaded, 16)
                    sp.dma_start(key_i[1][:], k.args["src"]).then_inc(loaded, 16)
                    sp.dma_start(vec[:], k.args["edge_vec"]).then_inc(loaded, 16)
                    sp.wait_ge(padded, 3)
                    n = 0
                    for t in (k.by_dst, k.by_src):
                        v = t.rearrange("(p c) w -> p c w", p=128)
                        for c in range(0, SLOTS // 128, 22):
                            sp.dma_start(v[:, c:c + 22, :], pad[:]).then_inc(fills, 16)
                            n += 16
                    sp.wait_ge(fills, n)

                @block.gpsimd
                def _(pool):
                    pool.memset(pad[:], 0.0).then_inc(padded, 1)
                    pool.memset(ones[:], 1.0).then_inc(padded, 1)
                    pool.wait_ge(padded, 1)
                    pool.memset(pad[:, :, R_LSRC:R_LDST + 1], -1.0).then_inc(padded, 1)
                    pool.wait_ge(unit, 3)
                    for i in range(2):
                        pool.tensor_tensor(n2[:, i, :], n2[:, i, :], k.half[0:EP, 0:EC], ALU.pow)\
                            .then_inc(unit, 1)

                @block.tensor
                def _(pe):
                    pe.wait_ge(padded, 3)
                    for i in range(2):
                        pe.wait_ge(totalled, 2 * i + 1)
                        pe.matmul(pc[:, 0:NB], k.const("before", EP), tot[:], start=True, stop=True)
                        pe.matmul(pc[:, NB:2 * NB], ones[:], tot[:], start=True, stop=True)\
                            .then_inc(totalled, 1)

                @block.vector
                def _(dve):
                    ch = Chain(dve, counted)
                    ch.then(dve.memset(zeros[:], 0.0))
                    dve.wait_ge(loaded, 48)
                    dve.tensor_tensor(sq[:], vec[:], vec[:], ALU.mult).then_inc(unit, 1)
                    dve.wait_ge(unit, 1)
                    dve.tensor_reduce(n2[:, 0, :], sq[:], AX_X, ALU.add).then_inc(unit, 1)
                    dve.wait_ge(unit, 2)
                    dve.tensor_scalar(n2[:, 1, :], n2[:, 0, :], 1e-12, None, ALU.add).then_inc(unit, 1)
                    for i, (raw, local) in enumerate(((R_DST, R_LDST), (R_SRC, R_LSRC))):
                        kf = tail[:, :, raw - RH]
                        ch.then(dve.tensor_copy(kf, key_i[i][:]))
                        ch.then(dve.tensor_scalar(bf[:], kf, float(PB), None, ALU.is_ge))
                        for b in range(2, NB):
                            ch.then(dve.scalar_tensor_tensor(bf[:], kf, float(PB * b), bf[:],
                                                             ALU.is_ge, ALU.add))
                        ch.add(dve.scalar_tensor_tensor(tail[:, :, local - RH], bf[:], -float(PB), kf,
                                                        ALU.mult, ALU.add))
                        ch.then(dve.tensor_tensor(
                            hot[:], bf[:].unsqueeze(1).to_broadcast([EP, NB, EC]),
                            k.const("blocks", EP).unsqueeze(2).to_broadcast([EP, NB, EC]),
                            ALU.is_equal))
                        for b in range(NB):
                            ch.add(dve.tensor_tensor_scan(rank[:, b, :], hot[:, b, :], zeros[:], 0.0,
                                                          ALU.add, ALU.add))
                        dve.wait_ge(counted, ch.n)
                        dve.tensor_copy(tot[:], rank[:, :, EC - 1]).then_inc(totalled, 1)
                        dve.wait_ge(totalled, 2 * i + 2)
                        ch.then(dve.tensor_scalar(ngr[:], pc[:, NB:2 * NB], float(GE - 1), None, ALU.add))
                        ch.then(dve.tensor_copy(cnt_i[:], ngr[:]))
                        ch.then(dve.tensor_scalar(cnt_i[:], cnt_i[:], GE.bit_length() - 1, None,
                                                  ALU.arith_shift_right))
                        ch.then(dve.tensor_copy(ngr[:], cnt_i[:]))
                        ch.then(dve.tensor_tensor_scan(inc[:], ngr[:], zeros[:, 0:NB], 0.0,
                                                       ALU.add, ALU.add))
                        ch.then(dve.tensor_tensor(inc[:], inc[:], ngr[:], ALU.subtract))
                        ch.then(dve.tensor_scalar(base[:], inc[:], float(GE), -1.0, ALU.mult, ALU.add))
                        ch.then(dve.tensor_tensor(base[:], base[:], pc[:, 0:NB], ALU.add))
                        ch.then(dve.tensor_tensor(rank[:], rank[:],
                                                  base[:].unsqueeze(2).to_broadcast([EP, NB, EC]), ALU.add))
                        ch.then(dve.tensor_tensor(rank[:], rank[:], hot[:], ALU.mult))
                        ch.then(dve.tensor_reduce(bf[:], rank[:].rearrange("p b c -> p c b"), AX_X, ALU.add))
                        ch.add(dve.tensor_copy(pos[i][:], bf[:]))
                        ch.then(dve.tensor_tensor(
                            gm[:], k.const("groups", 1).unsqueeze(2).to_broadcast([1, NG, NB]),
                            inc[0:1, :].unsqueeze(1).to_broadcast([1, NG, NB]), ALU.is_ge))
                        ch.then(dve.tensor_reduce(gmf[:], gm[:, :, 1:NB], AX_X, ALU.add))
                        ch.then(dve.tensor_copy((k.block_of_dst, k.block_of_src)[i][:], gmf[:]))
                    dve.wait_ge(unit, 5)
                    for i, col in enumerate((R_U1, R_U3)):
                        ch.add(dve.tensor_tensor(
                            tail[:, :, col - RH:col - RH + 3], vec[:],
                            n2[:, i, :].unsqueeze(2).to_broadcast([EP, EC, 3]), ALU.mult))

        with k.phase("place"):
            rows = [k.sb(f"row_buffer{i}", [EP, CH, RW]) for i in range(2)]
            idx = [k.sb(f"slot_index{i}", [EP, 2, CH], I32) for i in range(2)]
            row_in = [k.sem(f"row_in{i}") for i in range(2)]
            placed = [k.sem(f"placed{i}") for i in range(2)]
            ready, gate = k.sem("ready"), k.sem("gate")
            edge_rows = k.args["edge_rows"]
            per = 2 * CH * 16
            with nc.Block() as block:

                def each(eng, body):
                    for c in range(2):
                        body(0, c)
                    with eng.Fori(1, EC // CH // 2) as j:
                        for c in range(2):
                            body(j, c)

                @block.sync
                def _(sp):
                    def body(j, c):
                        if past(j, 1):
                            sp.wait_ge(placed[c], j * per)
                        sp.dma_start(rows[c][:, :, 0:RH], edge_rows[:, ds((2 * j + c) * CH, CH), :])\
                            .then_inc(row_in[c], 16)
                    each(sp, body)

                @block.vector
                def _(dve):
                    def body(j, c):
                        if past(j, 1):
                            dve.wait_ge(placed[c], j * per)
                        cols = ds((2 * j + c) * CH, CH)
                        dve.tensor_scalar(rows[c][:, :, RH:RW], tail[:, cols, :], 1.0, None, ALU.mult)\
                            .then_inc(ready, 1)
                        for i in range(2):
                            dve.tensor_copy(idx[c][:, i, :], pos[i][:, cols]).then_inc(ready, 1)
                    each(dve, body)

                @block.gpsimd
                def _(pool):
                    def body(j, c):
                        pool.wait_ge(row_in[c], (j + 1) * 16)
                        pool.wait_ge(ready, (2 * j + c) * 3 + 3)
                        pool.sem_inc(gate, 1)
                        for i, t in enumerate((k.by_dst, k.by_src)):
                            for n in range(CH):
                                pool.indirect_dma_start(
                                    out=t, out_offset=bass.IndirectOffsetOnAxis(ap=idx[c][:, i, n:n + 1], axis=0),
                                    in_=rows[c][:, n, :], in_offset=None).then_inc(placed[c], 16)
                    each(pool, body)
                    for c in range(2):
                        pool.wait_ge(placed[c], EC // CH // 2 * per)


def norm_nodes(k, tag, relu, source=None, target=None, gains=None, v_div=None):
    nc = k.nc
    with k.phase(tag), nc.Block() as block:
        done, powed = k.sem("done"), k.sem("powed")
        sq = k.sb("sq", [PB, NB, FN])
        var = k.sb("var", [PB, 3, NB])
        mean = k.sb("mean", [PB, 2, NB])
        marks = []

        def over(ap, n):
            return ap.unsqueeze(2).to_broadcast([PB, NB, n])

        @block.vector
        def _(dve):
            ch = Chain(dve, done)
            if relu:
                m, v = mean[:, 0, :], var[:, 0, :]
                ch.then(dve.tensor_reduce(m, k.x[:], AX_X, ALU.add))
                ch.then(dve.tensor_scalar(m, m, 1 / FN, None, ALU.mult))
                ch.then(dve.tensor_tensor(k.h[:], k.x[:], over(m, FN), ALU.subtract))
                ch.then(dve.tensor_tensor(sq[:], k.h[:], k.h[:], ALU.mult))
                ch.then(dve.tensor_reduce(v, sq[:], AX_X, ALU.add))
                ch.then(dve.tensor_scalar(v, v, 1 / FN, EPS, ALU.mult, ALU.add))
                marks.append((ch.n, v))
                dve.wait_ge(powed, len(marks))
                ch.then(dve.tensor_tensor(k.h[:], k.h[:], over(v, FN), ALU.mult))
                ch.then(dve.tensor_scalar(k.h[:], k.h[:], 0.0, None, ALU.max))
            if gains:
                m = mean[:, 1, :]
                s, v = slice(0, CS), slice(CS, FN)
                ch.then(dve.tensor_reduce(m, source[:, :, s], AX_X, ALU.add))
                ch.then(dve.tensor_scalar(m, m, 1 / CS, None, ALU.mult))
                ch.then(dve.tensor_tensor(target[:, :, s], source[:, :, s], over(m, CS), ALU.subtract))
                ch.add(dve.tensor_tensor(sq[:, :, s], target[:, :, s], target[:, :, s], ALU.mult))
                ch.then(dve.tensor_tensor(sq[:, :, v], source[:, :, v], source[:, :, v], ALU.mult))
                ch.add(dve.tensor_reduce(var[:, 1, :], sq[:, :, s], AX_X, ALU.add))
                ch.then(dve.tensor_reduce(var[:, 2, :], sq[:, :, v], AX_X, ALU.add))
                ch.add(dve.tensor_scalar(var[:, 1, :], var[:, 1, :], 1 / CS, EPS, ALU.mult, ALU.add))
                ch.add(dve.tensor_scalar(var[:, 2, :], var[:, 2, :], 1 / v_div, EPS, ALU.mult, ALU.add))
                marks.append((ch.n, var[:, 1:3, :]))
                dve.wait_ge(powed, len(marks))
                ch.add(dve.tensor_tensor(target[:, :, s], target[:, :, s], over(var[:, 1, :], CS), ALU.mult))
                ch.then(dve.tensor_tensor(target[:, :, v], source[:, :, v], over(var[:, 2, :], FV), ALU.mult))
                gs, bs, gv = (k.blockrow(n) for n in gains)
                ch.add(dve.tensor_tensor(target[:, :, v], target[:, :, v], gv, ALU.mult))
                ch.then(dve.tensor_tensor(target[:, :, s], target[:, :, s], gs, ALU.mult))
                ch.then(dve.tensor_tensor(target[:, :, s], target[:, :, s], bs, ALU.add))

        @block.gpsimd
        def _(pool):
            for at, v in marks:
                pool.wait_ge(done, at)
                n = v.shape[1] * v.shape[2] if len(v.shape) == 3 else v.shape[1]
                e = k.half[0:PB, 0:n]
                e = e.rearrange("p (a b) -> p a b", a=v.shape[1]) if len(v.shape) == 3 else e
                pool.tensor_tensor(v, v, e, ALU.pow).then_inc(powed, 1)


def node_linear(k, tag, width, fill, fills, slices, evacs, products, outs):
    nc = k.nc
    with k.phase(tag), nc.Block() as block:
        staged, turned, copied, multiplied, stored, gate = (
            k.sem(n) for n in ("staged", "turned", "copied", "multiplied", "stored", "gate"))
        stage = [k.sb(f"stage{c}", [PB, width]) for c in range(2)]
        banks = -(-len(slices) // 4)
        turned_sb = [k.sb(f"turned{c}", [128, banks * 4, 128]) for c in range(2)]
        pt = [k.ps(f"pt{c}", [128, banks * 4, 128]) for c in range(2)]
        po = [k.ps(f"po{c}", [128, 512]) for c in range(2)]

        @block.vector
        def _(dve):
            def body(j, c):
                g = group(j, c, 0, 2, NB)
                if g:
                    b, s, _ = g
                    if past(b, 2):
                        dve.wait_ge(turned, b - 1)
                    fill(dve, b, stage[s], staged)
                g = group(j, c, 1, 2, NB)
                if g:
                    b, s, _ = g
                    dve.wait_ge(multiplied, b + 1)
                    for lo, n, tile in outs:
                        dve.tensor_scalar(tile[:, ds(b, 1), :], po[s][0:PB, lo:lo + n].unsqueeze(1),
                                          1.0, None, ALU.mult).then_inc(stored, 1)
            steps(dve, body, 1, 2, NB)

        @block.tensor
        def _(pe):
            def body(j, c):
                g = group(j, c, 0, 2, NB)
                if g:
                    b, s, _ = g
                    pe.wait_ge(staged, fills * b + fills)
                    if past(b, 2):
                        pe.wait_ge(copied, len(evacs) * b - len(evacs))
                    pe.sem_inc(gate, 1)
                    for n, (lo, hi) in enumerate(slices):
                        last = pe.transpose(pt[s][0:hi - lo, n, 0:PB], stage[s][:, lo:hi],
                                            k.const("ident", PB)[:, 0:PB])
                    last.then_inc(turned, 1)
                g = group(j, c, 1, 2, NB)
                if g:
                    b, s, _ = g
                    pe.wait_ge(copied, len(evacs) * b + len(evacs))
                    if past(b, 2):
                        pe.wait_ge(stored, len(outs) * b - len(outs))
                    pe.sem_inc(gate, 1)
                    for n, rows, w, lo, start, stop in products:
                        last = pe.matmul(po[s][0:PB, lo:lo + w.shape[1]], turned_sb[s][0:rows, n, 0:PB],
                                         w, start=start, stop=stop, skip_group_check=True)
                    last.then_inc(multiplied, 1)
            steps(pe, body, 1, 2, NB)

        @block.scalar
        def _(act):
            def body(j, c):
                g = group(j, c, 0, 2, NB)
                if g:
                    b, s, _ = g
                    act.wait_ge(turned, b + 1)
                    if past(b, 2):
                        act.wait_ge(multiplied, b - 1)
                    for n, m, rows in evacs:
                        act.activation(turned_sb[s][0:rows, n:n + m, 0:PB], pt[s][0:rows, n:n + m, 0:PB],
                                       ACT.Copy).then_inc(copied, 1)
            steps(act, body, 1, 2, NB)


def copy_fill(tile, width):
    def fill(dve, b, stage, staged):
        dve.tensor_scalar(stage[:, 0:width].unsqueeze(1), tile[:, ds(b, 1), 0:width], 1.0, None,
                          ALU.mult).then_inc(staged, 1)
    return fill


SV_SLICES = [(0, CS), (CS, FN)]
SV_EVACS = [(0, 1, CS), (1, 1, FV)]


def write_table(k, tag, tile):
    nc = k.nc
    with k.phase(tag), nc.Block() as block:
        written, scaled = k.sem("written"), k.sem("scaled")

        @block.vector
        def _(dve):
            if tag == "l2_table":
                dve.tensor_tensor(tile[:], tile[:], k.a0[:].unsqueeze(2).to_broadcast([PB, NB, FN]),
                                  ALU.mult).then_inc(scaled, 1)

        @block.sync
        def _(sp):
            if tag == "l2_table":
                sp.wait_ge(scaled, 1)
            sp.dma_start(k.table.rearrange("(b p) f -> p b f", p=PB), tile[:]).then_inc(written, 16)
            sp.wait_ge(written, 16)


def late_edges(k, tag, rows_dram, block_of, gather_col, local_col, y_cols, silu, acc):
    nc = k.nc
    lo_y, n_y = y_cols
    with k.phase(tag), nc.Block() as block:
        rows = [k.sb(f"rows{s}", [128, 2, RW]) for s in range(RING)]
        idx = [k.sb(f"index{s}", [128, 2], I32) for s in range(RING)]
        msg = [k.sb(f"message{s}", [128, 2, FN]) for s in range(RING)]
        hot = [k.sb(f"hot{s}", [128, 2, 4, PB]) for s in range(2)]
        prod = [k.sb(f"prod{s}", [128, 2, PW]) for s in range(2)]
        one = k.sb("one", [128, 2, PB])
        feat = [k.sb(f"features{s}", [64, GE]) for s in range(2)]
        hid = [k.sb(f"hidden{s}", [64, GE]) for s in range(2)]
        tanh = [k.sb(f"tanh{s}", [64, GE]) for s in range(2)]
        p1 = [k.ps(f"turned{s}", [128, 2, GE]) for s in range(2)]
        pw = [k.ps(f"weights{s}", [128, 2, 256]) for s in range(2)]
        pa = [k.ps(f"sums{s}", [128, 2, 512]) for s in range(2)]
        row_in = [k.sem(f"row_in{s}") for s in range(RING)]
        gathered = [k.sem(f"gathered{s}") for s in range(RING)]
        (indexed, hots, turned, copied, hidden, silued, weighed, multiplied, summed, added, gate,
         compared, tanhed, sp_gate) = (
            k.sem(n) for n in ("indexed", "hots", "turned", "copied", "hidden", "silued", "weighed",
                               "multiplied", "summed", "added", "gate", "compared", "tanhed",
                               "sp_gate"))
        scaled_hot = k.sem("scaled_hot")
        view = rows_dram.rearrange("(g p u) w -> g p u w", p=128, u=2)

        @block.sync
        def _(sp):
            def body(j, c):
                g, s, r = group(j, c, 0)
                if past(g, RING):
                    sp.wait_ge(hots, g - RING + 1)
                    sp.wait_ge(turned, g - RING + 1)
                sp.sem_inc(sp_gate, 1)
                sp.dma_start(rows[s][:], view[ds(g, 1)].rearrange("a p u w -> p (a u) w"))\
                    .then_inc(row_in[s], 16)
            steps(sp, body, 0)

        @block.gpsimd
        def _(pool):
            def body(j, c):
                g, s, r = group(j, c, 0)
                pool.wait_ge(indexed, g + 1)
                if past(g, RING):
                    pool.wait_ge(multiplied, (g - RING) * 3 + 3)
                pool.sem_inc(gate, 1)
                for u in range(2):
                    pool.indirect_dma_start(
                        out=msg[s][:, u, :], out_offset=None, in_=k.table,
                        in_offset=bass.IndirectOffsetOnAxis(ap=idx[s][:, u:u + 1], axis=0))\
                        .then_inc(gathered[s], 16)
            steps(pool, body, 0)

        @block.scalar
        def _(act):
            def body(j, c):
                at = group(j, c, 0)
                if at:
                    g, s, r = at
                    act.wait_ge(turned, g + 1)
                    if past(g, 2):
                        act.wait_ge(hidden, g - 1)
                    act.activation(feat[s % 2][:], p1[s % 2][0:64, 0, :], ACT.Copy).then_inc(copied, 1)
                at = group(j, c, 1)
                if at:
                    g, s, r = at
                    act.wait_ge(hidden, g + 1)
                    if silu:
                        if past(g, 2):
                            act.wait_ge(silued, g - 1)
                        act.activation(tanh[s % 2][:], p1[s % 2][0:64, 1, :], ACT.Tanh, scale=1 / 16)\
                            .then_inc(tanhed, 1)
                    else:
                        if past(g, 2):
                            act.wait_ge(weighed, g - 1)
                        act.activation(hid[s % 2][:], p1[s % 2][0:64, 1, :], ACT.Relu)\
                            .then_inc(silued, 1)
            steps(act, body, 3)

        @block.tensor
        def _(pe):
            fc1, fc2 = (k.wt(f"{tag[0:2]}_fc{n}") for n in (1, 2))

            def body(j, c):
                at = group(j, c, 0)
                if at:
                    g, s, r = at
                    pe.wait_ge(row_in[s], r * 16 + 16)
                    if past(g, 2):
                        pe.wait_ge(silued, g - 1)
                    pe.sem_inc(gate, 1)
                    for u in range(2):
                        last = pe.transpose(p1[s % 2][0:64, 0, u * 128:u * 128 + 128],
                                            rows[s][:, u, R_A64:R_A64 + 64], k.const("ident"))
                    last.then_inc(turned, 1)
                at = group(j, c, 3)
                if at:
                    g, s, r = at
                    b = s % 2
                    pe.wait_ge(hots, g + 1)
                    pe.wait_ge(multiplied, g * 3 + 3)
                    if past(g, 2):
                        pe.wait_ge(added, g * 2 - 2)
                    pe.sem_inc(gate, 1)
                    out = pa[b]
                    for y, lo, n, bank, col in ((0, P_A, 160, 0, 0), (1, P_B, 160, 0, 160),
                                                (2, P_B, 160, 0, 320), (3, P_B, 160, 1, 0)):
                        for u in range(2):
                            pe.matmul(out[0:PB, bank, col:col + n], hot[b][:, u, y, :],
                                      prod[b][:, u, lo:lo + n], start=u == 0, stop=u == 1,
                                      skip_group_check=True)
                    for y in range(3):
                        for u in range(2):
                            last = pe.matmul(out[0:PB, 1, 160:192], hot[b][:, u, 1 + y, :],
                                             prod[b][:, u, P_D + CV * y:P_D + CV * y + CV],
                                             start=y == 0 and u == 0, stop=y == 2 and u == 1,
                                             skip_group_check=True)
                    last.then_inc(summed, 1)
                at = group(j, c, 0)
                if at:
                    g, s, r = at
                    pe.wait_ge(copied, g + 1)
                    pe.sem_inc(gate, 1)
                    pe.matmul(p1[s % 2][0:64, 1, :], fc1, feat[s % 2][:], start=True, stop=True)\
                        .then_inc(hidden, 1)
                at = group(j, c, 1)
                if at:
                    g, s, r = at
                    pe.wait_ge(silued, g + 1)
                    if past(g, 2):
                        pe.wait_ge(multiplied, g * 3 - 3)
                    pe.sem_inc(gate, 1)
                    for u in range(2):
                        last = pe.matmul(pw[s % 2][:, u, 0:WN], hid[s % 2][:, u * 128:u * 128 + 128], fc2,
                                         start=True, stop=True)
                    last.then_inc(weighed, 1)
            steps(pe, body, 4)

        @block.vector
        def _(dve):
            dve.memset(one[:], 1.0).then_inc(compared, 1)
            dve.memset(acc[:], 0.0).then_inc(compared, 1)
            dve.wait_ge(compared, 2)

            def body(j, c):
                at = group(j, c, 0)
                if at:
                    g, s, r = at
                    dve.wait_ge(row_in[s], r * 16 + 16)
                    if past(g, RING):
                        dve.wait_ge(gathered[s], r * 32)
                    dve.tensor_copy(idx[s][:], rows[s][:, :, gather_col]).then_inc(indexed, 1)
                at = group(j, c, 1)
                if at and silu:
                    g, s, r = at
                    dve.wait_ge(tanhed, g + 1)
                    if past(g, 2):
                        dve.wait_ge(weighed, g - 1)
                    dve.scalar_tensor_tensor(hid[s % 2][:], tanh[s % 2][:], 1.0, p1[s % 2][0:64, 1, :],
                                             ALU.add, ALU.mult).then_inc(silued, 1)
                at = group(j, c, 2)
                if at:
                    g, s, r = at
                    b = s % 2
                    if past(g, 2):
                        dve.wait_ge(summed, g - 1)
                    dve.tensor_tensor(hot[b][:, :, 0, :],
                                      k.const("nodes").unsqueeze(1).to_broadcast([128, 2, PB]),
                                      rows[s][:, :, local_col:local_col + 1].to_broadcast([128, 2, PB]),
                                      ALU.is_equal).then_inc(compared, 1)
                    dve.wait_ge(compared, g + 3)
                    last = dve.tensor_tensor(
                        hot[b][:, :, 1:4, :], hot[b][:, :, 0:1, :].to_broadcast([128, 2, 3, PB]),
                        rows[s][:, :, lo_y + n_y - 3:lo_y + n_y].unsqueeze(3).to_broadcast([128, 2, 3, PB]),
                        ALU.mult)
                    if n_y == 4:
                        last.then_inc(scaled_hot, 1)
                        dve.wait_ge(scaled_hot, g + 1)
                        last = dve.tensor_tensor(hot[b][:, :, 0, :], hot[b][:, :, 0, :],
                                                 rows[s][:, :, lo_y:lo_y + 1].to_broadcast([128, 2, PB]),
                                                 ALU.mult)
                    last.then_inc(hots, 1)
                    dve.wait_ge(gathered[s], r * 32 + 32)
                    dve.wait_ge(weighed, g + 1)
                    w = pw[b]
                    pr = prod[b]
                    dve.tensor_tensor(
                        ab_view(pr), w[:, :, 0:128].rearrange("p u (t n) -> p u t n", t=2),
                        msg[s][:, :, 0:CS].unsqueeze(2).to_broadcast([128, 2, 2, CS]),
                        ALU.mult).then_inc(multiplied, 1)
                    for u in range(2):
                        dve.tensor_tensor(
                            cdx_view(pr, u),
                            w[:, u, 128:WN].rearrange("p (t n) -> p t n", t=3).unsqueeze(2)
                            .to_broadcast([128, 3, 3, CV]),
                            msg[s][:, u, CS:FN].rearrange("p (i n) -> p i n", i=3).unsqueeze(1)
                            .to_broadcast([128, 3, 3, CV]),
                            ALU.mult).then_inc(multiplied, 1)
                at = group(j, c, 4)
                if at:
                    g, s, r = at
                    b = s % 2
                    blk = dve.value_load(block_of[0:1, ds(g, 1)], min_val=0, max_val=NB - 1)
                    dve.wait_ge(summed, g + 1)
                    dve.wait_ge(added, g * 2) if past(g, 1) else None
                    for bank, lo, n in ((0, 0, 480), (1, 480, 192)):
                        part = acc[:, ds(blk, 1), lo:lo + n]
                        dve.tensor_tensor(part, part, pa[b][0:PB, bank, 0:n].unsqueeze(1), ALU.add)\
                            .then_inc(added, 1)
            steps(dve, body, 4)


def ab_view(pr):
    return pr[:].rearrange("p u (t q) -> p u t q", q=P_B)[:, :, :, 0:CS]


def cdx_view(pr, u):
    return pr[:, u, 0:480].rearrange("p (t q) -> p t q", q=160)[:, :, CS:CS + FV]\
        .rearrange("p t (i n) -> p t i n", i=3)


def late_nodes(k, tag, acc):
    nc = k.nc
    layer = tag[0:2]
    with k.phase(tag):
        pre = k.sb("pre", [PB, NB, 2 * 96])

        def fill(dve, b, stage, staged):
            a = acc[:, ds(b, 1), :]

            def put(lo, n, ap, blocks=None):
                out = stage[:, lo:lo + n].unsqueeze(1)
                dve.tensor_scalar(out, ap, 1.0, None, ALU.mult).then_inc(staged, 1)

            put(0, 64, a[:, :, 0:64])
            put(64, CV, a[:, :, 640:672])
            vec = stage[:, 96:480].rearrange("p (o i n) -> p o i n", o=1, i=3)
            dve.tensor_scalar(vec[:, :, :, 0:64],
                              a[:, :, 160:640].rearrange("p o (i n) -> p o i n", i=3)[:, :, :, 0:64],
                              1.0, None, ALU.mult).then_inc(staged, 1)
            dve.tensor_scalar(vec[:, :, :, 64:96],
                              a[:, :, 64:160].rearrange("p o (i n) -> p o i n", i=3),
                              1.0, None, ALU.mult).then_inc(staged, 1)
            for i in range(3):
                j, m = (i + 1) % 3, (i + 2) % 3
                plus, minus = (160 + 160 * f + 64 + CV * e for f, e in ((m, j), (j, m)))
                dve.tensor_tensor(vec[:, :, i, 96:128], a[:, :, plus:plus + CV],
                                  a[:, :, minus:minus + CV], ALU.subtract).then_inc(staged, 1)
            dve.tensor_scalar(stage[:, 480:640].unsqueeze(1), k.h[:, ds(b, 1), :], 1.0, None,
                              ALU.mult).then_inc(staged, 1)

        w = lambda n: k.wt(f"{layer}_{n}")
        node_linear(k, f"{layer}_out", 640, fill, 8,
                    [(0, 96), (96, 224), (224, 352), (352, 480), (480, 544), (544, 640)],
                    [(0, 1, 96), (1, 3, 128), (4, 1, CS), (5, 1, FV)],
                    [(4, CS, w("skip_s"), 0, True, False), (0, 96, w("out_s"), 0, False, True),
                     (5, FV, w("skip_v"), 96, True, False)]
                    + [(1 + i, 128, w("out_v"), 96 + CV * i, False, True) for i in range(3)],
                    [(0, 192, pre)])
        with nc.Block() as block:
            done, tanhed = k.sem("done"), k.sem("tanhed")
            gate = k.sb("gate_values", [PB, NB, 96])

            @block.scalar
            def _(act):
                act.wait_ge(done, 1)
                act.activation(gate[:], pre[:, :, 0:96], ACT.Tanh, scale=0.5).then_inc(tanhed, 1)

            @block.vector
            def _(dve):
                ch = Chain(dve, done)
                if layer == "l2":
                    ch.then(dve.tensor_tensor(pre[:], pre[:], k.a0[:].unsqueeze(2)
                                              .to_broadcast([PB, NB, 192]), ALU.mult))
                else:
                    ch.then(dve.memset(gate[:, 0:1, 0:1], 0.0))
                dve.wait_ge(tanhed, 1)
                ch.then(dve.tensor_scalar(gate[:], gate[:], 0.5, 0.5, ALU.mult, ALU.add))
                ch.add(dve.tensor_tensor(pre[:, :, 0:64], pre[:, :, 0:64], gate[:, :, 0:64], ALU.mult))
                for i in range(3):
                    v = pre[:, :, 96 + CV * i:96 + CV * i + CV]
                    ch.add(dve.tensor_tensor(v, v, gate[:, :, 64:96], ALU.mult))
                dve.wait_ge(done, ch.n)
                ch.add(dve.tensor_tensor(k.x[:, :, 0:CS], k.x[:, :, 0:CS], pre[:, :, 0:64], ALU.add))
                ch.then(dve.tensor_tensor(k.x[:, :, CS:FN], k.x[:, :, CS:FN], pre[:, :, 96:192], ALU.add))


def radial_hidden(k, tag):
    nc = k.nc
    with k.phase(tag), nc.Block() as block:
        rows = [k.sb(f"rows{s}", [128, 2, RW]) for s in range(RING)]
        feat = [k.sb(f"features{s}", [65, GE]) for s in range(2)]
        cen = [[k.sb(f"centred{n}{s}", [128, 2, 64]) for s in range(2)] for n in range(2)]
        sq = [[k.sb(f"squares{n}{s}", [128, 2, 64]) for s in range(2)] for n in range(2)]
        var = [[k.sb(f"variance{n}{s}", [128, 2]) for s in range(2)] for n in range(2)]
        tan = [[k.sb(f"tanh{n}{s}", [64, GE]) for s in range(2)] for n in range(2)]
        z = [[k.sb(f"affine{n}{s}", [64, GE]) for s in range(2)] for n in range(2)]
        hid = [[k.sb(f"hidden{n}{s}", [65, GE]) for s in range(2)] for n in range(2)]
        pt = [k.ps(f"features_t{s}", [128, 512]) for s in range(2)]
        pm = [[k.ps(f"product{n}{s}", [128, 512]) for s in range(2)] for n in range(2)]
        gb = k.sb("half_gains", [64, 4])
        row_in = [k.sem(f"row_in{s}") for s in range(RING)]
        out_done = [k.sem(f"out_done{s}") for s in range(2)]
        turned, copied, ones, gate, sp_gate = (
            k.sem(n) for n in ("turned", "copied", "ones", "gate", "sp_gate"))
        mul, cent, squared, vard, powed, normed, flipped, affined, silued = (
            [k.sem(f"{m}{n}") for n in range(2)] for m in (
                "mul", "cent", "squared", "vard", "powed", "normed", "flipped", "affined", "silued"))
        view = k.by_dst.rearrange("(g p u) w -> g p u w", p=128, u=2)
        L = (1, 3)

        @block.sync
        def _(sp):
            def body(j, c):
                at = group(j, c, 0)
                if at:
                    g, s, r = at
                    if past(g, RING):
                        sp.wait_ge(turned, g - RING + 1)
                        sp.sem_inc(sp_gate, 1)
                    sp.dma_start(rows[s][:], view[ds(g, 1)].rearrange("a p u w -> p (a u) w"))\
                        .then_inc(row_in[s], 16)
                at = group(j, c, 5)
                if at:
                    g, s, r = at
                    sp.wait_ge(silued[1], g + 1)
                    sp.sem_inc(sp_gate, 1)
                    sp.dma_start(k.hidden[ds(g * 64, 64), :], hid[1][s % 2][0:64, :])\
                        .then_inc(out_done[s % 2], 16)
            steps(sp, body, 5)
            for s in range(2):
                sp.wait_ge(out_done[s], NG // 2 * 16)

        @block.gpsimd
        def _(pool):
            def body(j, c):
                for n in range(2):
                    at = group(j, c, L[n])
                    if at:
                        g, s, r = at
                        pool.wait_ge(vard[n], 2 * g + 2)
                        v = var[n][s % 2][:]
                        pool.tensor_tensor(v, v, k.half[:, 0:2], ALU.pow).then_inc(powed[n], 1)
            steps(pool, body, 5)

        @block.tensor
        def _(pe):
            pe.wait_ge(ones, 7)

            def body(j, c):
                at = group(j, c, 0)
                if at:
                    g, s, r = at
                    pe.wait_ge(row_in[s], r * 16 + 16)
                    if past(g, 2):
                        pe.wait_ge(copied, g - 1)
                    pe.sem_inc(gate, 1)
                    for u in range(2):
                        last = pe.transpose(pt[s % 2][0:64, u * 128:u * 128 + 128],
                                            rows[s][:, u, R_A64:R_A64 + 64], k.const("ident"))
                    last.then_inc(turned, 1)
                for n in range(2):
                    at = group(j, c, L[n] + 1)
                    if at:
                        g, s, r = at
                        b = s % 2
                        pe.wait_ge(normed[n], g + 1)
                        pe.sem_inc(gate, 1)
                        for u in range(2):
                            last = pe.transpose(pm[n][b][0:64, 128 + u * 128:256 + u * 128],
                                                cen[n][b][:, u, :], k.const("ident"))
                        last.then_inc(flipped[n], 1)
                    at = group(j, c, L[n] - 1 if n == 0 else L[n])
                    if at:
                        g, s, r = at
                        b = s % 2
                        if n == 0:
                            pe.wait_ge(copied, g + 1)
                        else:
                            pe.wait_ge(silued[0], g + 1)
                        if past(g, 2):
                            pe.wait_ge(affined[n], 2 * g - 2)
                        pe.sem_inc(gate, 1)
                        src = feat[b] if n == 0 else hid[0][b]
                        for u in range(2):
                            last = pe.matmul(pm[n][b][:, u * 64:u * 64 + 64],
                                             src[:, u * 128:u * 128 + 128], k.wt(f"l3_rw{n + 1}"),
                                             start=True, stop=True)
                        last.then_inc(mul[n], 1)
            steps(pe, body, 5)

        @block.scalar
        def _(act):
            act.wait_ge(ones, 7)

            def body(j, c):
                at = group(j, c, 0)
                if at:
                    g, s, r = at
                    act.wait_ge(turned, g + 1)
                    if past(g, 2):
                        act.wait_ge(mul[0], g - 1)
                    act.activation(feat[s % 2][0:64, :], pt[s % 2][0:64, 0:GE], ACT.Copy)\
                        .then_inc(copied, 1)
                for n in range(2):
                    at = group(j, c, L[n])
                    if at:
                        g, s, r = at
                        b = s % 2
                        act.wait_ge(mul[n], g + 1)
                        if past(g, 2):
                            act.wait_ge(flipped[n], g - 1)
                        act.activation(cen[n][b][:], pm[n][b][:, 0:128].rearrange("p (u f) -> p u f", u=2),
                                       ACT.Copy).then_inc(cent[n], 1)
                    at = group(j, c, L[n] + 1)
                    if at:
                        g, s, r = at
                        b = s % 2
                        act.wait_ge(flipped[n], g + 1)
                        if past(g, 2):
                            act.wait_ge(silued[n], g - 1)
                        src = pm[n][b][0:64, 128:384]
                        act.activation(tan[n][b][:], src, ACT.Tanh, scale=gb[:, 2 * n:2 * n + 1],
                                       bias=gb[:, 2 * n + 1:2 * n + 2]).then_inc(affined[n], 1)
                        act.activation(z[n][b][:], src, ACT.Identity, scale=k.wt(f"l3_rg{n + 1}"),
                                       bias=k.wt(f"l3_rb{n + 1}")).then_inc(affined[n], 1)
            steps(act, body, 5)

        @block.vector
        def _(dve):
            for n in range(2):
                dve.memset(feat[n][64:65, :], 1.0).then_inc(ones, 1)
                dve.memset(hid[0][n][64:65, :], 1.0).then_inc(ones, 1)
            dve.tensor_scalar(gb[:, 0:1], k.wt("l3_rg1"), 0.5, None, ALU.mult).then_inc(ones, 1)
            dve.tensor_scalar(gb[:, 1:2], k.wt("l3_rb1"), 0.5, None, ALU.mult).then_inc(ones, 1)
            dve.tensor_scalar(gb[:, 2:4], k.wt_pair("l3_rg2", "l3_rb2"), 0.5, None, ALU.mult)\
                .then_inc(ones, 1)

            def body(j, c):
                for n in range(2):
                    at = group(j, c, L[n] + 1)
                    if at:
                        g, s, r = at
                        b = s % 2
                        dve.wait_ge(powed[n], g + 1)
                        dve.tensor_tensor(cen[n][b][:], cen[n][b][:],
                                          var[n][b][:].unsqueeze(2).to_broadcast([128, 2, 64]),
                                          ALU.mult).then_inc(normed[n], 1)
                        dve.wait_ge(affined[n], 2 * g + 2)
                        if n == 1 and past(g, 2):
                            dve.wait_ge(out_done[b], (2 * r + (s // 2)) * 16)
                        if n == 0 and past(g, 2):
                            dve.wait_ge(mul[1], g - 1)
                        dve.scalar_tensor_tensor(hid[n][b][0:64, :], tan[n][b][:], 1.0, z[n][b][:],
                                                 ALU.add, ALU.mult).then_inc(silued[n], 1)
                    at = group(j, c, L[n])
                    if at:
                        g, s, r = at
                        b = s % 2
                        dve.wait_ge(cent[n], g + 1)
                        dve.tensor_tensor(sq[n][b][:], cen[n][b][:], cen[n][b][:], ALU.mult)\
                            .then_inc(squared[n], 1)
                        dve.wait_ge(squared[n], g + 1)
                        dve.tensor_reduce(var[n][b][:], sq[n][b][:], AX_X, ALU.add).then_inc(vard[n], 1)
                        dve.wait_ge(vard[n], 2 * g + 1)
                        dve.tensor_scalar(var[n][b][:], var[n][b][:], 1 / 64, EPS, ALU.mult, ALU.add)\
                            .then_inc(vard[n], 1)
            steps(dve, body, 5)


def deep_group(j, c, lag):
    return group(j, c, lag, DEEP)


def later(g, n):
    return min(g + n, NG) if isinstance(g, int) else g + n


def attention_edges(k, tag, heads, keys, head_w, dst_part, acc):
    nc = k.nc
    first = tag[0:2] == "l0"
    HW = head_w + 1
    VW = heads * HW
    ns = CS
    sh, vh = ns // heads, CV // heads
    KD = 16 if first else 64
    with k.phase(tag), nc.Block() as block:
        rows = [k.sb(f"rows{s}", [128, 2, RW]) for s in range(DEEP)]
        idx = [k.sb(f"index{s}", [128, 2], I32) for s in range(DEEP)]
        msg = [k.sb(f"message{s}", [128, 2, FN]) for s in range(DEEP)]
        hot = [k.sb(f"hot{s}", [128, 2, PB]) for s in range(DEEP)]
        hot_t = [k.sb(f"hot_t{s}", [PB, 2, 128]) for s in range(DEEP)]
        feat = [k.sb(f"features{s}", [KD if first else 65, GE]) for s in range(DEEP)]
        full = k.sb("message_sum", [128, 2, FN])
        prod = k.sb("prod", [128, 2, PW])
        t1 = k.sb("dot_terms", [128, 2, 3, CV])
        t2 = k.sb("cross_terms", [128, 2, 3, FV])
        ten = [k.sb(f"tensor_product{n}", [128, 2, MW]) for n in range(2 if first else 1)]
        ten_t = [k.sb(f"tensor_turned{n}", [128, 2, 4, 128]) for n in range(2 if first else 1)]
        logit = [k.sb(f"logits{s}", [128, 2, heads]) for s in range(DEEP)]
        al = k.sb("alpha", [128, 2, 64])
        al2 = k.sb("alpha_act", [128, 2, 64])
        gates = k.sb("gates", [128, 2, 96])
        vv = k.sb("gated", [128, 2, FV])
        vals = [k.sb(f"values{s}", [128, 2, 160]) for s in range(DEEP)] if not first else None
        log_t = k.sb("logits_turned", [heads, GE])
        off = k.sb("off_block", [PB, 2, 128])
        junk = k.sb("junk", [PB, heads, GE])
        mx = k.sb("group_max", [PB, heads])
        mrun = k.sb("running_max", [PB, NB, heads])
        mnew = k.sb("new_max", [PB, heads])
        corr = k.sb("correction", [PB, 2, heads])
        ex = k.sb("exp", [128, 2, heads, HW])
        arg = k.sb("exp_arg", [128, 2, heads])
        scaled = k.sb("scaled_sums", [PB, VW])
        select = k.sb("head_rows", [heads, heads, PB])
        p_front = k.ps("front", [128, 512])
        p_w = k.ps("weights", [128, 2, 256])
        p_dst = k.ps("dst_part", [128, 512])
        p_t = k.ps("turned", [128, 2, 512])
        p_d = k.ps("dense", [128, 512])
        p_a = k.ps("head_logits", [128, 512])
        p_v = k.ps("values", [128, 512])
        row_in = [k.sem(f"row_in{s}") for s in range(DEEP)]
        gathered = [k.sem(f"gathered{s}") for s in range(DEEP)]
        feat_in = [k.sem(f"feat_in{s}") for s in range(DEEP)]
        (set_up, indexed, hots, fronted, copied, weighed, dsted, tensored, turned1, evac1, densed,
         squashed, logited, turned2, evac2, valued, spread, maxed, renewed, fetched, argued, exped,
         weighted, summed, added, gate, rowed, log_turned, offed, dve_gate, pe_gate,
         sp_gate) = (
            k.sem(n) for n in (
                "set_up", "indexed", "hots", "fronted", "copied", "weighed", "dsted", "tensored",
                "turned1", "evac1", "densed", "squashed", "logited", "turned2", "evac2", "valued",
                "spread", "maxed", "renewed", "fetched", "argued", "exped", "weighted", "summed",
                "added", "gate", "rowed", "log_turned", "offed", "dve_gate", "pe_gate",
                "sp_gate"))
        view = k.by_dst.rearrange("(g p u) w -> g p u w", p=128, u=2)
        S1 = 14
        S2 = 15 if first else 4
        NF = 3 if first else 2
        DL = k.wt(f"{tag[0:2]}_as") if first else k.wt("l3_lin_s")
        DW = 256 if first else 224
        pair_bank = [p_w[:].rearrange("p u q -> p (u q)"), p_dst[:], p_t[:, 0, :], p_t[:, 1, :]]
        PAIRS = heads // 2

        @block.sync
        def _(sp):
            def body(j, c):
                g, s, r = deep_group(j, c, 0)
                if past(g, DEEP):
                    sp.wait_ge(*((logited, (g - DEEP + 1) * S2) if first else
                                 (tensored, (g - DEEP + 1) * S1)))
                sp.sem_inc(sp_gate, 1)
                sp.dma_start(rows[s][:], view[ds(g, 1)].rearrange("a p u w -> p (a u) w"))\
                    .then_inc(row_in[s], 16)
                if not first:
                    if past(g, DEEP):
                        sp.wait_ge(weighed, g - DEEP + 1)
                    sp.sem_inc(sp_gate, 1)
                    sp.dma_start(feat[s][0:64, :], k.hidden[ds(g * 64, 64), :])\
                        .then_inc(feat_in[s], 16)
            steps(sp, body, 0, DEEP)

        @block.gpsimd
        def _(pool):
            def body(j, c):
                g, s, r = deep_group(j, c, 0)
                pool.wait_ge(indexed, g + 1)
                if past(g, DEEP):
                    pool.wait_ge(tensored, (g - DEEP + 1) * S1)
                pool.sem_inc(gate, 1)
                for u in range(2):
                    pool.indirect_dma_start(
                        out=msg[s][:, u, :], out_offset=None, in_=k.table,
                        in_offset=bass.IndirectOffsetOnAxis(ap=idx[s][:, u:u + 1], axis=0))\
                        .then_inc(gathered[s], 16)
            steps(pool, body, 0, DEEP)

        @block.tensor
        def _(pe):
            pe.wait_ge(set_up, 5 if first else 4 + DEEP)

            def front(at):
                g, s, r = at
                pe.wait_ge(row_in[s], r * 16 + 16)
                pe.wait_ge(hots, g + 1)
                if past(g, 1):
                    pe.wait_ge(copied, NF * g)
                pe.sem_inc(pe_gate, 1)
                if first:
                    for u in range(2):
                        pe.transpose(p_front[0:16, u * 128:u * 128 + 128],
                                     rows[s][:, u, R_A16:R_A16 + 16], k.const("ident"))
                for u in range(2):
                    last = pe.transpose(p_front[0:PB, 256 + u * 128:384 + u * 128], hot[s][:, u, :],
                                        k.const("ident"))
                last.then_inc(fronted, 2)

            def edge_weights(at):
                g, s, r = at
                blk = pe.value_load(k.block_of_dst[0:1, ds(g, 1)], min_val=0, max_val=NB - 1)
                pe.wait_ge(copied, NF * g + NF)
                if not first:
                    pe.wait_ge(feat_in[s], r * 16 + 16)
                if past(g, 1):
                    pe.wait_ge(tensored, g * S1)
                if past(g, 3):
                    pe.wait_ge(maxed, g * heads - 3 * heads + 4)
                pe.sem_inc(pe_gate, 1)
                kd = 16 if first else 65
                wr = k.wt("l0_rbf") if first else k.wt("l3_rw3")
                for u in range(2):
                    last = pe.matmul(p_w[:, u, 0:WN], feat[s][0:kd, u * 128:u * 128 + 128], wr,
                                     start=True, stop=True)
                last.then_inc(weighed, 1)
                for u in range(2):
                    last = pe.matmul(p_dst[:, u * FN:u * FN + FN], hot_t[s][:, u, :],
                                     dst_part[:, ds(blk, 1), :], start=True, stop=True)
                last.then_inc(dsted, 1)

            def turn(src, counter):
                for u in range(2):
                    for t in range(4):
                        last = pe.transpose(p_t[:, u, t * 128:t * 128 + 128],
                                            src[:, u, t * 128:t * 128 + 128], k.const("ident"))
                last.then_inc(counter, 1)

            def turn_first(at):
                g, s, r = at
                pe.wait_ge(tensored, g * S1 + S1)
                if first:
                    if past(g, 2):
                        pe.wait_ge(evac2, g - 1)
                elif past(g, 3):
                    pe.wait_ge(maxed, (g - 2) * heads)
                pe.sem_inc(pe_gate, 1)
                turn(ten[0], turned1)

            def dense(at):
                g, s, r = at
                pe.wait_ge(evac1, g + 1)
                if past(g, 1):
                    pe.wait_ge(logited, g * S2 - S2 + (4 if first else 2))
                    pe.wait_ge(squashed, g * 2)
                pe.sem_inc(pe_gate, 1)
                kk, n = (96, 160) if first else (97, 128)
                wv = k.wt("l0_val_v" if first else "l3_lin_v")
                for u in range(2):
                    pe.matmul(p_d[:, u * DW:u * DW + n], ten_t[0][0:kk, u, 0, :], DL, start=True,
                              stop=True, skip_group_check=True)
                    for i in range(3):
                        lo = u * DW + n + CV * i
                        last = pe.matmul(p_d[:, lo:lo + CV], ten_t[0][:, u, 1 + i, :], wv, start=True,
                                         stop=True, skip_group_check=True)
                last.then_inc(densed, 1)

            def turn_second(at):
                g, s, r = at
                pe.wait_ge(logited, g * S2 + S2)
                if first:
                    pe.wait_ge(evac1, later(g, 2))
                    pe.sem_inc(pe_gate, 1)
                    turn(ten[1], turned2)
                if past(g, 1):
                    pe.wait_ge(argued, g * 2)
                pe.sem_inc(pe_gate, 1)
                for u in range(2):
                    last = pe.transpose(p_a[0:heads, u * 128:u * 128 + 128], logit[s][:, u, :],
                                        k.const("ident"))
                last.then_inc(log_turned, 1)

            def values(at):
                g, s, r = at
                if first:
                    pe.wait_ge(evac2, g + 1)
                    if past(g, 1):
                        pe.wait_ge(weighted, g)
                    pe.sem_inc(pe_gate, 1)
                    for u in range(2):
                        out = p_v[:, u * 160:u * 160 + 160].rearrange("p (h q) -> p h q", h=heads)
                        pe.matmul(out[:, :, 0:sh], ten_t[1][0:96, u, 0, :], k.wt("l0_vlin_s"),
                                  start=True, stop=True, skip_group_check=True)
                        for i in range(3):
                            lo = sh + vh * i
                            last = pe.matmul(out[:, :, lo:lo + vh], ten_t[1][:, u, 1 + i, :],
                                             k.wt("l0_vlin_v"), start=True, stop=True,
                                             skip_group_check=True)
                    last.then_inc(valued, 1)

            def maxima(at):
                g, s, r = at
                pe.wait_ge(rowed, g + 1)
                pe.wait_ge(tensored, later(g, 3) * S1)
                pe.sem_inc(pe_gate, 1)
                for n in range(PAIRS):
                    if n == 2:
                        pe.wait_ge(evac1, later(g, 3))
                        pe.sem_inc(pe_gate, 1)
                    for h in range(2):
                        last = pe.matmul(pair_bank[n][0:PB, h * GE:h * GE + GE],
                                         select[:, 2 * n + h, :], log_t[:], start=True, stop=True,
                                         skip_group_check=True)
                    last.then_inc(spread, 1)

            def fetch(at):
                g, s, r = at
                pe.wait_ge(renewed, g * 3 + 3)
                pe.sem_inc(pe_gate, 1)
                for u in range(2):
                    last = pe.matmul(p_a[:, heads * u:heads * u + heads], hot_t[s][:, u, :],
                                     mnew[:], start=True, stop=True, skip_group_check=True)
                last.then_inc(fetched, 1)

            def total(at):
                g, s, r = at
                pe.wait_ge(weighted, g + 1)
                if past(g, 1):
                    pe.wait_ge(added, g * 2)
                pe.sem_inc(pe_gate, 1)
                for u in range(2):
                    last = pe.matmul(p_v[0:PB, 320:320 + VW], hot[s][:, u, :],
                                     ex[:, u, :, :].rearrange("p h q -> p (h q)"),
                                     start=u == 0, stop=u == 1, skip_group_check=True)
                last.then_inc(summed, 1)

            def body(j, c):
                for stage, lag in ((total, 5), (front, 1), (values, 4), (turn_first, 2), (maxima, 4),
                                   (dense, 2), (fetch, 4), (edge_weights, 1), (turn_second, 3)):
                    at = deep_group(j, c, lag)
                    if at:
                        stage(at)
            steps(pe, body, 5, DEEP)

        @block.scalar
        def _(act):
            act.wait_ge(set_up, 5 if first else 4 + DEEP)

            def front(at):
                g, s, r = at
                act.wait_ge(fronted, 2 * g + 2)
                if first:
                    if past(g, DEEP):
                        act.wait_ge(weighed, g - DEEP + 1)
                    act.activation(feat[s][:], p_front[0:16, 0:GE], ACT.Copy).then_inc(copied, 1)
                if past(g, DEEP):
                    act.wait_ge(fetched, g - DEEP + 1)
                oh = p_front[0:PB, 256:512].rearrange("p (u e) -> p u e", u=2)
                act.activation(hot_t[s][:], oh, ACT.Copy).then_inc(copied, 2)

            def evac(src_done, dst, counter, at):
                g, s, r = at
                act.wait_ge(src_done, g + 1)
                if past(g, 1):
                    act.wait_ge(densed if counter is evac1 else valued, g)
                act.activation(dst[:].rearrange("p u t e -> p u (t e)"), p_t[:], ACT.Copy)\
                    .then_inc(counter, 1)

            def squash(at):
                g, s, r = at
                act.wait_ge(densed, g + 1)
                if past(g, 1):
                    act.wait_ge(logited, g * S2)
                d = p_d[:, 0:2 * DW].rearrange("p (u q) -> p u q", u=2)
                if first:
                    act.activation(al[:], d[:, :, 0:64], ACT.Copy, scale=0.2).then_inc(squashed, 1)
                    act.activation(gates[:], d[:, :, 64:160], ACT.Tanh, scale=0.5).then_inc(squashed, 1)
                else:
                    act.activation(al[:], d[:, :, 0:64], ACT.Tanh, scale=0.5).then_inc(squashed, 1)
                    if past(g, DEEP):
                        act.wait_ge(weighted, g - DEEP + 1)
                    act.activation(vals[s][:], d[:, :, 64:224], ACT.Copy).then_inc(squashed, 1)

            def rows_of_logits(at):
                g, s, r = at
                act.wait_ge(log_turned, g + 1)
                act.activation(log_t[:], p_a[0:heads, 0:GE], ACT.Copy).then_inc(rowed, 1)

            def exps(at):
                g, s, r = at
                act.wait_ge(argued, g * 2 + 2)
                if past(g, 1):
                    act.wait_ge(summed, g)
                act.activation(ex[:, :, :, head_w], arg[:], ACT.Exp).then_inc(exped, 1)
                act.wait_ge(renewed, g * 3 + 3)
                if past(g, 1):
                    act.wait_ge(added, g * 2)
                act.activation(corr[:, 1, :], corr[:, 0, :], ACT.Exp).then_inc(exped, 1)

            def body(j, c):
                at = deep_group(j, c, 1)
                if at:
                    front(at)
                at = deep_group(j, c, 2)
                if at:
                    evac(turned1, ten_t[0], evac1, at)
                    squash(at)
                at = deep_group(j, c, 4)
                if at:
                    exps(at)
                at = deep_group(j, c, 3)
                if at:
                    if first:
                        evac(turned2, ten_t[1], evac2, at)
                    rows_of_logits(at)
            steps(act, body, 4, DEEP)

        @block.vector
        def _(dve):
            dve.memset(acc[:], 0.0).then_inc(set_up, 1)
            dve.memset(mrun[:], -BIG).then_inc(set_up, 1)
            for n in range(len(ten)):
                dve.memset(ten[n][:, :, 96:128], 0.0 if first else 1.0).then_inc(set_up, 1)
            if not first:
                for s in range(DEEP):
                    dve.memset(feat[s][64:65, :], 1.0).then_inc(set_up, 1)
            dve.tensor_copy(select[:], k.const("ident", heads)[:, 0:heads].unsqueeze(2)
                            .to_broadcast([heads, heads, PB])).then_inc(set_up, 1)
            dve.wait_ge(set_up, 5 if first else 4 + DEEP)

            def begin(at):
                g, s, r = at
                dve.wait_ge(row_in[s], r * 16 + 16)
                if past(g, DEEP):
                    dve.wait_ge(gathered[s], r * 32)
                dve.tensor_copy(idx[s][:], rows[s][:, :, R_SRC]).then_inc(indexed, 1)
                if past(g, DEEP):
                    dve.wait_ge(summed, g - DEEP + 1)
                dve.tensor_tensor(hot[s][:], k.const("nodes").unsqueeze(1).to_broadcast([128, 2, PB]),
                                  rows[s][:, :, R_LDST:R_LDST + 1].to_broadcast([128, 2, PB]),
                                  ALU.is_equal).then_inc(hots, 1)

            def product(a, b, cvec, dvec, xvec, y0, y, m, sem, base):
                at = [base]

                def add(ins):
                    ins.then_inc(sem, 1)
                    at[0] = at[0] + 1

                vec = m[:, :, 128:512].rearrange("p u (i q) -> p u i q", i=3)
                y4 = y.unsqueeze(3)
                if y0 is not None:
                    add(dve.tensor_tensor(m[:, :, 0:64], a, y0.to_broadcast([128, 2, 64]), ALU.mult))
                    add(dve.tensor_tensor(vec[:, :, :, 64:96], cvec,
                                          y0.unsqueeze(3).to_broadcast([128, 2, 3, CV]), ALU.mult))
                add(dve.tensor_tensor(t1[:], dvec, y4.to_broadcast([128, 2, 3, CV]), ALU.mult))
                dot_at = at[0]
                add(dve.tensor_tensor(t2[:], xvec.unsqueeze(2).to_broadcast([128, 2, 3, FV]),
                                      y4.to_broadcast([128, 2, 3, FV]), ALU.mult))
                cross_at = at[0]
                add(dve.tensor_tensor(vec[:, :, :, 0:64], b.unsqueeze(2).to_broadcast([128, 2, 3, 64]),
                                      y4.to_broadcast([128, 2, 3, 64]), ALU.mult))
                dve.wait_ge(sem, dot_at)
                add(dve.tensor_tensor(t1[:, :, 0, :], t1[:, :, 0, :], t1[:, :, 1, :], ALU.add))
                sum_at = at[0]
                dve.wait_ge(sem, cross_at)
                for i in range(3):
                    q, z = (i + 1) % 3, (i + 2) % 3
                    add(dve.tensor_tensor(vec[:, :, i, 96:128], t2[:, :, z, CV * q:CV * q + CV],
                                          t2[:, :, q, CV * z:CV * z + CV], ALU.subtract))
                    if i == 0:
                        dve.wait_ge(sem, sum_at)
                        add(dve.tensor_tensor(m[:, :, 64:96], t1[:, :, 0, :], t1[:, :, 2, :], ALU.add))

            def factors(s):
                rw = rows[s]
                if first:
                    return rw[:, :, R_Y:R_Y + 1], rw[:, :, R_Y + 1:R_Y + 4]
                return None, rw[:, :, R_U3:R_U3 + 3]

            def tensor(at):
                g, s, r = at
                base = g * S1
                dve.wait_ge(gathered[s], r * 32 + 32)
                dve.wait_ge(dsted, g + 1)
                dve.tensor_tensor(full[:], msg[s][:],
                                  p_dst[:, 0:2 * FN].rearrange("p (u f) -> p u f", u=2), ALU.add)\
                    .then_inc(tensored, 1)
                dve.wait_ge(weighed, g + 1)
                dve.wait_ge(tensored, base + 1)
                if past(g, 1):
                    dve.wait_ge(turned1, g)
                pr, m = prod, ten[0]
                wa = p_w[:, :, 0:128].rearrange("p u (t n) -> p u t n", t=2)
                wv = p_w[:, :, 128:WN].rearrange("p u (t n) -> p u t n", t=3)
                sc = full[:, :, 0:CS]
                fv = full[:, :, CS:FN].rearrange("p u (i n) -> p u i n", i=3)
                if first:
                    dve.tensor_tensor(ab_view(pr), wa, sc.unsqueeze(2).to_broadcast([128, 2, 2, CS]),
                                      ALU.mult).then_inc(tensored, 1)
                    for u in range(2):
                        dve.tensor_tensor(
                            cdx_view(pr, u), wv[:, u].unsqueeze(2).to_broadcast([128, 3, 3, CV]),
                            fv[:, u].unsqueeze(1).to_broadcast([128, 3, 3, CV]), ALU.mult)\
                            .then_inc(tensored, 1)
                    n = 4
                else:
                    dve.tensor_tensor(m[:, :, 0:64], wa[:, :, 0, :], sc, ALU.mult).then_inc(tensored, 1)
                    dve.tensor_tensor(pr[:, :, P_B:P_B + 64], wa[:, :, 1, :], sc, ALU.mult)\
                        .then_inc(tensored, 1)
                    vec = m[:, :, 128:512].rearrange("p u (i q) -> p u i q", i=3)
                    for t, out in ((0, vec[:, :, :, 64:96]),
                                   (1, pr[:, :, P_D:P_D + FV].rearrange("p u (i n) -> p u i n", i=3))):
                        dve.tensor_tensor(out, wv[:, :, t:t + 1, :].to_broadcast([128, 2, 3, CV]), fv,
                                          ALU.mult).then_inc(tensored, 1)
                    dve.tensor_tensor(pr[:, :, P_X:P_X + FV].rearrange("p u (i n) -> p u i n", i=3),
                                      wv[:, :, 2:3, :].to_broadcast([128, 2, 3, CV]), fv,
                                      ALU.mult).then_inc(tensored, 1)
                    n = 6
                dve.wait_ge(tensored, base + n)
                y0, y = factors(s)
                vec3 = lambda lo: pr[:, :, lo:lo + FV].rearrange("p u (i n) -> p u i n", i=3)
                product(pr[:, :, P_A:P_A + 64], pr[:, :, P_B:P_B + 64], vec3(P_C), vec3(P_D),
                        pr[:, :, P_X:P_X + FV], y0, y, m, tensored, base + n)

            def logits(at):
                g, s, r = at
                base = g * S2
                d = p_d[:, 0:2 * DW].rearrange("p (u q) -> p u q", u=2)
                dve.wait_ge(squashed, g * 2 + 2)
                if past(g, DEEP):
                    dve.wait_ge(log_turned, g - DEEP + 1)
                ad = k.row(f"{tag[0:2]}_adot").unsqueeze(1).to_broadcast([128, 2, 64])
                if first:
                    dve.tensor_tensor(al2[:], d[:, :, 0:64], al[:], ALU.max).then_inc(logited, 1)
                    dve.tensor_scalar(gates[:], gates[:], 0.5, 0.5, ALU.mult, ALU.add).then_inc(logited, 1)
                    dve.wait_ge(logited, base + 1)
                    dve.tensor_tensor(al2[:], al2[:], ad, ALU.mult).then_inc(logited, 1)
                    dve.wait_ge(logited, base + 2)
                    dve.tensor_tensor(
                        vv[:].rearrange("p u (i n) -> p u i n", i=3),
                        d[:, :, 160:256].rearrange("p u (i n) -> p u i n", i=3),
                        gates[:, :, 64:96].unsqueeze(2).to_broadcast([128, 2, 3, CV]), ALU.mult)\
                        .then_inc(logited, 1)
                    dve.wait_ge(logited, base + 3)
                    dve.tensor_reduce(logit[s][:], al2[:].rearrange("p u (h q) -> p u h q", h=heads),
                                      AX_X, ALU.add).then_inc(logited, 1)
                    dve.wait_ge(logited, base + 4)
                    if past(g, 1):
                        dve.wait_ge(turned2, g)
                    y0, y = factors(s)
                    v4 = vv[:].rearrange("p u (i n) -> p u i n", i=3)
                    product(gates[:, :, 0:64], gates[:, :, 0:64], v4, v4, vv[:], y0, y, ten[1],
                            logited, base + 5)
                else:
                    dve.tensor_scalar(al2[:], al[:], 0.4, 0.6, ALU.mult, ALU.add).then_inc(logited, 1)
                    dve.wait_ge(logited, base + 1)
                    dve.tensor_tensor(al2[:], d[:, :, 0:64], al2[:], ALU.mult).then_inc(logited, 1)
                    dve.wait_ge(logited, base + 2)
                    dve.tensor_tensor(al2[:], al2[:], ad, ALU.mult).then_inc(logited, 1)
                    dve.wait_ge(logited, base + 3)
                    dve.tensor_reduce(logit[s][:], al2[:].rearrange("p u (h q) -> p u h q", h=heads),
                                      AX_X, ALU.add).then_inc(logited, 1)

            def maxima(at):
                g, s, r = at
                blk = dve.value_load(k.block_of_dst[0:1, ds(g, 1)], min_val=0, max_val=NB - 1)
                if past(g, 1):
                    dve.wait_ge(maxed, g * heads)
                dve.tensor_scalar(off[:], hot_t[s][:], BIG, -BIG, ALU.mult, ALU.add).then_inc(offed, 1)
                dve.wait_ge(offed, g + 1)
                o = off[:].rearrange("p u e -> p (u e)")
                for n in range(heads):
                    if n % 2 == 0:
                        dve.wait_ge(spread, g * PAIRS + n // 2 + 1)
                        dve.sem_inc(dve_gate, 1)
                    h = n % 2 * GE
                    dve.tensor_tensor_reduce(junk[:, n, :], pair_bank[n // 2][0:PB, h:h + GE], o, 1.0,
                                             -BIG, ALU.add, ALU.max, mx[:, n:n + 1]).then_inc(maxed, 1)
                dve.wait_ge(maxed, g * heads + heads)
                if past(g, 1):
                    dve.wait_ge(fetched, g)
                    dve.wait_ge(exped, g * 2)
                    dve.wait_ge(renewed, g * 3)
                old = mrun[:, ds(blk, 1), :]
                dve.tensor_tensor(mnew[:].unsqueeze(1), old, mx[:].unsqueeze(1), ALU.max)\
                    .then_inc(renewed, 1)
                dve.wait_ge(renewed, g * 3 + 1)
                dve.tensor_tensor(corr[:, 0:1, :], old, mnew[:].unsqueeze(1), ALU.subtract)\
                    .then_inc(renewed, 1)
                dve.wait_ge(renewed, g * 3 + 2)
                dve.tensor_scalar(old, mnew[:].unsqueeze(1), 1.0, None, ALU.mult).then_inc(renewed, 1)

            def argue(at):
                g, s, r = at
                dve.wait_ge(fetched, g + 1)
                dve.tensor_tensor(arg[:], logit[s][:],
                                  p_a[:, 0:2 * heads].rearrange("p (u h) -> p u h", u=2),
                                  ALU.subtract).then_inc(argued, 1)
                dve.wait_ge(argued, g * 2 + 1)
                dve.tensor_scalar(arg[:], arg[:], 0.0, None, ALU.min).then_inc(argued, 1)

            def weight(at):
                g, s, r = at
                dve.wait_ge(exped, g * 2 + 1)
                if past(g, 1):
                    dve.wait_ge(summed, g)
                if first:
                    dve.wait_ge(valued, g + 1)
                for u in range(2):
                    e = ex[:, u, :, head_w:HW]
                    if first:
                        last = dve.tensor_tensor(
                            ex[:, u, :, 0:head_w],
                            p_v[:, u * 160:u * 160 + 160].rearrange("p (h q) -> p h q", h=heads),
                            e.to_broadcast([128, heads, head_w]), ALU.mult)
                    else:
                        v = vals[s]
                        dve.tensor_tensor(ex[:, u, :, 0:sh],
                                          v[:, u, 0:ns].rearrange("p (h q) -> p h q", h=heads),
                                          e.to_broadcast([128, heads, sh]), ALU.mult)
                        last = dve.tensor_tensor(
                            ex[:, u, :, sh:head_w].rearrange("p h (i q) -> p i h q", i=3),
                            v[:, u, ns:160].rearrange("p (i h q) -> p i h q", i=3, h=heads),
                            ex[:, u, :, head_w:HW].unsqueeze(1).to_broadcast([128, 3, heads, vh]),
                            ALU.mult)
                last.then_inc(weighted, 1)

            def add(at):
                g, s, r = at
                blk = dve.value_load(k.block_of_dst[0:1, ds(g, 1)], min_val=0, max_val=NB - 1)
                dve.wait_ge(exped, g * 2 + 2)
                if past(g, 1):
                    dve.wait_ge(added, g * 2)
                a = acc[:, ds(blk, 1), :]
                dve.tensor_tensor(scaled[:].rearrange("p (o h q) -> p o h q", o=1, h=heads),
                                  a.rearrange("p o (h q) -> p o h q", h=heads),
                                  corr[:, 1:2, :].unsqueeze(3).to_broadcast([PB, 1, heads, HW]), ALU.mult)\
                    .then_inc(added, 1)
                dve.wait_ge(added, g * 2 + 1)
                dve.wait_ge(summed, g + 1)
                dve.tensor_tensor(a, scaled[:].unsqueeze(1), p_v[0:PB, 320:320 + VW].unsqueeze(1), ALU.add)\
                    .then_inc(added, 1)

            def body(j, c):
                for stage, lag in ((tensor, 2), (logits, 3), (maxima, 4), (begin, 0), (argue, 4),
                                   (add, 5), (weight, 4)):
                    at = deep_group(j, c, lag)
                    if at:
                        stage(at)
            steps(dve, body, 5, DEEP)


def attended(k, tag, heads, head_w, acc, out):
    nc = k.nc
    ns = heads * head_w - FV
    sh, vh = ns // heads, CV // heads
    with k.phase(tag), nc.Block() as block:
        done = k.sem("done")
        inv = k.sb("inverse", [PB, NB, heads])

        @block.vector
        def _(dve):
            ch = Chain(dve, done)
            a = acc[:].rearrange("p b (h q) -> p b h q", h=heads)
            eps = 1e-16 if tag[0:2] == "l0" else 1e-12
            ch.then(dve.tensor_scalar(inv[:], a[:, :, :, head_w], eps, None, ALU.add))
            ch.then(dve.reciprocal(inv[:], inv[:]))
            parts = [(0, sh, 0)] + [(ns + CV * i, vh, sh + vh * i) for i in range(3)]
            for lo, n, at in parts:
                ch.add(dve.tensor_tensor(
                    out[:, :, lo:lo + heads * n].rearrange("p b (h q) -> p b h q", h=heads),
                    a[:, :, :, at:at + n], inv[:].unsqueeze(3).to_broadcast([PB, NB, heads, n]),
                    ALU.mult))
            dve.wait_ge(done, ch.n)


def add_nodes(k, tag, terms):
    with k.phase(tag), k.nc.Block() as block:
        done = k.sem("done")

        @block.vector
        def _(dve):
            ch = Chain(dve, done)
            for target, a, b in terms:
                ch.then(dve.tensor_tensor(target, a, b, ALU.add))


def layer0(k):
    with k.phase("l0"):
        acc = k.sb("acc", [PB, NB, 4 * 41])
        with k.phase("l0_in"):
            dst = k.sb("dst_part", [PB, NB, FN])
            with k.phase("l0_pre"):
                n = k.sb("normed", [PB, NB, FN])
                t = k.sb("src_part", [PB, NB, FN])
                norm_nodes(k, "l0_norm", True, k.h, n, ("l0_gs", "l0_bs", "l0_gv"), CV)
                node_linear(k, "l0_lin", FN, copy_fill(n, FN), 1, SV_SLICES, SV_EVACS,
                            [(0, CS, k.wt("l0_src_s"), 0, True, True),
                             (1, FV, k.wt("l0_src_v"), CS, True, True),
                             (0, CS, k.wt("l0_dst_s"), FN, True, True),
                             (1, FV, k.wt("l0_dst_v"), FN + CS, True, True)],
                            [(0, FN, t), (FN, FN, dst)])
                write_table(k, "l0_table", t)
            attention_edges(k, "l0_edges", 4, 16, 40, dst, acc)
        m = k.sb("attended", [PB, NB, FN])
        u = k.sb("update", [PB, NB, FN])
        attended(k, "l0_attended", 4, 40, acc, m)
        node_linear(k, "l0_out", FN, copy_fill(m, FN), 1, SV_SLICES, SV_EVACS,
                    [(0, CS, k.wt("l0_ps"), 0, True, True), (1, FV, k.wt("l0_pv"), CS, True, True)],
                    [(0, FN, u)])
        add_nodes(k, "l0_add", [(k.x[:], k.x[:], k.h[:]), (k.x[:], k.x[:], u[:])])


def late_layer(k, layer, rows_dram, block_of, gather_col, local_col, y_cols):
    with k.phase(layer):
        acc = k.sb("acc", [PB, NB, 672])
        with k.phase(f"{layer}_pre"):
            t = k.sb("src_part", [PB, NB, FN])
            norm_nodes(k, f"{layer}_norm", True)
            node_linear(k, f"{layer}_lin", FN, copy_fill(k.h, FN), 1, SV_SLICES, SV_EVACS,
                        [(0, CS, k.wt(f"{layer}_in_s"), 0, True, True),
                         (1, FV, k.wt(f"{layer}_in_v"), CS, True, True)], [(0, FN, t)])
            write_table(k, f"{layer}_table", t)
        late_edges(k, f"{layer}_edges", rows_dram, block_of, gather_col, local_col, y_cols,
                   layer == "l2", acc)
        late_nodes(k, f"{layer}_nodes", acc)


def layer3(k):
    nc = k.nc
    radial_hidden(k, "l3_radial")
    with k.phase("l3"):
        acc = k.sb("acc", [PB, NB, 8 * 21])
        with k.phase("l3_in"):
            dst = k.sb("dst_part", [PB, NB, FN])
            with k.phase("l3_pre"):
                n = k.sb("normed", [PB, NB, FN])
                t = k.sb("src_part", [PB, NB, FN])
                norm_nodes(k, "l3_norm", True, k.h, n, ("l3_gs1", "l3_bs1", "l3_gv1"), FV)
                node_linear(k, "l3_lin", FN, copy_fill(n, FN), 1, SV_SLICES, SV_EVACS,
                            [(0, CS, k.wt("l3_src_s"), 0, True, True),
                             (1, FV, k.wt("l3_src_v"), CS, True, True),
                             (0, CS, k.wt("l3_dst_s"), FN, True, True),
                             (1, FV, k.wt("l3_dst_v"), FN + CS, True, True)],
                            [(0, FN, t), (FN, FN, dst)])
                add_nodes(k, "l3_bias", [(dst[:, :, 0:CS], dst[:, :, 0:CS], k.blockrow("l3_dst_b"))])
                write_table(k, "l3_table", t)
            attention_edges(k, "l3_edges", 8, 8, 20, dst, acc)
        m = k.sb("attended", [PB, NB, FN])
        u = k.sb("update", [PB, NB, FN])
        f = k.sb("feed", [PB, NB, 384])
        attended(k, "l3_attended", 8, 20, acc, m)
        node_linear(k, "l3_proj", FN, copy_fill(m, FN), 1, SV_SLICES, SV_EVACS,
                    [(0, CS, k.wt("l3_proj_s"), 0, True, True), (1, FV, k.wt("l3_proj_v"), CS, True, True)],
                    [(0, FN, u)])
        add_nodes(k, "l3_mid", [(k.h[:], k.h[:], u[:]),
                                (k.h[:, :, 0:CS], k.h[:, :, 0:CS], k.blockrow("l3_proj_b"))])
        norm_nodes(k, "l3_norm2", False, k.h, m, ("l3_gs2", "l3_bs2", "l3_gv2"), FV)
        node_linear(k, "l3_f1", FN, copy_fill(m, FN), 1, SV_SLICES, SV_EVACS,
                    [(0, CS, k.wt("l3_f1_s"), 0, True, True), (1, FV, k.wt("l3_f1_v"), 192, True, True)],
                    [(0, 384, f)])
        with nc.Block() as block:
            done, tanhed = k.sem("done"), k.sem("tanhed")
            sg = k.sb("squashed", [PB, NB, 192])
            a0 = k.a0[:].unsqueeze(2)

            @block.scalar
            def _(act):
                act.wait_ge(done, 2)
                act.activation(sg[:], f[:, :, 0:192], ACT.Tanh, scale=0.5).then_inc(tanhed, 1)

            @block.vector
            def _(dve):
                ch = Chain(dve, done)
                ch.then(dve.tensor_tensor(f[:, :, 0:192], f[:, :, 0:192], k.blockrow("l3_f1_b"), ALU.add))
                ch.then(dve.tensor_tensor(f[:], f[:], a0.to_broadcast([PB, NB, 384]), ALU.mult))
                dve.wait_ge(tanhed, 1)
                ch.then(dve.tensor_scalar(sg[:], sg[:], 0.5, 0.5, ALU.mult, ALU.add))
                ch.add(dve.tensor_tensor(f[:, :, 0:128], f[:, :, 0:128], sg[:, :, 0:128], ALU.mult))
                for i in range(3):
                    v = f[:, :, 192 + 64 * i:256 + 64 * i]
                    ch.add(dve.tensor_tensor(v, v, sg[:, :, 128:192], ALU.mult))
                dve.wait_ge(done, ch.n)

        node_linear(k, "l3_f2", 384, copy_fill(f, 384), 1,
                    [(0, 128)] + [(192 + 64 * i, 256 + 64 * i) for i in range(3)],
                    [(0, 1, 128), (1, 3, 64)],
                    [(0, 128, k.wt("l3_f2_s"), 0, True, True)]
                    + [(1 + i, 64, k.wt("l3_f2_v"), CS + CV * i, True, True) for i in range(3)],
                    [(0, FN, u)])
        with nc.Block() as block:
            merged = k.sem("merged")

            @block.vector
            def _(dve):
                ch = Chain(dve, merged)
                ch.then(dve.tensor_tensor(u[:, :, 0:CS], u[:, :, 0:CS], k.blockrow("l3_f2_b"), ALU.add))
                ch.then(dve.tensor_tensor(u[:], u[:], k.a0[:].unsqueeze(2).to_broadcast([PB, NB, FN]),
                                          ALU.mult))
                ch.then(dve.tensor_tensor(k.x[:], k.x[:], k.h[:], ALU.add))
                ch.then(dve.tensor_tensor(k.x[:], k.x[:], u[:], ALU.add))


def gnn_kernel(nc, args, layers=4):
    with ExitStack() as stack:
        k = Kernel(nc, stack, args)
        prepare(k)
        sort_edges(k)
        if layers > 0:
            layer0(k)
        if layers > 1:
            late_layer(k, "l1", k.by_src, k.block_of_src, R_DST, R_LSRC, (R_U1, 3))
        if layers > 2:
            late_layer(k, "l2", k.by_dst, k.block_of_dst, R_SRC, R_LDST, (R_Y, 4))
        if layers > 3:
            layer3(k)
        with nc.Block() as block:
            stored = k.sem("stored")

            @block.sync
            def _(sp):
                sp.dma_start(args["out"], k.x[:]).then_inc(stored, 16)
                sp.wait_ge(stored, 16)


def by_component(a, s=CS):
    import numpy as np
    v = a[..., s:]
    v = v.reshape(*v.shape[:-1], v.shape[-1] // 3, 3)
    return np.concatenate([a[..., :s], np.moveaxis(v, -1, -2).reshape(*a.shape[:-1], -1)], -1)


def layout(inputs):
    import numpy as np
    g = {n: np.asarray(a) for n, a in inputs.items()}
    z = lambda *s: np.zeros(s, np.float32)

    def diag(w):
        r, c = w.shape
        out = z(3 * r, 3 * c)
        for i in range(3):
            out[i * r:i * r + r, i * c:i * c + c] = w
        return out

    def col(*a):
        return np.concatenate(a)[:, None]

    def biased(w, b):
        return np.concatenate([w, b[None, :]], 0)

    w = {}
    p = "L0_gnn_"
    w.update(l0_src_s=g[p + "Ws_src"], l0_src_v=diag(g[p + "Wv_src"]), l0_dst_s=g[p + "Ws_dst"],
             l0_dst_v=diag(g[p + "Wv_dst"]), l0_rbf=g[p + "W_rbf"],
             l0_as=np.concatenate([g[p + "W_alpha"], g[p + "Ws_val"], z(96, 32)], 1),
             l0_val_t=g[p + "Ws_val"].T, l0_gate=g[p + "Wg"], l0_val_v=g[p + "Wv_val"],
             l0_vlin_s=g[p + "Ws_vlin"], l0_vlin_v=g[p + "Wv_vlin"], l0_ps=g[p + "Wps"],
             l0_pv=diag(g[p + "Wpv"]), l0_w2s=col(g[p + "w2_ss"], g[p + "w2_vv0"]),
             l0_w2v=col(g[p + "w2_sv"], g[p + "w2_vs"], g[p + "w2_vv1"]))
    p = "L1_gnn_"
    w.update(l1_skip_s=g[p + "W_skip0"], l1_skip_v=diag(g[p + "W_skip1"]), l1_in_s=g[p + "W_nl0"],
             l1_in_v=diag(g[p + "W_nl1"]), l1_fc1=g[p + "W_fc1"], l1_fc2=g[p + "W_fc2"],
             l1_out_s=g[p + "W_out_s"], l1_out_v=g[p + "W_out_v"])
    p = "L2_gnn_"
    w.update(l2_skip_s=g[p + "sc_ws"], l2_skip_v=diag(g[p + "sc_wv"]), l2_in_s=g[p + "lin1_ws"],
             l2_in_v=diag(g[p + "lin1_wv"]), l2_fc1=g[p + "fc_w1"], l2_fc2=g[p + "fc_w2"],
             l2_out_s=g[p + "lin2_ws"], l2_out_v=g[p + "lin2_wv"])
    p = "L3_gnn_"
    w.update(l3_src_s=g[p + "msrc_ws"], l3_src_v=diag(g[p + "msrc_wv"]), l3_dst_s=g[p + "mdst_ws"],
             l3_dst_v=diag(g[p + "mdst_wv"]), l3_rw1=biased(g[p + "rw1"], g[p + "rb1"]),
             l3_rw2=biased(g[p + "rw2"], g[p + "rb2"]), l3_rw3=biased(g[p + "rw3"], g[p + "roff"]),
             l3_rg1=col(g[p + "rg1"]), l3_rb1=col(g[p + "rbe1"]), l3_rg2=col(g[p + "rg2"]),
             l3_rb2=col(g[p + "rbe2"]), l3_lin_s=biased(g[p + "lin_ws"], g[p + "lin_bs"]),
             l3_lin_v=g[p + "lin_wv"], l3_proj_s=g[p + "proj_ws"], l3_proj_v=diag(g[p + "proj_wv"]),
             l3_f1_s=g[p + "f1_ws"], l3_f1_v=diag(g[p + "f1_wv"]), l3_f2_s=g[p + "f2_ws"],
             l3_f2_v=g[p + "f2_wv"])
    weights = z(128, WEIGHT_W)
    for name, (at, n) in WEIGHT_AT.items():
        weights[:WEIGHTS[name][0], at:at + n] = w[name]
    r = dict(
        l0_gs=g["L0_gnn_gamma_s"], l0_bs=g["L0_gnn_beta_s"], l0_gv=np.tile(g["L0_gnn_gamma_v"], 3),
        l0_adot=g["L0_gnn_alpha_dot"].reshape(-1), l3_gs1=g[p + "ln1_w0"], l3_bs1=g[p + "ln1_b0"],
        l3_gv1=np.tile(g[p + "ln1_w1"], 3), l3_gs2=g[p + "ln2_w0"], l3_bs2=g[p + "ln2_b0"],
        l3_gv2=np.tile(g[p + "ln2_w1"], 3), l3_adot=g[p + "alpha_dot"].reshape(-1),
        l3_dst_b=g[p + "mdst_bs"], l3_proj_b=g[p + "proj_bs"], l3_f1_b=g[p + "f1_bs"],
        l3_f2_b=g[p + "f2_bs"])
    rows = np.concatenate([r[n] for n in ROWS])
    c = z(128, CONST_W)
    for name, a in dict(ident=np.eye(128), before=np.triu(np.ones((128, PB)), 1), nodes=np.arange(PB),
                        blocks=np.arange(NB), groups=np.arange(NG)).items():
        at, n = CONST_AT[name]
        c[:, at:at + n] = a
    f = np.concatenate([g["edge_attr_64"], g["edge_attr_16"], g["edge_attr_4"]], 1)
    out = dict(
        x_rows=by_component(g["x"]).reshape(NB, PB, FN).transpose(1, 0, 2),
        consts=c, weights=weights, row_vectors=np.broadcast_to(rows, (128, ROW_W)),
        node_attr=g["node_vec1"].reshape(NB, PB).T, edge_rows=f.reshape(EP, EC, RH),
        edge_vec=g["edge_attr_3"].reshape(EP, EC, 3), src=g["src"].reshape(EP, EC),
        dst=g["dst"].reshape(EP, EC))
    return {n: np.ascontiguousarray(a) for n, a in out.items()}


def back(out):
    import numpy as np
    a = out.transpose(1, 0, 2).reshape(N, FN)
    v = a[:, CS:].reshape(N, 3, CV).transpose(0, 2, 1).reshape(N, FV)
    return np.ascontiguousarray(np.concatenate([a[:, :CS], v], 1))


def declare(nc, arrays):
    args = {n: nc.dram_tensor(f"in_{n}_dram", a.shape, mybir.dt.from_np(a.dtype),
                              kind="ExternalInput").ap() for n, a in arrays.items()}
    args["out"] = nc.dram_tensor("out_0_dram", (PB, NB, FN), F32, kind="ExternalOutput").ap()
    return args


def kernel(**inputs):
    import concourse.bacc as _bacc
    from concourse.bass_utils import run_bass_kernel_spmd as _run

    nc = _bacc.Bacc("TRN2", target_bir_lowering=False, num_devices=1)
    arrays = layout(inputs)
    gnn_kernel(nc, declare(nc, arrays))
    r = _run(nc, [{f"in_{n}_dram": a for n, a in arrays.items()}], core_ids=[0])
    return back(r.results[0]["out_0_dram"])
```

```python
from contextlib import ExitStack

import concourse.bass as bass
from concourse import mybir

F32 = mybir.dt.float32
I32 = mybir.dt.int32
BF16 = mybir.dt.bfloat16
ALU = mybir.AluOpType
ACT = mybir.ActivationFunctionType
AX_X = mybir.AxisListType.X
ds = bass.ds

N, E = 3125, 50000
CS, CV = 64, 32
FV = 3 * CV
FN = CS + FV
WN = 2 * CS + 3 * CV
PB, NB = 125, 25
EP, EC = 125, 400
GE = 256
NG = E // GE + NB
SLOTS = NG * GE
RING = 4
DEEP = 6
BIG = 1.0e30
EPS = 1e-5
SQ2, SQ3 = 2.0 ** 0.5, 3.0 ** 0.5
assert PB * NB == N and EP * EC == E and (E + NB * (GE - 1)) // GE <= NG and NG % RING == 0

R_A64, R_A16, R_Y, R_U1, R_U3, R_SRC, R_DST, R_LSRC, R_LDST = 0, 64, 80, 84, 87, 90, 91, 92, 93
RH, RW = 84, 94

P_A, P_C, P_D, P_B, P_X, PW = 0, 64, 224, 320, 384, 640
MW = 512

CONST_COLS = dict(ident=128, before=PB, nodes=PB, blocks=NB, groups=NG)
WEIGHTS = dict(
    l0_src_s=(CS, CS), l0_src_v=(FV, FV), l0_dst_s=(CS, CS), l0_dst_v=(FV, FV), l0_rbf=(16, WN),
    l0_as=(96, 160), l0_val_t=(CS, 96), l0_gate=(CS, CV), l0_val_v=(128, CV), l0_vlin_s=(96, CS),
    l0_vlin_v=(128, CV), l0_ps=(CS, CS), l0_pv=(FV, FV), l0_w2s=(96, 1), l0_w2v=(128, 1),
    l1_skip_s=(CS, 96), l1_skip_v=(FV, FV), l1_in_s=(CS, CS), l1_in_v=(FV, FV), l1_fc1=(64, 64),
    l1_fc2=(64, WN), l1_out_s=(96, 96), l1_out_v=(128, CV),
    l2_skip_s=(CS, 96), l2_skip_v=(FV, FV), l2_in_s=(CS, CS), l2_in_v=(FV, FV), l2_fc1=(64, 64),
    l2_fc2=(64, WN), l2_out_s=(96, 96), l2_out_v=(128, CV),
    l3_src_s=(CS, CS), l3_src_v=(FV, FV), l3_dst_s=(CS, CS), l3_dst_v=(FV, FV),
    l3_rw1=(65, 64), l3_rw2=(65, 64), l3_rw3=(65, WN), l3_rg1=(64, 1), l3_rb1=(64, 1),
    l3_rg2=(64, 1), l3_rb2=(64, 1), l3_lin_s=(97, 128), l3_lin_v=(128, CV),
    l3_proj_s=(CS, CS), l3_proj_v=(FV, FV), l3_f1_s=(CS, 192), l3_f1_v=(FV, 192),
    l3_f2_s=(128, CS), l3_f2_v=(64, CV),
)
ROWS = dict(
    l0_gs=CS, l0_bs=CS, l0_gv=FV, l0_adot=64, l3_gs1=CS, l3_bs1=CS, l3_gv1=FV, l3_gs2=CS,
    l3_bs2=CS, l3_gv2=FV, l3_adot=64, l3_dst_b=CS, l3_proj_b=CS, l3_f1_b=192, l3_f2_b=CS,
)


def offsets(columns):
    at, out = 0, {}
    for name, n in columns.items():
        out[name] = (at, n)
        at += n
    return out, at


CONST_AT, CONST_W = offsets(CONST_COLS)
WEIGHT_AT, WEIGHT_W = offsets({k: c for k, (_, c) in WEIGHTS.items()})
ROW_AT, ROW_W = offsets(ROWS)


class Chain:

    def __init__(self, eng, sem):
        self.eng, self.sem, self.n = eng, sem, 0

    def add(self, ins):
        ins.then_inc(self.sem, 1)
        self.n += 1

    def then(self, ins):
        self.add(ins)
        self.eng.wait_ge(self.sem, self.n)


def group(j, c, lag, ring=RING, count=NG):
    g = ring * j + (c - lag)
    if isinstance(g, int) and not 0 <= g < count:
        return None
    return g, (c - lag) % ring, j + (c - lag) // ring


def past(g, n):
    return g >= n if isinstance(g, int) else True


def steps(eng, body, lag, ring=RING, count=NG):
    first = -(-(lag + ring) // ring)
    for j in range(first):
        for c in range(ring):
            body(j, c)
    with eng.Fori(first, count // ring) as j:
        for c in range(ring):
            body(j, c)
    for i in range(count - count % ring, count + lag):
        body(i // ring, i % ring)


class Kernel:
    def __init__(self, nc, stack, args):
        self.nc = nc
        self.args = args
        self.stack = stack
        self.scope = stack
        self.sems = []
        self.tag = "k"
        d = nc.dram_tensor
        self.by_dst = d("rows_by_dst", (SLOTS, RW), F32, kind="Internal").ap()
        self.by_src = d("rows_by_src", (SLOTS, RW), F32, kind="Internal").ap()
        self.table = d("message_table", (N, FN), F32, kind="Internal").ap()
        self.hidden = d("radial_hidden", (NG * 64, GE), F32, kind="Internal").ap()
        self.x = self.sb("x", [PB, NB, FN])
        self.h = self.sb("h", [PB, NB, FN])
        self.c = self.sb("consts", [128, CONST_W])
        self.w = self.sb("weights", [128, WEIGHT_W])
        self.r = self.sb("rows", [128, ROW_W])
        self.block_of_dst = self.sb("block_of_dst", [1, NG], I32)
        self.block_of_src = self.sb("block_of_src", [1, NG], I32)
        self.a0 = self.sb("node_attr", [PB, NB])
        self.half = self.sb("minus_half", [128, 512])

    def sb(self, name, shape, dt=F32):
        return self.scope.enter_context(self.nc.sbuf_tensor(f"{self.tag}_{name}", shape, dt))

    def ps(self, name, shape):
        return self.scope.enter_context(self.nc.psum_tensor(f"{self.tag}_{name}", shape, F32))

    def sem(self, name):
        s = self.nc.alloc_semaphore(name=f"{self.tag}_{name}")
        self.sems.append(s)
        return s

    def const(self, name, rows=128):
        at, n = CONST_AT[name]
        return self.c[0:rows, at:at + n]

    def wt(self, name, lo=0, hi=None):
        at, n = WEIGHT_AT[name]
        return self.w[lo:WEIGHTS[name][0] if hi is None else hi, at:at + n]

    def wt_pair(self, a, b):
        at = WEIGHT_AT[a][0]
        assert WEIGHT_AT[b][0] == at + 1
        return self.w[0:WEIGHTS[a][0], at:at + 2]

    def row(self, name, rows=128):
        at, n = ROW_AT[name]
        return self.r[0:rows, at:at + n]

    def blockrow(self, name):
        return self.row(name, PB).unsqueeze(1).to_broadcast([PB, NB, ROWS[name]])

    def phase(self, tag):
        return Phase(self, tag)


class Phase:

    def __init__(self, k, tag):
        self.k, self.tag = k, tag

    def __enter__(self):
        self.old = (self.k.scope, self.k.tag, self.k.sems)
        self.k.sems = []
        self.stack = ExitStack()
        self.stack.__enter__()
        self.k.scope, self.k.tag = self.stack, self.tag
        return self.k

    def __exit__(self, *e):
        done = self.k.sems
        self.k.scope, self.k.tag, self.k.sems = self.old
        self.stack.__exit__(*e)
        if done and e[0] is None:
            self.k.nc.clear_and_free_semaphores(done)
            self.k.nc.all_engine_barrier()


def prepare(k):
    nc = k.nc
    with k.phase("prep"), nc.Block() as block:
        loaded, scaled, gated, zeroed = (k.sem(n) for n in ("loaded", "scaled", "gated", "zeroed"))
        pg = k.ps("gate_product", [128, 512])
        mean = k.sb("row_mean", [128, 2])

        @block.sync
        def _(sp):
            for dst, src in ((k.x[:], k.args["x_rows"]), (k.c[:], k.args["consts"]),
                             (k.w[:], k.args["weights"]), (k.r[:], k.args["row_vectors"]),
                             (k.a0[:], k.args["node_attr"])):
                sp.dma_start(dst, src).then_inc(loaded, 16)
            sp.wait_ge(loaded, 80)

        @block.gpsimd
        def _(pool):
            pool.memset(k.half[:], -0.5).then_inc(zeroed, 1)

        @block.tensor
        def _(pe):
            pe.wait_ge(loaded, 80)
            pe.matmul(pg[0:96, 0:CV], k.wt("l0_val_t"), k.wt("l0_gate"), start=True, stop=True)\
                .then_inc(gated, 1)

        @block.vector
        def _(dve):
            ch = Chain(dve, scaled)
            dve.wait_ge(loaded, 80)
            dve.wait_ge(gated, 1)
            ch.then(dve.tensor_copy(k.wt("l0_as")[:, 128:160], pg[0:96, 0:CV]))

            def scale(name, lo, hi, by):
                ap = k.wt(name, lo, hi)
                ch.then(dve.tensor_scalar(ap, ap, by, None, ALU.mult))

            scale("l0_as", 64, 96, 1 / SQ3)
            scale("l0_val_v", 96, 128, 1 / SQ2)
            scale("l0_vlin_s", 0, 96, k.wt("l0_w2s"))
            scale("l0_vlin_s", 64, 96, 1 / SQ3)
            scale("l0_vlin_v", 0, 128, k.wt("l0_w2v"))
            scale("l0_vlin_v", 96, 128, 1 / SQ2)
            scale("l1_out_s", 0, 96, 1 / 32)
            scale("l1_out_v", 0, 64, SQ3 / 32)
            scale("l1_out_v", 64, 96, 1 / 32)
            scale("l1_out_v", 96, 128, SQ3 / SQ2 / 32)
            for n in ("l2_skip_s", "l2_in_s"):
                scale(n, 0, CS, 1 / 8)
            for n in ("l2_skip_v", "l2_in_v"):
                scale(n, 0, FV, 32 ** -0.5)
            scale("l2_out_s", 0, 64, 96 ** -0.5 / 512)
            scale("l2_out_s", 64, 96, 96 ** -0.5 / SQ3 / 512)
            scale("l2_out_v", 0, 96, 128 ** -0.5 / 512)
            scale("l2_out_v", 96, 128, 128 ** -0.5 / SQ2 / 512)
            scale("l3_lin_v", 0, 64, SQ3)
            scale("l3_lin_v", 96, 128, SQ3 / SQ2)
            scale("l3_rw2", 0, 64, 0.5)
            scale("l3_rw3", 0, 64, 0.5)
            for n, name in enumerate(("l3_rw1", "l3_rw2")):
                m = mean[0:65, n:n + 1]
                ch.then(dve.tensor_reduce(m, k.wt(name), AX_X, ALU.add))
                ch.then(dve.tensor_scalar(m, m, 1 / 64, None, ALU.mult))
                ch.then(dve.tensor_scalar(k.wt(name), k.wt(name), m, None, ALU.subtract))


def sort_edges(k):
    nc = k.nc
    CH = 8
    with k.phase("sort"):
        loaded, padded, counted, totalled, unit, fills = (
            k.sem(n) for n in ("loaded", "padded", "counted", "totalled", "unit", "fills"))
        pos = [k.sb(f"position{i}", [EP, EC], I32) for i in range(2)]
        tail = k.sb("tail", [EP, EC, RW - RH])
        with k.phase("count"):
            key_i = [k.sb(f"key_i{i}", [EP, EC], I32) for i in range(2)]
            vec = k.sb("vec", [EP, EC, 3])
            sq = k.sb("sq", [EP, EC, 3])
            n2 = k.sb("n2", [EP, 2, EC])
            zeros = k.sb("zeros", [EP, EC])
            bf = k.sb("block", [EP, EC])
            hot = k.sb("hot", [EP, NB, EC])
            rank = k.sb("rank", [EP, NB, EC])
            tot = k.sb("tot", [EP, NB])
            ones = k.sb("ones", [EP, EP])
            cnt_i = k.sb("cnt_i", [EP, NB], I32)
            ngr = k.sb("ngr", [EP, NB])
            inc = k.sb("inc", [EP, NB])
            base = k.sb("base", [EP, NB])
            gm = k.sb("gm", [1, NG, NB])
            gmf = k.sb("gmf", [1, NG])
            pad = k.sb("pad", [128, 22, RW])
            pc = k.ps("counts", [EP, 512])
            with nc.Block() as block:

                @block.sync
                def _(sp):
                    sp.dma_start(key_i[0][:], k.args["dst"]).then_inc(loaded, 16)
                    sp.dma_start(key_i[1][:], k.args["src"]).then_inc(loaded, 16)
                    sp.dma_start(vec[:], k.args["edge_vec"]).then_inc(loaded, 16)
                    sp.wait_ge(padded, 3)
                    n = 0
                    for t in (k.by_dst, k.by_src):
                        v = t.rearrange("(p c) w -> p c w", p=128)
                        for c in range(0, SLOTS // 128, 22):
                            sp.dma_start(v[:, c:c + 22, :], pad[:]).then_inc(fills, 16)
                            n += 16
                    sp.wait_ge(fills, n)

                @block.gpsimd
                def _(pool):
                    pool.memset(pad[:], 0.0).then_inc(padded, 1)
                    pool.memset(ones[:], 1.0).then_inc(padded, 1)
                    pool.wait_ge(padded, 1)
                    pool.memset(pad[:, :, R_LSRC:R_LDST + 1], -1.0).then_inc(padded, 1)
                    pool.wait_ge(unit, 3)
                    for i in range(2):
                        pool.tensor_tensor(n2[:, i, :], n2[:, i, :], k.half[0:EP, 0:EC], ALU.pow)\
                            .then_inc(unit, 1)

                @block.tensor
                def _(pe):
                    pe.wait_ge(padded, 3)
                    for i in range(2):
                        pe.wait_ge(totalled, 2 * i + 1)
                        pe.matmul(pc[:, 0:NB], k.const("before", EP), tot[:], start=True, stop=True)
                        pe.matmul(pc[:, NB:2 * NB], ones[:], tot[:], start=True, stop=True)\
                            .then_inc(totalled, 1)

                @block.vector
                def _(dve):
                    ch = Chain(dve, counted)
                    ch.then(dve.memset(zeros[:], 0.0))
                    dve.wait_ge(loaded, 48)
                    dve.tensor_tensor(sq[:], vec[:], vec[:], ALU.mult).then_inc(unit, 1)
                    dve.wait_ge(unit, 1)
                    dve.tensor_reduce(n2[:, 0, :], sq[:], AX_X, ALU.add).then_inc(unit, 1)
                    dve.wait_ge(unit, 2)
                    dve.tensor_scalar(n2[:, 1, :], n2[:, 0, :], 1e-12, None, ALU.add).then_inc(unit, 1)
                    for i, (raw, local) in enumerate(((R_DST, R_LDST), (R_SRC, R_LSRC))):
                        kf = tail[:, :, raw - RH]
                        ch.then(dve.tensor_copy(kf, key_i[i][:]))
                        ch.then(dve.tensor_scalar(bf[:], kf, float(PB), None, ALU.is_ge))
                        for b in range(2, NB):
                            ch.then(dve.scalar_tensor_tensor(bf[:], kf, float(PB * b), bf[:],
                                                             ALU.is_ge, ALU.add))
                        ch.add(dve.scalar_tensor_tensor(tail[:, :, local - RH], bf[:], -float(PB), kf,
                                                        ALU.mult, ALU.add))
                        ch.then(dve.tensor_tensor(
                            hot[:], bf[:].unsqueeze(1).to_broadcast([EP, NB, EC]),
                            k.const("blocks", EP).unsqueeze(2).to_broadcast([EP, NB, EC]),
                            ALU.is_equal))
                        for b in range(NB):
                            ch.add(dve.tensor_tensor_scan(rank[:, b, :], hot[:, b, :], zeros[:], 0.0,
                                                          ALU.add, ALU.add))
                        dve.wait_ge(counted, ch.n)
                        dve.tensor_copy(tot[:], rank[:, :, EC - 1]).then_inc(totalled, 1)
                        dve.wait_ge(totalled, 2 * i + 2)
                        ch.then(dve.tensor_scalar(ngr[:], pc[:, NB:2 * NB], float(GE - 1), None, ALU.add))
                        ch.then(dve.tensor_copy(cnt_i[:], ngr[:]))
                        ch.then(dve.tensor_scalar(cnt_i[:], cnt_i[:], GE.bit_length() - 1, None,
                                                  ALU.arith_shift_right))
                        ch.then(dve.tensor_copy(ngr[:], cnt_i[:]))
                        ch.then(dve.tensor_tensor_scan(inc[:], ngr[:], zeros[:, 0:NB], 0.0,
                                                       ALU.add, ALU.add))
                        ch.then(dve.tensor_tensor(inc[:], inc[:], ngr[:], ALU.subtract))
                        ch.then(dve.tensor_scalar(base[:], inc[:], float(GE), -1.0, ALU.mult, ALU.add))
                        ch.then(dve.tensor_tensor(base[:], base[:], pc[:, 0:NB], ALU.add))
                        ch.then(dve.tensor_tensor(rank[:], rank[:],
                                                  base[:].unsqueeze(2).to_broadcast([EP, NB, EC]), ALU.add))
                        ch.then(dve.tensor_tensor(rank[:], rank[:], hot[:], ALU.mult))
                        ch.then(dve.tensor_reduce(bf[:], rank[:].rearrange("p b c -> p c b"), AX_X, ALU.add))
                        ch.add(dve.tensor_copy(pos[i][:], bf[:]))
                        ch.then(dve.tensor_tensor(
                            gm[:], k.const("groups", 1).unsqueeze(2).to_broadcast([1, NG, NB]),
                            inc[0:1, :].unsqueeze(1).to_broadcast([1, NG, NB]), ALU.is_ge))
                        ch.then(dve.tensor_reduce(gmf[:], gm[:, :, 1:NB], AX_X, ALU.add))
                        ch.then(dve.tensor_copy((k.block_of_dst, k.block_of_src)[i][:], gmf[:]))
                    dve.wait_ge(unit, 5)
                    for i, col in enumerate((R_U1, R_U3)):
                        ch.add(dve.tensor_tensor(
                            tail[:, :, col - RH:col - RH + 3], vec[:],
                            n2[:, i, :].unsqueeze(2).to_broadcast([EP, EC, 3]), ALU.mult))

        with k.phase("place"):
            rows = [k.sb(f"row_buffer{i}", [EP, CH, RW]) for i in range(2)]
            idx = [k.sb(f"slot_index{i}", [EP, 2, CH], I32) for i in range(2)]
            row_in = [k.sem(f"row_in{i}") for i in range(2)]
            placed = [k.sem(f"placed{i}") for i in range(2)]
            ready, gate = k.sem("ready"), k.sem("gate")
            edge_rows = k.args["edge_rows"]
            per = 2 * CH * 16
            with nc.Block() as block:

                def each(eng, body):
                    for c in range(2):
                        body(0, c)
                    with eng.Fori(1, EC // CH // 2) as j:
                        for c in range(2):
                            body(j, c)

                @block.sync
                def _(sp):
                    def body(j, c):
                        if past(j, 1):
                            sp.wait_ge(placed[c], j * per)
                        sp.dma_start(rows[c][:, :, 0:RH], edge_rows[:, ds((2 * j + c) * CH, CH), :])\
                            .then_inc(row_in[c], 16)
                    each(sp, body)

                @block.vector
                def _(dve):
                    def body(j, c):
                        if past(j, 1):
                            dve.wait_ge(placed[c], j * per)
                        cols = ds((2 * j + c) * CH, CH)
                        dve.tensor_scalar(rows[c][:, :, RH:RW], tail[:, cols, :], 1.0, None, ALU.mult)\
                            .then_inc(ready, 1)
                        for i in range(2):
                            dve.tensor_copy(idx[c][:, i, :], pos[i][:, cols]).then_inc(ready, 1)
                    each(dve, body)

                @block.gpsimd
                def _(pool):
                    def body(j, c):
                        pool.wait_ge(row_in[c], (j + 1) * 16)
                        pool.wait_ge(ready, (2 * j + c) * 3 + 3)
                        pool.sem_inc(gate, 1)
                        for i, t in enumerate((k.by_dst, k.by_src)):
                            for n in range(CH):
                                pool.indirect_dma_start(
                                    out=t, out_offset=bass.IndirectOffsetOnAxis(ap=idx[c][:, i, n:n + 1], axis=0),
                                    in_=rows[c][:, n, :], in_offset=None).then_inc(placed[c], 16)
                    each(pool, body)
                    for c in range(2):
                        pool.wait_ge(placed[c], EC // CH // 2 * per)


def norm_nodes(k, tag, relu, source=None, target=None, gains=None, v_div=None):
    nc = k.nc
    with k.phase(tag), nc.Block() as block:
        done, powed = k.sem("done"), k.sem("powed")
        sq = k.sb("sq", [PB, NB, FN])
        var = k.sb("var", [PB, 3, NB])
        mean = k.sb("mean", [PB, 2, NB])
        marks = []

        def over(ap, n):
            return ap.unsqueeze(2).to_broadcast([PB, NB, n])

        @block.vector
        def _(dve):
            ch = Chain(dve, done)
            if relu:
                m, v = mean[:, 0, :], var[:, 0, :]
                ch.then(dve.tensor_reduce(m, k.x[:], AX_X, ALU.add))
                ch.then(dve.tensor_scalar(m, m, 1 / FN, None, ALU.mult))
                ch.then(dve.tensor_tensor(k.h[:], k.x[:], over(m, FN), ALU.subtract))
                ch.then(dve.tensor_tensor(sq[:], k.h[:], k.h[:], ALU.mult))
                ch.then(dve.tensor_reduce(v, sq[:], AX_X, ALU.add))
                ch.then(dve.tensor_scalar(v, v, 1 / FN, EPS, ALU.mult, ALU.add))
                marks.append((ch.n, v))
                dve.wait_ge(powed, len(marks))
                ch.then(dve.tensor_tensor(k.h[:], k.h[:], over(v, FN), ALU.mult))
                ch.then(dve.tensor_scalar(k.h[:], k.h[:], 0.0, None, ALU.max))
            if gains:
                m = mean[:, 1, :]
                s, v = slice(0, CS), slice(CS, FN)
                ch.then(dve.tensor_reduce(m, source[:, :, s], AX_X, ALU.add))
                ch.then(dve.tensor_scalar(m, m, 1 / CS, None, ALU.mult))
                ch.then(dve.tensor_tensor(target[:, :, s], source[:, :, s], over(m, CS), ALU.subtract))
                ch.add(dve.tensor_tensor(sq[:, :, s], target[:, :, s], target[:, :, s], ALU.mult))
                ch.then(dve.tensor_tensor(sq[:, :, v], source[:, :, v], source[:, :, v], ALU.mult))
                ch.add(dve.tensor_reduce(var[:, 1, :], sq[:, :, s], AX_X, ALU.add))
                ch.then(dve.tensor_reduce(var[:, 2, :], sq[:, :, v], AX_X, ALU.add))
                ch.add(dve.tensor_scalar(var[:, 1, :], var[:, 1, :], 1 / CS, EPS, ALU.mult, ALU.add))
                ch.add(dve.tensor_scalar(var[:, 2, :], var[:, 2, :], 1 / v_div, EPS, ALU.mult, ALU.add))
                marks.append((ch.n, var[:, 1:3, :]))
                dve.wait_ge(powed, len(marks))
                ch.add(dve.tensor_tensor(target[:, :, s], target[:, :, s], over(var[:, 1, :], CS), ALU.mult))
                ch.then(dve.tensor_tensor(target[:, :, v], source[:, :, v], over(var[:, 2, :], FV), ALU.mult))
                gs, bs, gv = (k.blockrow(n) for n in gains)
                ch.add(dve.tensor_tensor(target[:, :, v], target[:, :, v], gv, ALU.mult))
                ch.then(dve.tensor_tensor(target[:, :, s], target[:, :, s], gs, ALU.mult))
                ch.then(dve.tensor_tensor(target[:, :, s], target[:, :, s], bs, ALU.add))

        @block.gpsimd
        def _(pool):
            for at, v in marks:
                pool.wait_ge(done, at)
                n = v.shape[1] * v.shape[2] if len(v.shape) == 3 else v.shape[1]
                e = k.half[0:PB, 0:n]
                e = e.rearrange("p (a b) -> p a b", a=v.shape[1]) if len(v.shape) == 3 else e
                pool.tensor_tensor(v, v, e, ALU.pow).then_inc(powed, 1)


def node_linear(k, tag, width, fill, fills, slices, evacs, products, outs):
    nc = k.nc
    with k.phase(tag), nc.Block() as block:
        staged, turned, copied, multiplied, stored, gate = (
            k.sem(n) for n in ("staged", "turned", "copied", "multiplied", "stored", "gate"))
        stage = [k.sb(f"stage{c}", [PB, width]) for c in range(2)]
        banks = -(-len(slices) // 4)
        turned_sb = [k.sb(f"turned{c}", [128, banks * 4, 128]) for c in range(2)]
        pt = [k.ps(f"pt{c}", [128, banks * 4, 128]) for c in range(2)]
        po = [k.ps(f"po{c}", [128, 512]) for c in range(2)]

        @block.vector
        def _(dve):
            def body(j, c):
                g = group(j, c, 0, 2, NB)
                if g:
                    b, s, _ = g
                    if past(b, 2):
                        dve.wait_ge(turned, b - 1)
                    fill(dve, b, stage[s], staged)
                g = group(j, c, 1, 2, NB)
                if g:
                    b, s, _ = g
                    dve.wait_ge(multiplied, b + 1)
                    for lo, n, tile in outs:
                        dve.tensor_scalar(tile[:, ds(b, 1), :], po[s][0:PB, lo:lo + n].unsqueeze(1),
                                          1.0, None, ALU.mult).then_inc(stored, 1)
            steps(dve, body, 1, 2, NB)

        @block.tensor
        def _(pe):
            def body(j, c):
                g = group(j, c, 0, 2, NB)
                if g:
                    b, s, _ = g
                    pe.wait_ge(staged, fills * b + fills)
                    if past(b, 2):
                        pe.wait_ge(copied, len(evacs) * b - len(evacs))
                    pe.sem_inc(gate, 1)
                    for n, (lo, hi) in enumerate(slices):
                        last = pe.transpose(pt[s][0:hi - lo, n, 0:PB], stage[s][:, lo:hi],
                                            k.const("ident", PB)[:, 0:PB])
                    last.then_inc(turned, 1)
                g = group(j, c, 1, 2, NB)
                if g:
                    b, s, _ = g
                    pe.wait_ge(copied, len(evacs) * b + len(evacs))
                    if past(b, 2):
                        pe.wait_ge(stored, len(outs) * b - len(outs))
                    pe.sem_inc(gate, 1)
                    for n, rows, w, lo, start, stop in products:
                        last = pe.matmul(po[s][0:PB, lo:lo + w.shape[1]], turned_sb[s][0:rows, n, 0:PB],
                                         w, start=start, stop=stop, skip_group_check=True)
                    last.then_inc(multiplied, 1)
            steps(pe, body, 1, 2, NB)

        @block.scalar
        def _(act):
            def body(j, c):
                g = group(j, c, 0, 2, NB)
                if g:
                    b, s, _ = g
                    act.wait_ge(turned, b + 1)
                    if past(b, 2):
                        act.wait_ge(multiplied, b - 1)
                    for n, m, rows in evacs:
                        act.activation(turned_sb[s][0:rows, n:n + m, 0:PB], pt[s][0:rows, n:n + m, 0:PB],
                                       ACT.Copy).then_inc(copied, 1)
            steps(act, body, 1, 2, NB)


def copy_fill(tile, width):
    def fill(dve, b, stage, staged):
        dve.tensor_scalar(stage[:, 0:width].unsqueeze(1), tile[:, ds(b, 1), 0:width], 1.0, None,
                          ALU.mult).then_inc(staged, 1)
    return fill


SV_SLICES = [(0, CS), (CS, FN)]
SV_EVACS = [(0, 1, CS), (1, 1, FV)]


def write_table(k, tag, tile):
    nc = k.nc
    with k.phase(tag), nc.Block() as block:
        written, scaled = k.sem("written"), k.sem("scaled")

        @block.vector
        def _(dve):
            if tag == "l2_table":
                dve.tensor_tensor(tile[:], tile[:], k.a0[:].unsqueeze(2).to_broadcast([PB, NB, FN]),
                                  ALU.mult).then_inc(scaled, 1)

        @block.sync
        def _(sp):
            if tag == "l2_table":
                sp.wait_ge(scaled, 1)
            sp.dma_start(k.table.rearrange("(b p) f -> p b f", p=PB), tile[:]).then_inc(written, 16)
            sp.wait_ge(written, 16)


def late_edges(k, tag, rows_dram, block_of, gather_col, local_col, y_cols, silu, acc):
    nc = k.nc
    lo_y, n_y = y_cols
    with k.phase(tag), nc.Block() as block:
        rows = [k.sb(f"rows{s}", [128, 2, RW]) for s in range(RING)]
        idx = [k.sb(f"index{s}", [128, 2], I32) for s in range(RING)]
        msg = [k.sb(f"message{s}", [128, 2, FN]) for s in range(RING)]
        hot = [k.sb(f"hot{s}", [128, 2, 4, PB]) for s in range(2)]
        prod = [k.sb(f"prod{s}", [128, 2, 544]) for s in range(2)]
        one = k.sb("one", [128, 2, PB])
        feat = [k.sb(f"features{s}", [64, GE]) for s in range(2)]
        hid = [k.sb(f"hidden{s}", [64, GE]) for s in range(2)]
        tanh = [k.sb(f"tanh{s}", [64, GE]) for s in range(2)]
        p1 = [k.ps(f"turned{s}", [128, 2, GE]) for s in range(2)]
        pw = [k.ps(f"weights{s}", [128, 2, 256]) for s in range(2)]
        pa = [k.ps(f"sums{s}", [128, 2, 512]) for s in range(2)]
        row_in = [k.sem(f"row_in{s}") for s in range(RING)]
        gathered = [k.sem(f"gathered{s}") for s in range(RING)]
        (indexed, hots, turned, copied, hidden, silued, weighed, multiplied, summed, added, gate,
         compared, tanhed, sp_gate) = (
            k.sem(n) for n in ("indexed", "hots", "turned", "copied", "hidden", "silued", "weighed",
                               "multiplied", "summed", "added", "gate", "compared", "tanhed",
                               "sp_gate"))
        scaled_hot = k.sem("scaled_hot")
        view = rows_dram.rearrange("(g p u) w -> g p u w", p=128, u=2)

        @block.sync
        def _(sp):
            def body(j, c):
                g, s, r = group(j, c, 0)
                if past(g, RING):
                    sp.wait_ge(hots, g - RING + 1)
                    sp.wait_ge(turned, g - RING + 1)
                sp.sem_inc(sp_gate, 1)
                sp.dma_start(rows[s][:], view[ds(g, 1)].rearrange("a p u w -> p (a u) w"))\
                    .then_inc(row_in[s], 16)
            steps(sp, body, 0)

        @block.gpsimd
        def _(pool):
            def body(j, c):
                g, s, r = group(j, c, 0)
                pool.wait_ge(indexed, g + 1)
                if past(g, RING):
                    pool.wait_ge(multiplied, (g - RING) * 5 + 5)
                pool.sem_inc(gate, 1)
                for u in range(2):
                    pool.indirect_dma_start(
                        out=msg[s][:, u, :], out_offset=None, in_=k.table,
                        in_offset=bass.IndirectOffsetOnAxis(ap=idx[s][:, u:u + 1], axis=0))\
                        .then_inc(gathered[s], 16)
            steps(pool, body, 0)

        @block.scalar
        def _(act):
            def body(j, c):
                at = group(j, c, 0)
                if at:
                    g, s, r = at
                    act.wait_ge(turned, g + 1)
                    if past(g, 2):
                        act.wait_ge(hidden, g - 1)
                    act.activation(feat[s % 2][:], p1[s % 2][0:64, 0, :], ACT.Copy).then_inc(copied, 1)
                at = group(j, c, 1)
                if at:
                    g, s, r = at
                    act.wait_ge(hidden, g + 1)
                    if silu:
                        if past(g, 2):
                            act.wait_ge(silued, g - 1)
                        act.activation(tanh[s % 2][:], p1[s % 2][0:64, 1, :], ACT.Tanh, scale=1 / 16)\
                            .then_inc(tanhed, 1)
                    else:
                        if past(g, 2):
                            act.wait_ge(weighed, g - 1)
                        act.activation(hid[s % 2][:], p1[s % 2][0:64, 1, :], ACT.Relu)\
                            .then_inc(silued, 1)
            steps(act, body, 3)

        @block.tensor
        def _(pe):
            fc1, fc2 = (k.wt(f"{tag[0:2]}_fc{n}") for n in (1, 2))

            def body(j, c):
                at = group(j, c, 0)
                if at:
                    g, s, r = at
                    pe.wait_ge(row_in[s], r * 16 + 16)
                    if past(g, 2):
                        pe.wait_ge(silued, g - 1)
                    pe.sem_inc(gate, 1)
                    for u in range(2):
                        last = pe.transpose(p1[s % 2][0:64, 0, u * 128:u * 128 + 128],
                                            rows[s][:, u, R_A64:R_A64 + 64], k.const("ident"))
                    last.then_inc(turned, 1)
                at = group(j, c, 3)
                if at:
                    g, s, r = at
                    b = s % 2
                    pe.wait_ge(hots, g + 1)
                    pe.wait_ge(multiplied, g * 5 + 5)
                    if past(g, 2):
                        pe.wait_ge(added, g * 2 - 2)
                    pe.sem_inc(gate, 1)
                    out = pa[b]
                    for y, bank, col in ((0, 0, 0), (1, 0, 160), (2, 1, 0), (3, 1, 192)):
                        for u in range(2):
                            if y == 0:
                                n, m = 160, prod[b][:, u, 0:160]
                            else:
                                n, m = 192, prod[b][:, u, 160:544].rearrange(
                                    "p (t n) -> p t n", n=96)[:, 0:y + 1:y, :]
                            last = pe.matmul(out[0:PB, bank, col:col + n], hot[b][:, u, y, :], m,
                                             start=u == 0, stop=u == 1, skip_group_check=True)
                    last.then_inc(summed, 1)
                at = group(j, c, 0)
                if at:
                    g, s, r = at
                    pe.wait_ge(copied, g + 1)
                    pe.sem_inc(gate, 1)
                    pe.matmul(p1[s % 2][0:64, 1, :], fc1, feat[s % 2][:], start=True, stop=True)\
                        .then_inc(hidden, 1)
                at = group(j, c, 1)
                if at:
                    g, s, r = at
                    pe.wait_ge(silued, g + 1)
                    if past(g, 2):
                        pe.wait_ge(multiplied, g * 5 - 5)
                    pe.sem_inc(gate, 1)
                    for u in range(2):
                        last = pe.matmul(pw[s % 2][:, u, 0:WN], hid[s % 2][:, u * 128:u * 128 + 128], fc2,
                                         start=True, stop=True)
                    last.then_inc(weighed, 1)
            steps(pe, body, 4)

        @block.vector
        def _(dve):
            dve.memset(one[:], 1.0).then_inc(compared, 1)
            dve.memset(acc[:], 0.0).then_inc(compared, 1)
            dve.wait_ge(compared, 2)

            def body(j, c):
                at = group(j, c, 0)
                if at:
                    g, s, r = at
                    dve.wait_ge(row_in[s], r * 16 + 16)
                    if past(g, RING):
                        dve.wait_ge(gathered[s], r * 32)
                    dve.tensor_copy(idx[s][:], rows[s][:, :, gather_col]).then_inc(indexed, 1)
                at = group(j, c, 1)
                if at and silu:
                    g, s, r = at
                    dve.wait_ge(tanhed, g + 1)
                    if past(g, 2):
                        dve.wait_ge(weighed, g - 1)
                    dve.scalar_tensor_tensor(hid[s % 2][:], tanh[s % 2][:], 1.0, p1[s % 2][0:64, 1, :],
                                             ALU.add, ALU.mult).then_inc(silued, 1)
                at = group(j, c, 2)
                if at:
                    g, s, r = at
                    b = s % 2
                    if past(g, 2):
                        dve.wait_ge(summed, g - 1)
                    dve.tensor_tensor(hot[b][:, :, 0, :],
                                      k.const("nodes").unsqueeze(1).to_broadcast([128, 2, PB]),
                                      rows[s][:, :, local_col:local_col + 1].to_broadcast([128, 2, PB]),
                                      ALU.is_equal).then_inc(compared, 1)
                    dve.wait_ge(compared, g + 3)
                    last = dve.tensor_tensor(
                        hot[b][:, :, 1:4, :], hot[b][:, :, 0:1, :].to_broadcast([128, 2, 3, PB]),
                        rows[s][:, :, lo_y + n_y - 3:lo_y + n_y].unsqueeze(3).to_broadcast([128, 2, 3, PB]),
                        ALU.mult)
                    if n_y == 4:
                        last.then_inc(scaled_hot, 1)
                        dve.wait_ge(scaled_hot, g + 1)
                        last = dve.tensor_tensor(hot[b][:, :, 0, :], hot[b][:, :, 0, :],
                                                 rows[s][:, :, lo_y:lo_y + 1].to_broadcast([128, 2, PB]),
                                                 ALU.mult)
                    last.then_inc(hots, 1)
                    dve.wait_ge(gathered[s], r * 32 + 32)
                    dve.wait_ge(weighed, g + 1)
                    w = pw[b]
                    pr = prod[b]
                    bd = pr[:, :, 256:544].rearrange("p u (i n) -> p u i n", i=3)
                    m_s = msg[s][:, :, 0:CS]
                    m_v = msg[s][:, :, CS:FN].rearrange("p u (i n) -> p u i n", i=3)
                    dve.tensor_tensor(pr[:, :, 0:64], w[:, :, 0:64], m_s, ALU.mult)\
                        .then_inc(multiplied, 1)
                    dve.tensor_tensor(bd[:, :, :, 0:64],
                                      w[:, :, 64:128].unsqueeze(2).to_broadcast([128, 2, 3, 64]),
                                      m_s.unsqueeze(2).to_broadcast([128, 2, 3, 64]), ALU.mult)\
                        .then_inc(multiplied, 1)
                    dve.tensor_tensor(bd[:, :, :, 64:96],
                                      w[:, :, 160:192].unsqueeze(2).to_broadcast([128, 2, 3, CV]),
                                      m_v, ALU.mult).then_inc(multiplied, 1)
                    for u in range(2):
                        dve.tensor_tensor(
                            pr[:, u, 64:256].rearrange("p (t i n) -> p t i n", t=2, i=3),
                            w[:, u, 128:WN].rearrange("p (t n) -> p t n", t=3)[:, 0:3:2, :]
                            .unsqueeze(2).to_broadcast([128, 2, 3, CV]),
                            msg[s][:, u, CS:FN].rearrange("p (i n) -> p i n", i=3).unsqueeze(1)
                            .to_broadcast([128, 2, 3, CV]),
                            ALU.mult).then_inc(multiplied, 1)
                at = group(j, c, 4)
                if at:
                    g, s, r = at
                    b = s % 2
                    blk = dve.value_load(block_of[0:1, ds(g, 1)], min_val=0, max_val=NB - 1)
                    dve.wait_ge(summed, g + 1)
                    dve.wait_ge(added, g * 2) if past(g, 1) else None
                    for bank, lo, n in ((0, 0, 352), (1, 352, 384)):
                        part = acc[:, ds(blk, 1), lo:lo + n]
                        dve.tensor_tensor(part, part, pa[b][0:PB, bank, 0:n].unsqueeze(1), ALU.add)\
                            .then_inc(added, 1)
            steps(dve, body, 4)


def ab_view(pr):
    return pr[:].rearrange("p u (t q) -> p u t q", q=P_B)[:, :, :, 0:CS]


def cdx_view(pr, u):
    return pr[:, u, 0:480].rearrange("p (t q) -> p t q", q=160)[:, :, CS:CS + FV]\
        .rearrange("p t (i n) -> p t i n", i=3)


def late_nodes(k, tag, acc):
    nc = k.nc
    layer = tag[0:2]
    with k.phase(tag):
        pre = k.sb("pre", [PB, NB, 2 * 96])
        dot, *rest = (acc[:, :, 320 + 192 * i:320 + 192 * i + CV] for i in range(3))
        add_nodes(k, f"{layer}_dot", [(dot, dot, rest[0]), (dot, dot, rest[1])])

        def fill(dve, b, stage, staged):
            a = acc[:, ds(b, 1), :]

            def put(lo, n, ap, blocks=None):
                out = stage[:, lo:lo + n].unsqueeze(1)
                dve.tensor_scalar(out, ap, 1.0, None, ALU.mult).then_inc(staged, 1)

            put(0, 64, a[:, :, 0:64])
            put(64, CV, dot[:, ds(b, 1), :])
            vec = stage[:, 96:480].rearrange("p (o i n) -> p o i n", o=1, i=3)
            dve.tensor_scalar(vec[:, :, :, 0:64],
                              a[:, :, 160:736].rearrange("p o (i n) -> p o i n", i=3)[:, :, :, 96:160],
                              1.0, None, ALU.mult).then_inc(staged, 1)
            dve.tensor_scalar(vec[:, :, :, 64:96],
                              a[:, :, 64:160].rearrange("p o (i n) -> p o i n", i=3),
                              1.0, None, ALU.mult).then_inc(staged, 1)
            for i in range(3):
                j, m = (i + 1) % 3, (i + 2) % 3
                plus, minus = (160 + 192 * f + CV * e for f, e in ((m, j), (j, m)))
                dve.tensor_tensor(vec[:, :, i, 96:128], a[:, :, plus:plus + CV],
                                  a[:, :, minus:minus + CV], ALU.subtract).then_inc(staged, 1)
            dve.tensor_scalar(stage[:, 480:640].unsqueeze(1), k.h[:, ds(b, 1), :], 1.0, None,
                              ALU.mult).then_inc(staged, 1)

        w = lambda n: k.wt(f"{layer}_{n}")
        node_linear(k, f"{layer}_out", 640, fill, 8,
                    [(0, 96), (96, 224), (224, 352), (352, 480), (480, 544), (544, 640)],
                    [(0, 1, 96), (1, 3, 128), (4, 1, CS), (5, 1, FV)],
                    [(4, CS, w("skip_s"), 0, True, False), (0, 96, w("out_s"), 0, False, True),
                     (5, FV, w("skip_v"), 96, True, False)]
                    + [(1 + i, 128, w("out_v"), 96 + CV * i, False, True) for i in range(3)],
                    [(0, 192, pre)])
        with nc.Block() as block:
            done, tanhed = k.sem("done"), k.sem("tanhed")
            gate = k.sb("gate_values", [PB, NB, 96])

            @block.scalar
            def _(act):
                act.wait_ge(done, 1)
                act.activation(gate[:], pre[:, :, 0:96], ACT.Tanh, scale=0.5).then_inc(tanhed, 1)

            @block.vector
            def _(dve):
                ch = Chain(dve, done)
                if layer == "l2":
                    ch.then(dve.tensor_tensor(pre[:], pre[:], k.a0[:].unsqueeze(2)
                                              .to_broadcast([PB, NB, 192]), ALU.mult))
                else:
                    ch.then(dve.memset(gate[:, 0:1, 0:1], 0.0))
                dve.wait_ge(tanhed, 1)
                ch.then(dve.tensor_scalar(gate[:], gate[:], 0.5, 0.5, ALU.mult, ALU.add))
                ch.add(dve.tensor_tensor(pre[:, :, 0:64], pre[:, :, 0:64], gate[:, :, 0:64], ALU.mult))
                for i in range(3):
                    v = pre[:, :, 96 + CV * i:96 + CV * i + CV]
                    ch.add(dve.tensor_tensor(v, v, gate[:, :, 64:96], ALU.mult))
                dve.wait_ge(done, ch.n)
                ch.add(dve.tensor_tensor(k.x[:, :, 0:CS], k.x[:, :, 0:CS], pre[:, :, 0:64], ALU.add))
                ch.then(dve.tensor_tensor(k.x[:, :, CS:FN], k.x[:, :, CS:FN], pre[:, :, 96:192], ALU.add))


def radial_hidden(k, tag):
    nc = k.nc
    with k.phase(tag), nc.Block() as block:
        rows = [k.sb(f"rows{s}", [128, 2, RW]) for s in range(RING)]
        feat = [k.sb(f"features{s}", [65, GE]) for s in range(2)]
        cen = [[k.sb(f"centred{n}{s}", [128, 2, 64]) for s in range(RING)] for n in range(2)]
        sq = [k.sb(f"squares{n}", [128, 2, 64]) for n in range(2)]
        var = [[k.sb(f"variance{n}{s}", [128, 2]) for s in range(2)] for n in range(2)]
        tan = [[k.sb(f"tanh{n}{s}", [64, GE]) for s in range(2)] for n in range(2)]
        z = [[k.sb(f"affine{n}{s}", [64, GE]) for s in range(2)] for n in range(2)]
        hid = [[k.sb(f"hidden{n}{s}", [65, GE]) for s in range(RING)] for n in range(2)]
        p_feat = k.ps("features_t", [128, 512])
        p_mul = [[k.ps(f"product{n}{s}", [128, 512]) for s in range(2)] for n in range(2)]
        p_flip = [k.ps(f"flipped{n}", [128, 512]) for n in range(2)]
        gb = k.sb("half_gains", [64, 4])
        row_in = [k.sem(f"row_in{s}") for s in range(RING)]
        out_done = [k.sem(f"out_done{s}") for s in range(RING)]
        turned, copied, ones, gate, sp_gate = (
            k.sem(n) for n in ("turned", "copied", "ones", "gate", "sp_gate"))
        mul, cent, squared, vard, powed, normed, flipped, affined, silued = (
            [k.sem(f"{m}{n}") for n in range(2)] for m in (
                "mul", "cent", "squared", "vard", "powed", "normed", "flipped", "affined", "silued"))
        view = k.by_dst.rearrange("(g p u) w -> g p u w", p=128, u=2)
        MUL, VAR, NORM, FLIP, SILU = (1, 6), (2, 7), (3, 8), (4, 9), (5, 10)
        OUT = 11

        @block.sync
        def _(sp):
            def body(j, c):
                at = group(j, c, 0)
                if at:
                    g, s, r = at
                    if past(g, RING):
                        sp.wait_ge(turned, g - RING + 1)
                        sp.sem_inc(sp_gate, 1)
                    sp.dma_start(rows[s][:], view[ds(g, 1)].rearrange("a p u w -> p (a u) w"))\
                        .then_inc(row_in[s], 16)
                at = group(j, c, OUT)
                if at:
                    g, s, r = at
                    sp.wait_ge(silued[1], g + 1)
                    sp.sem_inc(sp_gate, 1)
                    sp.dma_start(k.hidden[ds(g * 64, 64), :], hid[1][s][0:64, :])\
                        .then_inc(out_done[s], 16)
            steps(sp, body, OUT)
            for s in range(RING):
                sp.wait_ge(out_done[s], NG // RING * 16)

        @block.gpsimd
        def _(pool):
            def body(j, c):
                for n in range(2):
                    at = group(j, c, VAR[n])
                    if at:
                        g, s, r = at
                        pool.wait_ge(vard[n], 2 * g + 2)
                        v = var[n][s % 2][:]
                        pool.tensor_tensor(v, v, k.half[:, 0:2], ALU.pow).then_inc(powed[n], 1)
            steps(pool, body, OUT)

        @block.tensor
        def _(pe):
            pe.wait_ge(ones, 3 + 2 + RING)

            def turn(at):
                g, s, r = at
                pe.wait_ge(row_in[s], r * 16 + 16)
                if past(g, 1):
                    pe.wait_ge(copied, g)
                pe.sem_inc(gate, 1)
                for u in range(2):
                    last = pe.transpose(p_feat[0:64, u * 128:u * 128 + 128],
                                        rows[s][:, u, R_A64:R_A64 + 64], k.const("ident"))
                last.then_inc(turned, 1)

            def multiply(n, at):
                g, s, r = at
                if n == 0:
                    pe.wait_ge(copied, g + 1)
                    src = feat[s % 2]
                else:
                    pe.wait_ge(silued[0], g + 1)
                    src = hid[0][s]
                if past(g, 2):
                    pe.wait_ge(cent[n], g - 1)
                pe.sem_inc(gate, 1)
                for u in range(2):
                    last = pe.matmul(p_mul[n][s % 2][:, u * 64:u * 64 + 64],
                                     src[:, u * 128:u * 128 + 128], k.wt(f"l3_rw{n + 1}"),
                                     start=True, stop=True)
                last.then_inc(mul[n], 1)

            def flip(n, at):
                g, s, r = at
                pe.wait_ge(normed[n], g + 1)
                if past(g, 1):
                    pe.wait_ge(affined[n], 2 * g)
                pe.sem_inc(gate, 1)
                for u in range(2):
                    last = pe.transpose(p_flip[n][0:64, u * 128:u * 128 + 128], cen[n][s][:, u, :],
                                        k.const("ident"))
                last.then_inc(flipped[n], 1)

            def body(j, c):
                at = group(j, c, 0)
                if at:
                    turn(at)
                for n in range(2):
                    at = group(j, c, FLIP[n])
                    if at:
                        flip(n, at)
                    at = group(j, c, MUL[n])
                    if at:
                        multiply(n, at)
            steps(pe, body, OUT)

        @block.scalar
        def _(act):
            act.wait_ge(ones, 3 + 2 + RING)

            def body(j, c):
                at = group(j, c, 0)
                if at:
                    g, s, r = at
                    act.wait_ge(turned, g + 1)
                    if past(g, 2):
                        act.wait_ge(mul[0], g - 1)
                    act.activation(feat[s % 2][0:64, :], p_feat[0:64, 0:GE], ACT.Copy)\
                        .then_inc(copied, 1)
                for n in range(2):
                    at = group(j, c, FLIP[n])
                    if at:
                        g, s, r = at
                        b = s % 2
                        act.wait_ge(flipped[n], g + 1)
                        if past(g, 2):
                            act.wait_ge(silued[n], g - 1)
                        src = p_flip[n][0:64, 0:GE]
                        act.activation(tan[n][b][:], src, ACT.Tanh, scale=gb[:, 2 * n:2 * n + 1],
                                       bias=gb[:, 2 * n + 1:2 * n + 2]).then_inc(affined[n], 1)
                        act.activation(z[n][b][:], src, ACT.Identity, scale=k.wt(f"l3_rg{n + 1}"),
                                       bias=k.wt(f"l3_rb{n + 1}")).then_inc(affined[n], 1)
                    at = group(j, c, MUL[n])
                    if at:
                        g, s, r = at
                        act.wait_ge(mul[n], g + 1)
                        if past(g, RING):
                            act.wait_ge(flipped[n], g - RING + 1)
                        act.activation(cen[n][s][:],
                                       p_mul[n][s % 2][:, 0:128].rearrange("p (u f) -> p u f", u=2),
                                       ACT.Copy).then_inc(cent[n], 1)
            steps(act, body, OUT)

        @block.vector
        def _(dve):
            for s in range(2):
                dve.memset(feat[s][64:65, :], 1.0).then_inc(ones, 1)
            for s in range(RING):
                dve.memset(hid[0][s][64:65, :], 1.0).then_inc(ones, 1)
            dve.tensor_scalar(gb[:, 0:1], k.wt("l3_rg1"), 0.5, None, ALU.mult).then_inc(ones, 1)
            dve.tensor_scalar(gb[:, 1:2], k.wt("l3_rb1"), 0.5, None, ALU.mult).then_inc(ones, 1)
            dve.tensor_scalar(gb[:, 2:4], k.wt_pair("l3_rg2", "l3_rb2"), 0.5, None, ALU.mult)\
                .then_inc(ones, 1)

            def square(n, at):
                g, s, r = at
                dve.wait_ge(cent[n], g + 1)
                if past(g, 1):
                    dve.wait_ge(vard[n], 2 * g)
                dve.tensor_tensor(sq[n][:], cen[n][s][:], cen[n][s][:], ALU.mult)\
                    .then_inc(squared[n], 1)

            def reduce(n, at):
                g, s, r = at
                dve.wait_ge(squared[n], g + 1)
                if past(g, 2):
                    dve.wait_ge(normed[n], g - 1)
                dve.tensor_reduce(var[n][s % 2][:], sq[n][:], AX_X, ALU.add).then_inc(vard[n], 1)

            def scale(n, at):
                g, s, r = at
                v = var[n][s % 2][:]
                dve.wait_ge(vard[n], 2 * g + 1)
                dve.tensor_scalar(v, v, 1 / 64, EPS, ALU.mult, ALU.add).then_inc(vard[n], 1)

            def norm(n, at):
                g, s, r = at
                dve.wait_ge(powed[n], g + 1)
                dve.tensor_tensor(cen[n][s][:], cen[n][s][:],
                                  var[n][s % 2][:].unsqueeze(2).to_broadcast([128, 2, 64]),
                                  ALU.mult).then_inc(normed[n], 1)

            def silu(n, at):
                g, s, r = at
                b = s % 2
                dve.wait_ge(affined[n], 2 * g + 2)
                if past(g, RING):
                    if n == 1:
                        dve.wait_ge(out_done[s], r * 16)
                    else:
                        dve.wait_ge(mul[1], g - RING + 1)
                dve.scalar_tensor_tensor(hid[n][s][0:64, :], tan[n][b][:], 1.0, z[n][b][:],
                                         ALU.add, ALU.mult).then_inc(silued[n], 1)

            def body(j, c):
                for stage, lags in ((norm, NORM), (silu, SILU), (square, VAR), (reduce, VAR),
                                    (scale, VAR)):
                    for n in range(2):
                        at = group(j, c, lags[n])
                        if at:
                            stage(n, at)
            steps(dve, body, OUT)


def deep_group(j, c, lag):
    return group(j, c, lag, DEEP)


def later(g, n):
    return min(g + n, NG) if isinstance(g, int) else g + n


def attention_edges(k, tag, heads, keys, head_w, dst_part, acc):
    nc = k.nc
    first = tag[0:2] == "l0"
    HW = head_w + 1
    VW = heads * HW
    ns = CS
    sh, vh = ns // heads, CV // heads
    KD = 16 if first else 64
    with k.phase(tag), nc.Block() as block:
        rows = [k.sb(f"rows{s}", [128, 2, RW]) for s in range(DEEP)]
        idx = [k.sb(f"index{s}", [128, 2], I32) for s in range(DEEP)]
        msg = [k.sb(f"message{s}", [128, 2, FN]) for s in range(DEEP)]
        hot = [k.sb(f"hot{s}", [128, 2, PB]) for s in range(DEEP)]
        hot_t = [k.sb(f"hot_t{s}", [PB, 2, 128]) for s in range(DEEP)]
        feat = [k.sb(f"features{s}", [KD if first else 65, GE]) for s in range(DEEP)]
        hot_b = [k.sb(f"hot_bf16_{s}", [PB, 2, 128], BF16) for s in range(DEEP)]
        dst_p = k.sb("dst_parts", [PB, NB, 3, FN], BF16)
        ident_b = k.sb("ident_bf16", [128, 128], BF16)
        logit_p = [k.sb(f"logit_parts{s}", [128, 2, 3 * heads], BF16) for s in range(DEEP)]
        rest = k.sb("logit_rest", [128, 2, heads])
        full = k.sb("message_sum", [128, 2, FN])
        prod = k.sb("prod", [128, 2, PW])
        t1 = k.sb("dot_terms", [128, 2, 3, CV])
        t2 = k.sb("cross_terms", [128, 2, 3, FV])
        ten = [k.sb(f"tensor_product{n}", [128, 2, MW]) for n in range(2 if first else 1)]
        ten_t = [k.sb(f"tensor_turned{n}", [128, 2, 4, 128]) for n in range(2 if first else 1)]
        logit = [k.sb(f"logits{s}", [128, 2, heads]) for s in range(DEEP)]
        al = k.sb("alpha", [128, 2, 64])
        al2 = k.sb("alpha_act", [128, 2, 64])
        gates = k.sb("gates", [128, 2, 96])
        vv = k.sb("gated", [128, 2, FV])
        vals = [k.sb(f"values{s}", [128, 2, 160]) for s in range(DEEP)] if not first else None
        log_t = k.sb("logits_turned", [3 * heads, GE], BF16)
        off = [k.sb(f"off_block{s}", [PB, 2, 128]) for s in range(DEEP)]
        junk = k.sb("junk", [PB, heads, GE])
        mx = k.sb("group_max", [PB, heads])
        mrun = k.sb("running_max", [PB, NB, heads])
        mnew = k.sb("new_max", [PB, heads])
        corr = k.sb("correction", [PB, 2, heads])
        ex = k.sb("exp", [128, 2, heads, HW])
        arg = k.sb("exp_arg", [128, 2, heads])
        scaled = k.sb("scaled_sums", [PB, VW])
        select = k.sb("head_rows", [3 * heads, heads, PB], BF16)
        headed = k.sb("head_of_row", [3 * heads, heads])
        p_front = k.ps("front", [128, 512])
        p_w = k.ps("weights", [128, 2, 256])
        p_dst = k.ps("dst_part", [128, 512])
        p_t = k.ps("turned", [128, 2, 512])
        p_d = k.ps("dense", [128, 512])
        p_a = k.ps("head_logits", [128, 512])
        p_v = k.ps("values", [128, 512])
        row_in = [k.sem(f"row_in{s}") for s in range(DEEP)]
        gathered = [k.sem(f"gathered{s}") for s in range(DEEP)]
        feat_in = [k.sem(f"feat_in{s}") for s in range(DEEP)]
        (set_up, indexed, hots, fronted, copied, weighed, dsted, tensored, turned1, evac1, densed,
         squashed, logited, turned2, evac2, valued, spread, maxed, renewed, fetched, argued, exped,
         weighted, summed, added, gate, rowed, log_turned, dve_gate, pe_gate,
         sp_gate, parted, prepared) = (
            k.sem(n) for n in (
                "set_up", "indexed", "hots", "fronted", "copied", "weighed", "dsted", "tensored",
                "turned1", "evac1", "densed", "squashed", "logited", "turned2", "evac2", "valued",
                "spread", "maxed", "renewed", "fetched", "argued", "exped", "weighted", "summed",
                "added", "gate", "rowed", "log_turned", "dve_gate", "pe_gate",
                "sp_gate", "parted", "prepared"))
        view = k.by_dst.rearrange("(g p u) w -> g p u w", p=128, u=2)
        S1 = 14
        S2 = 15 if first else 4
        NF = 5 if first else 4
        DL = k.wt(f"{tag[0:2]}_as") if first else k.wt("l3_lin_s")
        DW = 256 if first else 224
        pair_bank = [p_w[:].rearrange("p u q -> p (u q)"), p_dst[:], p_t[:, 0, :], p_t[:, 1, :]]
        PAIRS = heads // 2

        @block.sync
        def _(sp):
            def body(j, c):
                g, s, r = deep_group(j, c, 0)
                if past(g, DEEP):
                    sp.wait_ge(*((logited, (g - DEEP + 1) * S2) if first else
                                 (tensored, (g - DEEP + 1) * S1)))
                sp.sem_inc(sp_gate, 1)
                sp.dma_start(rows[s][:], view[ds(g, 1)].rearrange("a p u w -> p (a u) w"))\
                    .then_inc(row_in[s], 16)
                if not first:
                    if past(g, DEEP):
                        sp.wait_ge(weighed, g - DEEP + 1)
                    sp.sem_inc(sp_gate, 1)
                    sp.dma_start(feat[s][0:64, :], k.hidden[ds(g * 64, 64), :])\
                        .then_inc(feat_in[s], 16)
            steps(sp, body, 0, DEEP)

        @block.gpsimd
        def _(pool):
            def split(at):
                g, s, r = at
                part = [logit_p[s][:, :, n * heads:n * heads + heads] for n in range(3)]
                pool.wait_ge(logited, g * S2 + (5 if first else 4))
                if past(g, DEEP):
                    pool.wait_ge(log_turned, g - DEEP + 1)
                pool.sem_inc(gate, 1)
                pool.tensor_copy(part[0], logit[s][:]).then_inc(parted, 1)
                pool.wait_ge(parted, g * 4 + 1)
                pool.tensor_tensor(rest[:], logit[s][:], part[0], ALU.subtract).then_inc(parted, 1)
                pool.wait_ge(parted, g * 4 + 2)
                pool.sem_inc(gate, 1)
                pool.tensor_copy(part[1], rest[:]).then_inc(parted, 1)
                pool.wait_ge(parted, g * 4 + 3)
                pool.tensor_tensor(part[2], rest[:], part[1], ALU.subtract).then_inc(parted, 1)

            def index(at):
                g, s, r = at
                pool.wait_ge(row_in[s], r * 16 + 16)
                if past(g, DEEP):
                    pool.wait_ge(gathered[s], r * 32)
                pool.sem_inc(gate, 1)
                pool.tensor_copy(idx[s][:], rows[s][:, :, R_SRC]).then_inc(indexed, 1)

            def gather(at):
                g, s, r = at
                pool.wait_ge(indexed, g + 1)
                if past(g, DEEP):
                    pool.wait_ge(tensored, (g - DEEP + 1) * S1)
                pool.sem_inc(gate, 1)
                for u in range(2):
                    pool.indirect_dma_start(
                        out=msg[s][:, u, :], out_offset=None, in_=k.table,
                        in_offset=bass.IndirectOffsetOnAxis(ap=idx[s][:, u:u + 1], axis=0))\
                        .then_inc(gathered[s], 16)

            def body(j, c):
                for stage, lag in ((index, 0), (gather, 0), (split, 3)):
                    at = deep_group(j, c, lag)
                    if at:
                        stage(at)
            steps(pool, body, 3, DEEP)

        @block.tensor
        def _(pe):
            pe.wait_ge(set_up, 5 if first else 4 + DEEP)
            pe.wait_ge(prepared, 7)

            def front(at):
                g, s, r = at
                pe.wait_ge(row_in[s], r * 16 + 16)
                pe.wait_ge(hots, g + 1)
                if past(g, 1):
                    pe.wait_ge(copied, NF * g)
                pe.sem_inc(pe_gate, 1)
                if first:
                    for u in range(2):
                        pe.transpose(p_front[0:16, u * 128:u * 128 + 128],
                                     rows[s][:, u, R_A16:R_A16 + 16], k.const("ident"))
                for u in range(2):
                    last = pe.transpose(p_front[0:PB, 256 + u * 128:384 + u * 128], hot[s][:, u, :],
                                        k.const("ident"))
                last.then_inc(fronted, 2)

            def edge_weights(at):
                g, s, r = at
                blk = pe.value_load(k.block_of_dst[0:1, ds(g, 1)], min_val=0, max_val=NB - 1)
                pe.wait_ge(copied, NF * g + NF)
                if not first:
                    pe.wait_ge(feat_in[s], r * 16 + 16)
                if past(g, 1):
                    pe.wait_ge(tensored, g * S1)
                if past(g, 3):
                    pe.wait_ge(maxed, g * heads - 3 * heads + 4)
                pe.sem_inc(pe_gate, 1)
                kd = 16 if first else 65
                wr = k.wt("l0_rbf") if first else k.wt("l3_rw3")
                for u in range(2):
                    last = pe.matmul(p_w[:, u, 0:WN], feat[s][0:kd, u * 128:u * 128 + 128], wr,
                                     start=True, stop=True)
                last.then_inc(weighed, 1)
                for u in range(2):
                    for n in range(3):
                        last = pe.matmul(p_dst[:, u * FN:u * FN + FN], hot_b[s][:, u, :],
                                         dst_p[:, ds(blk, 1), n, :], start=n == 0, stop=n == 2)
                last.then_inc(dsted, 1)

            def turn(src, counter):
                for u in range(2):
                    for t in range(4):
                        last = pe.transpose(p_t[:, u, t * 128:t * 128 + 128],
                                            src[:, u, t * 128:t * 128 + 128], k.const("ident"))
                last.then_inc(counter, 1)

            def turn_first(at):
                g, s, r = at
                pe.wait_ge(tensored, g * S1 + S1)
                if first:
                    if past(g, 2):
                        pe.wait_ge(evac2, g - 1)
                elif past(g, 3):
                    pe.wait_ge(maxed, (g - 2) * heads)
                pe.sem_inc(pe_gate, 1)
                turn(ten[0], turned1)

            def dense(at):
                g, s, r = at
                pe.wait_ge(evac1, g + 1)
                if past(g, 1):
                    pe.wait_ge(logited, g * S2 - S2 + (4 if first else 2))
                    pe.wait_ge(squashed, g * 2)
                pe.sem_inc(pe_gate, 1)
                kk, n = (96, 160) if first else (97, 128)
                wv = k.wt("l0_val_v" if first else "l3_lin_v")
                for u in range(2):
                    pe.matmul(p_d[:, u * DW:u * DW + n], ten_t[0][0:kk, u, 0, :], DL, start=True,
                              stop=True, skip_group_check=True)
                    for i in range(3):
                        lo = u * DW + n + CV * i
                        last = pe.matmul(p_d[:, lo:lo + CV], ten_t[0][:, u, 1 + i, :], wv, start=True,
                                         stop=True, skip_group_check=True)
                last.then_inc(densed, 1)

            def turn_logits(at):
                g, s, r = at
                pe.wait_ge(parted, g * 4 + 4)
                if past(g, 2):
                    pe.wait_ge(argued, g * 2 - 2)
                pe.sem_inc(pe_gate, 1)
                for u in range(2):
                    last = pe.matmul(p_a[0:3 * heads, u * 128:u * 128 + 128], logit_p[s][:, u, :],
                                     ident_b[:], start=True, stop=True, skip_group_check=True)
                last.then_inc(log_turned, 1)

            def turn_second(at):
                g, s, r = at
                if first:
                    pe.wait_ge(logited, g * S2 + S2)
                    pe.wait_ge(evac1, later(g, 2))
                    pe.sem_inc(pe_gate, 1)
                    turn(ten[1], turned2)

            def values(at):
                g, s, r = at
                if first:
                    pe.wait_ge(evac2, g + 1)
                    if past(g, 1):
                        pe.wait_ge(weighted, g)
                    pe.sem_inc(pe_gate, 1)
                    for u in range(2):
                        out = p_v[:, u * 160:u * 160 + 160].rearrange("p (h q) -> p h q", h=heads)
                        pe.matmul(out[:, :, 0:sh], ten_t[1][0:96, u, 0, :], k.wt("l0_vlin_s"),
                                  start=True, stop=True, skip_group_check=True)
                        for i in range(3):
                            lo = sh + vh * i
                            last = pe.matmul(out[:, :, lo:lo + vh], ten_t[1][:, u, 1 + i, :],
                                             k.wt("l0_vlin_v"), start=True, stop=True,
                                             skip_group_check=True)
                    last.then_inc(valued, 1)

            def maxima(at):
                g, s, r = at
                pe.wait_ge(rowed, g + 1)
                pe.wait_ge(tensored, later(g, 3) * S1)
                pe.sem_inc(pe_gate, 1)
                spread_pairs(0, 2)

            def more_maxima(at):
                g, s, r = at
                if not first:
                    pe.wait_ge(evac1, later(g, 3))
                    pe.sem_inc(pe_gate, 1)
                    spread_pairs(2, PAIRS)

            def spread_pairs(lo, hi):
                for n in range(lo, hi):
                    for h in range(2):
                        last = pe.matmul(pair_bank[n][0:PB, h * GE:h * GE + GE],
                                         select[:, 2 * n + h, :], log_t[:], start=True, stop=True,
                                         skip_group_check=True)
                    last.then_inc(spread, 1)

            def fetch(at):
                g, s, r = at
                pe.wait_ge(renewed, g * 3 + 3)
                if past(g, 1):
                    pe.wait_ge(argued, g * 2)
                pe.sem_inc(pe_gate, 1)
                for u in range(2):
                    at = GE + heads * u
                    last = pe.matmul(p_a[:, at:at + heads], hot_t[s][:, u, :],
                                     mnew[:], start=True, stop=True, skip_group_check=True)
                last.then_inc(fetched, 1)

            def total(at):
                g, s, r = at
                pe.wait_ge(weighted, g + 1)
                if past(g, 1):
                    pe.wait_ge(added, g * 2)
                pe.sem_inc(pe_gate, 1)
                for u in range(2):
                    last = pe.matmul(p_v[0:PB, 320:320 + VW], hot[s][:, u, :],
                                     ex[:, u, :, :].rearrange("p h q -> p (h q)"),
                                     start=u == 0, stop=u == 1, skip_group_check=True)
                last.then_inc(summed, 1)

            if first:
                order = ((turn_second, 4), (front, 1), (maxima, 4), (turn_first, 2), (values, 4),
                         (edge_weights, 1), (dense, 2), (fetch, 4), (turn_logits, 3), (total, 5))
            else:
                order = ((front, 1), (turn_first, 2), (maxima, 4), (more_maxima, 4),
                         (edge_weights, 1), (dense, 2), (fetch, 4), (turn_logits, 3), (total, 5))

            def body(j, c):
                for stage, lag in order:
                    at = deep_group(j, c, lag)
                    if at:
                        stage(at)
            steps(pe, body, 5, DEEP)

        @block.scalar
        def _(act):
            act.wait_ge(set_up, 5 if first else 4 + DEEP)
            act.wait_ge(prepared, 7)

            def front(at):
                g, s, r = at
                act.wait_ge(fronted, 2 * g + 2)
                if first:
                    if past(g, DEEP):
                        act.wait_ge(weighed, g - DEEP + 1)
                    act.activation(feat[s][:], p_front[0:16, 0:GE], ACT.Copy).then_inc(copied, 1)
                if past(g, DEEP):
                    act.wait_ge(fetched, g - DEEP + 1)
                oh = p_front[0:PB, 256:512].rearrange("p (u e) -> p u e", u=2)
                act.activation(hot_b[s][:], oh, ACT.Copy).then_inc(copied, 1)
                act.activation(hot_t[s][:], oh, ACT.Copy).then_inc(copied, 2)
                if past(g, DEEP):
                    act.wait_ge(maxed, (g - DEEP + 1) * heads)
                act.activation(off[s][:], oh, ACT.Copy, scale=BIG, bias=-BIG).then_inc(copied, 1)

            def evac(src_done, dst, counter, at):
                g, s, r = at
                act.wait_ge(src_done, g + 1)
                if past(g, 1):
                    act.wait_ge(densed if counter is evac1 else valued, g)
                act.activation(dst[:].rearrange("p u t e -> p u (t e)"), p_t[:], ACT.Copy)\
                    .then_inc(counter, 1)

            def evac_first(at):
                evac(turned1, ten_t[0], evac1, at)

            def evac_second(at):
                if first:
                    evac(turned2, ten_t[1], evac2, at)

            def squash(at):
                g, s, r = at
                act.wait_ge(densed, g + 1)
                if past(g, 1):
                    act.wait_ge(logited, g * S2)
                d = p_d[:, 0:2 * DW].rearrange("p (u q) -> p u q", u=2)
                if first:
                    act.activation(al[:], d[:, :, 0:64], ACT.Copy, scale=0.2).then_inc(squashed, 1)
                    act.activation(gates[:], d[:, :, 64:160], ACT.Tanh, scale=0.5).then_inc(squashed, 1)
                else:
                    act.activation(al[:], d[:, :, 0:64], ACT.Tanh, scale=0.5).then_inc(squashed, 1)
                    if past(g, DEEP):
                        act.wait_ge(weighted, g - DEEP + 1)
                    act.activation(vals[s][:], d[:, :, 64:224], ACT.Copy).then_inc(squashed, 1)

            def rows_of_logits(at):
                g, s, r = at
                act.wait_ge(log_turned, g + 1)
                act.activation(log_t[:], p_a[0:3 * heads, 0:GE], ACT.Copy).then_inc(rowed, 1)

            def exps(at):
                g, s, r = at
                act.wait_ge(argued, g * 2 + 2)
                if past(g, 1):
                    act.wait_ge(summed, g)
                act.activation(ex[:, :, :, head_w], arg[:], ACT.Exp).then_inc(exped, 1)

            def exp_correction(at):
                g, s, r = at
                act.wait_ge(renewed, g * 3 + 3)
                if past(g, 1):
                    act.wait_ge(added, g * 2)
                act.activation(corr[:, 1, :], corr[:, 0, :], ACT.Exp).then_inc(exped, 1)

            if first:
                order = ((exps, 5), (evac_second, 4), (exp_correction, 5), (evac_first, 2),
                         (front, 1), (rows_of_logits, 3), (squash, 2))
            else:
                order = ((exps, 5), (exp_correction, 5), (evac_first, 2), (front, 1),
                         (rows_of_logits, 3), (squash, 2))

            def body(j, c):
                for stage, lag in order:
                    at = deep_group(j, c, lag)
                    if at:
                        stage(at)
            steps(act, body, 5, DEEP)

        @block.vector
        def _(dve):
            dve.memset(acc[:], 0.0).then_inc(set_up, 1)
            dve.memset(mrun[:], -BIG).then_inc(set_up, 1)
            for n in range(len(ten)):
                dve.memset(ten[n][:, :, 96:128], 0.0 if first else 1.0).then_inc(set_up, 1)
            if not first:
                for s in range(DEEP):
                    dve.memset(feat[s][64:65, :], 1.0).then_inc(set_up, 1)
            dve.tensor_copy(ident_b[:], k.const("ident")).then_inc(set_up, 1)
            ch = Chain(dve, prepared)
            rows_of = k.const("ident", 3 * heads)
            ch.then(dve.tensor_tensor(headed[:], rows_of[:, 0:heads], rows_of[:, heads:2 * heads],
                                      ALU.add))
            ch.then(dve.tensor_tensor(headed[:], headed[:], rows_of[:, 2 * heads:3 * heads], ALU.add))
            ch.then(dve.tensor_copy(select[:], headed[:].unsqueeze(2)
                                    .to_broadcast([3 * heads, heads, PB])))
            ch.then(dve.tensor_copy(dst_p[:, :, 0, :], dst_part[:]))
            ch.then(dve.tensor_tensor(dst_part[:], dst_part[:], dst_p[:, :, 0, :], ALU.subtract))
            ch.then(dve.tensor_copy(dst_p[:, :, 1, :], dst_part[:]))
            ch.then(dve.tensor_tensor(dst_p[:, :, 2, :], dst_part[:], dst_p[:, :, 1, :],
                                      ALU.subtract))
            dve.wait_ge(set_up, 5 if first else 4 + DEEP)

            def one_hot(at):
                g, s, r = at
                dve.wait_ge(row_in[s], r * 16 + 16)
                if past(g, DEEP):
                    dve.wait_ge(summed, g - DEEP + 1)
                dve.tensor_tensor(hot[s][:], k.const("nodes").unsqueeze(1).to_broadcast([128, 2, PB]),
                                  rows[s][:, :, R_LDST:R_LDST + 1].to_broadcast([128, 2, PB]),
                                  ALU.is_equal).then_inc(hots, 1)

            def product(a, b, cvec, dvec, xvec, y0, y, m, sem, base):
                at = [base]

                def add(ins):
                    ins.then_inc(sem, 1)
                    at[0] = at[0] + 1

                vec = m[:, :, 128:512].rearrange("p u (i q) -> p u i q", i=3)
                y4 = y.unsqueeze(3)
                if y0 is not None:
                    add(dve.tensor_tensor(m[:, :, 0:64], a, y0.to_broadcast([128, 2, 64]), ALU.mult))
                    add(dve.tensor_tensor(vec[:, :, :, 64:96], cvec,
                                          y0.unsqueeze(3).to_broadcast([128, 2, 3, CV]), ALU.mult))
                add(dve.tensor_tensor(t1[:], dvec, y4.to_broadcast([128, 2, 3, CV]), ALU.mult))
                dot_at = at[0]
                add(dve.tensor_tensor(t2[:], xvec.unsqueeze(2).to_broadcast([128, 2, 3, FV]),
                                      y4.to_broadcast([128, 2, 3, FV]), ALU.mult))
                cross_at = at[0]
                add(dve.tensor_tensor(vec[:, :, :, 0:64], b.unsqueeze(2).to_broadcast([128, 2, 3, 64]),
                                      y4.to_broadcast([128, 2, 3, 64]), ALU.mult))
                dve.wait_ge(sem, dot_at)
                add(dve.tensor_tensor(t1[:, :, 0, :], t1[:, :, 0, :], t1[:, :, 1, :], ALU.add))
                sum_at = at[0]
                dve.wait_ge(sem, cross_at)
                for i in range(3):
                    q, z = (i + 1) % 3, (i + 2) % 3
                    add(dve.tensor_tensor(vec[:, :, i, 96:128], t2[:, :, z, CV * q:CV * q + CV],
                                          t2[:, :, q, CV * z:CV * z + CV], ALU.subtract))
                    if i == 0:
                        dve.wait_ge(sem, sum_at)
                        add(dve.tensor_tensor(m[:, :, 64:96], t1[:, :, 0, :], t1[:, :, 2, :], ALU.add))

            def factors(s):
                rw = rows[s]
                if first:
                    return rw[:, :, R_Y:R_Y + 1], rw[:, :, R_Y + 1:R_Y + 4]
                return None, rw[:, :, R_U3:R_U3 + 3]

            def tensor(at):
                g, s, r = at
                base = g * S1
                dve.wait_ge(gathered[s], r * 32 + 32)
                dve.wait_ge(dsted, g + 1)
                dve.tensor_tensor(full[:], msg[s][:],
                                  p_dst[:, 0:2 * FN].rearrange("p (u f) -> p u f", u=2), ALU.add)\
                    .then_inc(tensored, 1)
                dve.wait_ge(weighed, g + 1)
                dve.wait_ge(tensored, base + 1)
                if past(g, 1):
                    dve.wait_ge(turned1, g)
                pr, m = prod, ten[0]
                wa = p_w[:, :, 0:128].rearrange("p u (t n) -> p u t n", t=2)
                wv = p_w[:, :, 128:WN].rearrange("p u (t n) -> p u t n", t=3)
                sc = full[:, :, 0:CS]
                fv = full[:, :, CS:FN].rearrange("p u (i n) -> p u i n", i=3)
                if first:
                    dve.tensor_tensor(ab_view(pr), wa, sc.unsqueeze(2).to_broadcast([128, 2, 2, CS]),
                                      ALU.mult).then_inc(tensored, 1)
                    for u in range(2):
                        dve.tensor_tensor(
                            cdx_view(pr, u), wv[:, u].unsqueeze(2).to_broadcast([128, 3, 3, CV]),
                            fv[:, u].unsqueeze(1).to_broadcast([128, 3, 3, CV]), ALU.mult)\
                            .then_inc(tensored, 1)
                    n = 4
                else:
                    dve.tensor_tensor(m[:, :, 0:64], wa[:, :, 0, :], sc, ALU.mult).then_inc(tensored, 1)
                    dve.tensor_tensor(pr[:, :, P_B:P_B + 64], wa[:, :, 1, :], sc, ALU.mult)\
                        .then_inc(tensored, 1)
                    vec = m[:, :, 128:512].rearrange("p u (i q) -> p u i q", i=3)
                    for t, out in ((0, vec[:, :, :, 64:96]),
                                   (1, pr[:, :, P_D:P_D + FV].rearrange("p u (i n) -> p u i n", i=3))):
                        dve.tensor_tensor(out, wv[:, :, t:t + 1, :].to_broadcast([128, 2, 3, CV]), fv,
                                          ALU.mult).then_inc(tensored, 1)
                    dve.tensor_tensor(pr[:, :, P_X:P_X + FV].rearrange("p u (i n) -> p u i n", i=3),
                                      wv[:, :, 2:3, :].to_broadcast([128, 2, 3, CV]), fv,
                                      ALU.mult).then_inc(tensored, 1)
                    n = 6
                dve.wait_ge(tensored, base + n)
                y0, y = factors(s)
                vec3 = lambda lo: pr[:, :, lo:lo + FV].rearrange("p u (i n) -> p u i n", i=3)
                product(pr[:, :, P_A:P_A + 64], pr[:, :, P_B:P_B + 64], vec3(P_C), vec3(P_D),
                        pr[:, :, P_X:P_X + FV], y0, y, m, tensored, base + n)

            def logits(at):
                g, s, r = at
                base = g * S2
                d = p_d[:, 0:2 * DW].rearrange("p (u q) -> p u q", u=2)
                dve.wait_ge(squashed, g * 2 + 2)
                if past(g, DEEP):
                    dve.wait_ge(log_turned, g - DEEP + 1)
                ad = k.row(f"{tag[0:2]}_adot").unsqueeze(1).to_broadcast([128, 2, 64])
                if first:
                    dve.tensor_tensor(al2[:], d[:, :, 0:64], al[:], ALU.max).then_inc(logited, 1)
                    dve.tensor_scalar(gates[:], gates[:], 0.5, 0.5, ALU.mult, ALU.add).then_inc(logited, 1)
                    dve.wait_ge(logited, base + 1)
                    dve.tensor_tensor(al2[:], al2[:], ad, ALU.mult).then_inc(logited, 1)
                    dve.wait_ge(logited, base + 2)
                    dve.tensor_tensor(
                        vv[:].rearrange("p u (i n) -> p u i n", i=3),
                        d[:, :, 160:256].rearrange("p u (i n) -> p u i n", i=3),
                        gates[:, :, 64:96].unsqueeze(2).to_broadcast([128, 2, 3, CV]), ALU.mult)\
                        .then_inc(logited, 1)
                    dve.wait_ge(logited, base + 3)
                    dve.tensor_reduce(logit[s][:], al2[:].rearrange("p u (h q) -> p u h q", h=heads),
                                      AX_X, ALU.add).then_inc(logited, 1)
                else:
                    dve.tensor_scalar(al2[:], al[:], 0.4, 0.6, ALU.mult, ALU.add).then_inc(logited, 1)
                    dve.wait_ge(logited, base + 1)
                    dve.tensor_tensor(al2[:], d[:, :, 0:64], al2[:], ALU.mult).then_inc(logited, 1)
                    dve.wait_ge(logited, base + 2)
                    dve.tensor_tensor(al2[:], al2[:], ad, ALU.mult).then_inc(logited, 1)
                    dve.wait_ge(logited, base + 3)
                    dve.tensor_reduce(logit[s][:], al2[:].rearrange("p u (h q) -> p u h q", h=heads),
                                      AX_X, ALU.add).then_inc(logited, 1)

            def second_product(at):
                g, s, r = at
                base = g * S2
                dve.wait_ge(logited, base + 4)
                if past(g, 1):
                    dve.wait_ge(turned2, g)
                y0, y = factors(s)
                v4 = vv[:].rearrange("p u (i n) -> p u i n", i=3)
                product(gates[:, :, 0:64], gates[:, :, 0:64], v4, v4, vv[:], y0, y, ten[1],
                        logited, base + 5)

            def maxima(at):
                g, s, r = at
                blk = dve.value_load(k.block_of_dst[0:1, ds(g, 1)], min_val=0, max_val=NB - 1)
                dve.wait_ge(copied, NF * g + NF)
                if past(g, 1):
                    dve.wait_ge(maxed, g * heads)
                o = off[s][:].rearrange("p u e -> p (u e)")
                for n in range(heads):
                    if n % 2 == 0:
                        dve.wait_ge(spread, g * PAIRS + n // 2 + 1)
                        dve.sem_inc(dve_gate, 1)
                    h = n % 2 * GE
                    dve.tensor_tensor_reduce(junk[:, n, :], pair_bank[n // 2][0:PB, h:h + GE], o, 1.0,
                                             -BIG, ALU.add, ALU.max, mx[:, n:n + 1]).then_inc(maxed, 1)
                dve.wait_ge(maxed, g * heads + heads)
                if past(g, 1):
                    dve.wait_ge(fetched, g)
                    dve.wait_ge(exped, g * 2)
                    dve.wait_ge(renewed, g * 3)
                old = mrun[:, ds(blk, 1), :]
                dve.tensor_tensor(mnew[:].unsqueeze(1), old, mx[:].unsqueeze(1), ALU.max)\
                    .then_inc(renewed, 1)
                dve.wait_ge(renewed, g * 3 + 1)
                dve.tensor_tensor(corr[:, 0:1, :], old, mnew[:].unsqueeze(1), ALU.subtract)\
                    .then_inc(renewed, 1)
                dve.wait_ge(renewed, g * 3 + 2)
                dve.tensor_scalar(old, mnew[:].unsqueeze(1), 1.0, None, ALU.mult).then_inc(renewed, 1)

            def argue(at):
                g, s, r = at
                dve.wait_ge(fetched, g + 1)
                dve.wait_ge(rowed, later(g, 2))
                dve.tensor_tensor(arg[:], logit[s][:],
                                  p_a[:, GE:GE + 2 * heads].rearrange("p (u h) -> p u h", u=2),
                                  ALU.subtract).then_inc(argued, 1)
                dve.wait_ge(argued, g * 2 + 1)
                dve.tensor_scalar(arg[:], arg[:], 0.0, None, ALU.min).then_inc(argued, 1)

            def weight(at):
                g, s, r = at
                dve.wait_ge(exped, g * 2 + 1)
                if past(g, 1):
                    dve.wait_ge(summed, g)
                if first:
                    dve.wait_ge(valued, g + 1)
                for u in range(2):
                    e = ex[:, u, :, head_w:HW]
                    if first:
                        last = dve.tensor_tensor(
                            ex[:, u, :, 0:head_w],
                            p_v[:, u * 160:u * 160 + 160].rearrange("p (h q) -> p h q", h=heads),
                            e.to_broadcast([128, heads, head_w]), ALU.mult)
                    else:
                        v = vals[s]
                        dve.tensor_tensor(ex[:, u, :, 0:sh],
                                          v[:, u, 0:ns].rearrange("p (h q) -> p h q", h=heads),
                                          e.to_broadcast([128, heads, sh]), ALU.mult)
                        last = dve.tensor_tensor(
                            ex[:, u, :, sh:head_w].rearrange("p h (i q) -> p i h q", i=3),
                            v[:, u, ns:160].rearrange("p (i h q) -> p i h q", i=3, h=heads),
                            ex[:, u, :, head_w:HW].unsqueeze(1).to_broadcast([128, 3, heads, vh]),
                            ALU.mult)
                last.then_inc(weighted, 1)

            blocks = []

            def locate(at):
                blocks.append(dve.value_load(k.block_of_dst[0:1, ds(at[0], 1)], min_val=0,
                                             max_val=NB - 1))

            def add(at):
                g, s, r = at
                blk = blocks.pop()
                dve.wait_ge(exped, g * 2 + 2)
                if past(g, 1):
                    dve.wait_ge(added, g * 2)
                a = acc[:, ds(blk, 1), :]
                dve.tensor_tensor(scaled[:].rearrange("p (o h q) -> p o h q", o=1, h=heads),
                                  a.rearrange("p o (h q) -> p o h q", h=heads),
                                  corr[:, 1:2, :].unsqueeze(3).to_broadcast([PB, 1, heads, HW]), ALU.mult)\
                    .then_inc(added, 1)
                dve.wait_ge(added, g * 2 + 1)
                dve.wait_ge(summed, g + 1)
                dve.tensor_tensor(a, scaled[:].unsqueeze(1), p_v[0:PB, 320:320 + VW].unsqueeze(1), ALU.add)\
                    .then_inc(added, 1)

            def body(j, c):
                for stage, lag in ((tensor, 2), (locate, 6), (argue, 5), (add, 6), (logits, 3), (weight, 5),
                                   (maxima, 4), (second_product, 3), (one_hot, 0)):
                    if stage is second_product and not first:
                        continue
                    at = deep_group(j, c, lag)
                    if at:
                        stage(at)
            steps(dve, body, 6, DEEP)


def attended(k, tag, heads, head_w, acc, out):
    nc = k.nc
    ns = heads * head_w - FV
    sh, vh = ns // heads, CV // heads
    with k.phase(tag), nc.Block() as block:
        done = k.sem("done")
        inv = k.sb("inverse", [PB, NB, heads])

        @block.vector
        def _(dve):
            ch = Chain(dve, done)
            a = acc[:].rearrange("p b (h q) -> p b h q", h=heads)
            eps = 1e-16 if tag[0:2] == "l0" else 1e-12
            ch.then(dve.tensor_scalar(inv[:], a[:, :, :, head_w], eps, None, ALU.add))
            ch.then(dve.reciprocal(inv[:], inv[:]))
            parts = [(0, sh, 0)] + [(ns + CV * i, vh, sh + vh * i) for i in range(3)]
            for lo, n, at in parts:
                ch.add(dve.tensor_tensor(
                    out[:, :, lo:lo + heads * n].rearrange("p b (h q) -> p b h q", h=heads),
                    a[:, :, :, at:at + n], inv[:].unsqueeze(3).to_broadcast([PB, NB, heads, n]),
                    ALU.mult))
            dve.wait_ge(done, ch.n)


def add_nodes(k, tag, terms):
    with k.phase(tag), k.nc.Block() as block:
        done = k.sem("done")

        @block.vector
        def _(dve):
            ch = Chain(dve, done)
            for target, a, b in terms:
                ch.then(dve.tensor_tensor(target, a, b, ALU.add))


def layer0(k):
    with k.phase("l0"):
        acc = k.sb("acc", [PB, NB, 4 * 41])
        with k.phase("l0_in"):
            dst = k.sb("dst_part", [PB, NB, FN])
            with k.phase("l0_pre"):
                n = k.sb("normed", [PB, NB, FN])
                t = k.sb("src_part", [PB, NB, FN])
                norm_nodes(k, "l0_norm", True, k.h, n, ("l0_gs", "l0_bs", "l0_gv"), CV)
                node_linear(k, "l0_lin", FN, copy_fill(n, FN), 1, SV_SLICES, SV_EVACS,
                            [(0, CS, k.wt("l0_src_s"), 0, True, True),
                             (1, FV, k.wt("l0_src_v"), CS, True, True),
                             (0, CS, k.wt("l0_dst_s"), FN, True, True),
                             (1, FV, k.wt("l0_dst_v"), FN + CS, True, True)],
                            [(0, FN, t), (FN, FN, dst)])
                write_table(k, "l0_table", t)
            attention_edges(k, "l0_edges", 4, 16, 40, dst, acc)
        m = k.sb("attended", [PB, NB, FN])
        u = k.sb("update", [PB, NB, FN])
        attended(k, "l0_attended", 4, 40, acc, m)
        node_linear(k, "l0_out", FN, copy_fill(m, FN), 1, SV_SLICES, SV_EVACS,
                    [(0, CS, k.wt("l0_ps"), 0, True, True), (1, FV, k.wt("l0_pv"), CS, True, True)],
                    [(0, FN, u)])
        add_nodes(k, "l0_add", [(k.x[:], k.x[:], k.h[:]), (k.x[:], k.x[:], u[:])])


def late_layer(k, layer, rows_dram, block_of, gather_col, local_col, y_cols):
    with k.phase(layer):
        acc = k.sb("acc", [PB, NB, 736])
        with k.phase(f"{layer}_pre"):
            t = k.sb("src_part", [PB, NB, FN])
            norm_nodes(k, f"{layer}_norm", True)
            node_linear(k, f"{layer}_lin", FN, copy_fill(k.h, FN), 1, SV_SLICES, SV_EVACS,
                        [(0, CS, k.wt(f"{layer}_in_s"), 0, True, True),
                         (1, FV, k.wt(f"{layer}_in_v"), CS, True, True)], [(0, FN, t)])
            write_table(k, f"{layer}_table", t)
        late_edges(k, f"{layer}_edges", rows_dram, block_of, gather_col, local_col, y_cols,
                   layer == "l2", acc)
        late_nodes(k, f"{layer}_nodes", acc)


def layer3(k):
    nc = k.nc
    radial_hidden(k, "l3_radial")
    with k.phase("l3"):
        acc = k.sb("acc", [PB, NB, 8 * 21])
        with k.phase("l3_in"):
            dst = k.sb("dst_part", [PB, NB, FN])
            with k.phase("l3_pre"):
                n = k.sb("normed", [PB, NB, FN])
                t = k.sb("src_part", [PB, NB, FN])
                norm_nodes(k, "l3_norm", True, k.h, n, ("l3_gs1", "l3_bs1", "l3_gv1"), FV)
                node_linear(k, "l3_lin", FN, copy_fill(n, FN), 1, SV_SLICES, SV_EVACS,
                            [(0, CS, k.wt("l3_src_s"), 0, True, True),
                             (1, FV, k.wt("l3_src_v"), CS, True, True),
                             (0, CS, k.wt("l3_dst_s"), FN, True, True),
                             (1, FV, k.wt("l3_dst_v"), FN + CS, True, True)],
                            [(0, FN, t), (FN, FN, dst)])
                add_nodes(k, "l3_bias", [(dst[:, :, 0:CS], dst[:, :, 0:CS], k.blockrow("l3_dst_b"))])
                write_table(k, "l3_table", t)
            attention_edges(k, "l3_edges", 8, 8, 20, dst, acc)
        m = k.sb("attended", [PB, NB, FN])
        u = k.sb("update", [PB, NB, FN])
        f = k.sb("feed", [PB, NB, 384])
        attended(k, "l3_attended", 8, 20, acc, m)
        node_linear(k, "l3_proj", FN, copy_fill(m, FN), 1, SV_SLICES, SV_EVACS,
                    [(0, CS, k.wt("l3_proj_s"), 0, True, True), (1, FV, k.wt("l3_proj_v"), CS, True, True)],
                    [(0, FN, u)])
        add_nodes(k, "l3_mid", [(k.h[:], k.h[:], u[:]),
                                (k.h[:, :, 0:CS], k.h[:, :, 0:CS], k.blockrow("l3_proj_b"))])
        norm_nodes(k, "l3_norm2", False, k.h, m, ("l3_gs2", "l3_bs2", "l3_gv2"), FV)
        node_linear(k, "l3_f1", FN, copy_fill(m, FN), 1, SV_SLICES, SV_EVACS,
                    [(0, CS, k.wt("l3_f1_s"), 0, True, True), (1, FV, k.wt("l3_f1_v"), 192, True, True)],
                    [(0, 384, f)])
        with nc.Block() as block:
            done, tanhed = k.sem("done"), k.sem("tanhed")
            sg = k.sb("squashed", [PB, NB, 192])
            a0 = k.a0[:].unsqueeze(2)

            @block.scalar
            def _(act):
                act.wait_ge(done, 2)
                act.activation(sg[:], f[:, :, 0:192], ACT.Tanh, scale=0.5).then_inc(tanhed, 1)

            @block.vector
            def _(dve):
                ch = Chain(dve, done)
                ch.then(dve.tensor_tensor(f[:, :, 0:192], f[:, :, 0:192], k.blockrow("l3_f1_b"), ALU.add))
                ch.then(dve.tensor_tensor(f[:], f[:], a0.to_broadcast([PB, NB, 384]), ALU.mult))
                dve.wait_ge(tanhed, 1)
                ch.then(dve.tensor_scalar(sg[:], sg[:], 0.5, 0.5, ALU.mult, ALU.add))
                ch.add(dve.tensor_tensor(f[:, :, 0:128], f[:, :, 0:128], sg[:, :, 0:128], ALU.mult))
                for i in range(3):
                    v = f[:, :, 192 + 64 * i:256 + 64 * i]
                    ch.add(dve.tensor_tensor(v, v, sg[:, :, 128:192], ALU.mult))
                dve.wait_ge(done, ch.n)

        node_linear(k, "l3_f2", 384, copy_fill(f, 384), 1,
                    [(0, 128)] + [(192 + 64 * i, 256 + 64 * i) for i in range(3)],
                    [(0, 1, 128), (1, 3, 64)],
                    [(0, 128, k.wt("l3_f2_s"), 0, True, True)]
                    + [(1 + i, 64, k.wt("l3_f2_v"), CS + CV * i, True, True) for i in range(3)],
                    [(0, FN, u)])
        with nc.Block() as block:
            merged = k.sem("merged")

            @block.vector
            def _(dve):
                ch = Chain(dve, merged)
                ch.then(dve.tensor_tensor(u[:, :, 0:CS], u[:, :, 0:CS], k.blockrow("l3_f2_b"), ALU.add))
                ch.then(dve.tensor_tensor(u[:], u[:], k.a0[:].unsqueeze(2).to_broadcast([PB, NB, FN]),
                                          ALU.mult))
                ch.then(dve.tensor_tensor(k.x[:], k.x[:], k.h[:], ALU.add))
                ch.then(dve.tensor_tensor(k.x[:], k.x[:], u[:], ALU.add))


def gnn_kernel(nc, args, layers=4):
    with ExitStack() as stack:
        k = Kernel(nc, stack, args)
        prepare(k)
        sort_edges(k)
        if layers > 0:
            layer0(k)
        if layers > 1:
            late_layer(k, "l1", k.by_src, k.block_of_src, R_DST, R_LSRC, (R_U1, 3))
        if layers > 2:
            late_layer(k, "l2", k.by_dst, k.block_of_dst, R_SRC, R_LDST, (R_Y, 4))
        if layers > 3:
            layer3(k)
        with nc.Block() as block:
            stored = k.sem("stored")

            @block.sync
            def _(sp):
                sp.dma_start(args["out"], k.x[:]).then_inc(stored, 16)
                sp.wait_ge(stored, 16)


def by_component(a, s=CS):
    import numpy as np
    v = a[..., s:]
    v = v.reshape(*v.shape[:-1], v.shape[-1] // 3, 3)
    return np.concatenate([a[..., :s], np.moveaxis(v, -1, -2).reshape(*a.shape[:-1], -1)], -1)


def layout(inputs):
    import numpy as np
    g = {n: np.asarray(a) for n, a in inputs.items()}
    z = lambda *s: np.zeros(s, np.float32)

    def diag(w):
        r, c = w.shape
        out = z(3 * r, 3 * c)
        for i in range(3):
            out[i * r:i * r + r, i * c:i * c + c] = w
        return out

    def col(*a):
        return np.concatenate(a)[:, None]

    def biased(w, b):
        return np.concatenate([w, b[None, :]], 0)

    w = {}
    p = "L0_gnn_"
    w.update(l0_src_s=g[p + "Ws_src"], l0_src_v=diag(g[p + "Wv_src"]), l0_dst_s=g[p + "Ws_dst"],
             l0_dst_v=diag(g[p + "Wv_dst"]), l0_rbf=g[p + "W_rbf"],
             l0_as=np.concatenate([g[p + "W_alpha"], g[p + "Ws_val"], z(96, 32)], 1),
             l0_val_t=g[p + "Ws_val"].T, l0_gate=g[p + "Wg"], l0_val_v=g[p + "Wv_val"],
             l0_vlin_s=g[p + "Ws_vlin"], l0_vlin_v=g[p + "Wv_vlin"], l0_ps=g[p + "Wps"],
             l0_pv=diag(g[p + "Wpv"]), l0_w2s=col(g[p + "w2_ss"], g[p + "w2_vv0"]),
             l0_w2v=col(g[p + "w2_sv"], g[p + "w2_vs"], g[p + "w2_vv1"]))
    p = "L1_gnn_"
    w.update(l1_skip_s=g[p + "W_skip0"], l1_skip_v=diag(g[p + "W_skip1"]), l1_in_s=g[p + "W_nl0"],
             l1_in_v=diag(g[p + "W_nl1"]), l1_fc1=g[p + "W_fc1"], l1_fc2=g[p + "W_fc2"],
             l1_out_s=g[p + "W_out_s"], l1_out_v=g[p + "W_out_v"])
    p = "L2_gnn_"
    w.update(l2_skip_s=g[p + "sc_ws"], l2_skip_v=diag(g[p + "sc_wv"]), l2_in_s=g[p + "lin1_ws"],
             l2_in_v=diag(g[p + "lin1_wv"]), l2_fc1=g[p + "fc_w1"], l2_fc2=g[p + "fc_w2"],
             l2_out_s=g[p + "lin2_ws"], l2_out_v=g[p + "lin2_wv"])
    p = "L3_gnn_"
    w.update(l3_src_s=g[p + "msrc_ws"], l3_src_v=diag(g[p + "msrc_wv"]), l3_dst_s=g[p + "mdst_ws"],
             l3_dst_v=diag(g[p + "mdst_wv"]), l3_rw1=biased(g[p + "rw1"], g[p + "rb1"]),
             l3_rw2=biased(g[p + "rw2"], g[p + "rb2"]), l3_rw3=biased(g[p + "rw3"], g[p + "roff"]),
             l3_rg1=col(g[p + "rg1"]), l3_rb1=col(g[p + "rbe1"]), l3_rg2=col(g[p + "rg2"]),
             l3_rb2=col(g[p + "rbe2"]), l3_lin_s=biased(g[p + "lin_ws"], g[p + "lin_bs"]),
             l3_lin_v=g[p + "lin_wv"], l3_proj_s=g[p + "proj_ws"], l3_proj_v=diag(g[p + "proj_wv"]),
             l3_f1_s=g[p + "f1_ws"], l3_f1_v=diag(g[p + "f1_wv"]), l3_f2_s=g[p + "f2_ws"],
             l3_f2_v=g[p + "f2_wv"])
    weights = z(128, WEIGHT_W)
    for name, (at, n) in WEIGHT_AT.items():
        weights[:WEIGHTS[name][0], at:at + n] = w[name]
    r = dict(
        l0_gs=g["L0_gnn_gamma_s"], l0_bs=g["L0_gnn_beta_s"], l0_gv=np.tile(g["L0_gnn_gamma_v"], 3),
        l0_adot=g["L0_gnn_alpha_dot"].reshape(-1), l3_gs1=g[p + "ln1_w0"], l3_bs1=g[p + "ln1_b0"],
        l3_gv1=np.tile(g[p + "ln1_w1"], 3), l3_gs2=g[p + "ln2_w0"], l3_bs2=g[p + "ln2_b0"],
        l3_gv2=np.tile(g[p + "ln2_w1"], 3), l3_adot=g[p + "alpha_dot"].reshape(-1),
        l3_dst_b=g[p + "mdst_bs"], l3_proj_b=g[p + "proj_bs"], l3_f1_b=g[p + "f1_bs"],
        l3_f2_b=g[p + "f2_bs"])
    rows = np.concatenate([r[n] for n in ROWS])
    c = z(128, CONST_W)
    for name, a in dict(ident=np.eye(128), before=np.triu(np.ones((128, PB)), 1), nodes=np.arange(PB),
                        blocks=np.arange(NB), groups=np.arange(NG)).items():
        at, n = CONST_AT[name]
        c[:, at:at + n] = a
    f = np.concatenate([g["edge_attr_64"], g["edge_attr_16"], g["edge_attr_4"]], 1)
    out = dict(
        x_rows=by_component(g["x"]).reshape(NB, PB, FN).transpose(1, 0, 2),
        consts=c, weights=weights, row_vectors=np.broadcast_to(rows, (128, ROW_W)),
        node_attr=g["node_vec1"].reshape(NB, PB).T, edge_rows=f.reshape(EP, EC, RH),
        edge_vec=g["edge_attr_3"].reshape(EP, EC, 3), src=g["src"].reshape(EP, EC),
        dst=g["dst"].reshape(EP, EC))
    return {n: np.ascontiguousarray(a) for n, a in out.items()}


def back(out):
    import numpy as np
    a = out.transpose(1, 0, 2).reshape(N, FN)
    v = a[:, CS:].reshape(N, 3, CV).transpose(0, 2, 1).reshape(N, FV)
    return np.ascontiguousarray(np.concatenate([a[:, :CS], v], 1))


def declare(nc, arrays):
    args = {n: nc.dram_tensor(f"in_{n}_dram", a.shape, mybir.dt.from_np(a.dtype),
                              kind="ExternalInput").ap() for n, a in arrays.items()}
    args["out"] = nc.dram_tensor("out_0_dram", (PB, NB, FN), F32, kind="ExternalOutput").ap()
    return args


def kernel(**inputs):
    import concourse.bacc as _bacc
    from concourse.bass_utils import run_bass_kernel_spmd as _run

    nc = _bacc.Bacc("TRN2", target_bir_lowering=False, num_devices=1)
    arrays = layout(inputs)
    gnn_kernel(nc, declare(nc, arrays))
    r = _run(nc, [{f"in_{n}_dram": a for n, a in arrays.items()}], core_ids=[0])
    return back(r.results[0]["out_0_dram"])
```
